# Optimizing a Trainium2 kernel written in Bass

```python
import numpy as np
import jax
import jax.numpy as jnp

def _softmax(x, axis=-1):
    return jax.nn.softmax(x, axis=axis)

def _gelu(x):
    return jax.nn.gelu(x, approximate=True)

def _silu(x):
    return jax.nn.silu(x)

def _sigmoid(x):
    return jax.nn.sigmoid(x)

def _layernorm(x, axis=-1, eps=1e-05):
    m = jnp.mean(x, axis=axis, keepdims=True)
    v = jnp.var(x, axis=axis, keepdims=True)
    return (x - m) / jnp.sqrt(v + eps)

def _scatter_add(tgt, idx, src, axis=0):
    return tgt.at[idx].add(src)

def _segment_sum(src, seg, n):
    return jax.ops.segment_sum(src, seg, n)
kernel_name = 'mk_gnn_preln_d4_gnn_r8_b7fc9b'

def setup_inputs(seed: int=0):
    np.random.seed(seed)
    _w = jnp.asarray

    def _rec_inputs():
        import jax
        import jax.numpy as jnp
        _gk = jax.random.key(seed)
        x = -0.0005963 + 1.001 * jax.random.normal(jax.random.fold_in(_gk, 1), (384, 1024), jnp.float32)
        src = jax.random.randint(jax.random.fold_in(_gk, 2), (6144,), 0, 384, jnp.int32)
        dst = jnp.minimum((384 * jax.random.uniform(jax.random.fold_in(_gk, 3), (6144,)) ** 2.0).astype(jnp.int32), 3071)
        _o = jnp.argsort(dst, stable=True)
        src = src[_o]
        dst = dst[_o]
        edge_type_5 = jax.random.randint(jax.random.fold_in(_gk, 13), (6144,), 0, 5, jnp.int32)
        edge_weight = -0.000130211 + 0.031236 * jax.random.normal(jax.random.fold_in(_gk, 14), (6144,), jnp.float32)
        return (x, src, dst, edge_type_5, edge_weight)
    x, src, dst, edge_type_5, edge_weight = _rec_inputs()

    def _L0_gnn_setup():
        import jax, jax.numpy as jnp
        import numpy as np
        N = 384
        E = 12288
        IN_F = 1024
        OUT_F = 1024
        H = 16
        D = OUT_F // H
        NUM_ETYPES = 4

        def _build_mask(edge_index, edge_type, edge_type_weights, dtype):
            src, dst = (edge_index[0], edge_index[1])
            w = jax.nn.softplus(edge_type_weights)
            mask = jnp.full((N, N), -jnp.inf, dtype=dtype)
            mask = mask.at[src, dst].set(w[edge_type - 1])
            diag = jnp.diagonal(mask)
            idx = jnp.arange(N)
            mask = mask.at[idx, idx].set(jnp.where(jnp.isneginf(diag), w[3], diag))
            return mask
        key = jax.random.key(seed)
        ks = jax.random.split(key, 20)
        p = lambda k, shape: jax.random.normal(k, shape, dtype=jnp.float32) * 0.02
        return {'x': jax.random.normal(ks[0], (N, IN_F), dtype=jnp.float32), 'edge_index': jax.random.randint(ks[1], (2, E), 0, N), 'edge_type': jax.random.randint(ks[2], (E,), 1, NUM_ETYPES + 1), 'edge_type_weights': jnp.ones((NUM_ETYPES,), jnp.float32) + 0.1 * jax.random.normal(ks[3], (NUM_ETYPES,), dtype=jnp.float32), 'wq': p(ks[4], (OUT_F, IN_F)), 'bq': p(ks[5], (OUT_F,)), 'wk': p(ks[6], (OUT_F, IN_F)), 'bk': p(ks[7], (OUT_F,)), 'wv': p(ks[8], (OUT_F, IN_F)), 'bv': p(ks[9], (OUT_F,)), 'wiq': p(ks[10], (OUT_F, OUT_F)), 'biq': p(ks[11], (OUT_F,)), 'wik': p(ks[12], (OUT_F, OUT_F)), 'bik': p(ks[13], (OUT_F,)), 'wiv': p(ks[14], (OUT_F, OUT_F)), 'biv': p(ks[15], (OUT_F,)), 'wo': p(ks[16], (OUT_F, OUT_F)), 'bo': p(ks[17], (OUT_F,))}
    _L0_gnn_all = _L0_gnn_setup()
    _L0_gnn_in = {k: v for k, v in _L0_gnn_all.items() if k in ('edge_type_weights', 'wq', 'bq', 'wk', 'bk', 'wv', 'bv', 'wiq', 'biq', 'wik', 'bik', 'wiv', 'biv', 'wo', 'bo')}
    del _L0_gnn_all

    def _L1_gnn_setup():
        import jax, jax.numpy as jnp
        import numpy as np
        N_NODES = 2048
        HID_IN = 1024
        HID_MID = 1500
        N_EDGES = 16384

        def _gcn_conv(x, W, b, src, dst, inv_sqrt_deg, n_nodes):
            h = x @ W
            norm = inv_sqrt_deg[src] * inv_sqrt_deg[dst]
            msg = h[src] * norm[:, None]
            out = jax.ops.segment_sum(msg, dst, num_segments=n_nodes)
            return out + b
        key = jax.random.key(seed)
        k1, k2, k3, k4, k5, k6 = jax.random.split(key, 6)
        x = jax.random.normal(k1, (N_NODES, HID_IN), dtype=jnp.float32)
        edge_index = jax.random.randint(k2, (2, N_EDGES), 0, N_NODES, dtype=jnp.int64)
        W1 = jax.random.normal(k3, (HID_IN, HID_MID), dtype=jnp.float32) / np.sqrt(HID_IN)
        b1 = jnp.zeros((HID_MID,), dtype=jnp.float32)
        W2 = jax.random.normal(k4, (HID_MID, HID_IN), dtype=jnp.float32) / np.sqrt(HID_MID)
        b2 = jnp.zeros((HID_IN,), dtype=jnp.float32)
        return {'x': x, 'edge_index': edge_index, 'W1': W1, 'b1': b1, 'W2': W2, 'b2': b2}
    _L1_gnn_all = _L1_gnn_setup()
    _L1_gnn_in = {k: v for k, v in _L1_gnn_all.items() if k in ('W1', 'b1', 'W2', 'b2')}
    del _L1_gnn_all

    def _L2_gnn_setup():
        import jax, jax.numpy as jnp
        import numpy as np
        N_NODES = 3125
        N_EDGES = 50000
        D = 1024

        def _sage_layer(h, edge_src, edge_dst, deg_inv, W_self, W_neigh, b):
            msg = h[edge_src]
            agg = jax.ops.segment_sum(msg, edge_dst, num_segments=h.shape[0])
            mean = agg * deg_inv[:, None]
            return h @ W_self + mean @ W_neigh + b
        key = jax.random.key(seed)
        ks = jax.random.split(key, 8)
        s = 1.0 / np.sqrt(D)
        return {'x': jax.random.normal(ks[0], (N_NODES, D), dtype=jnp.float32), 'edge_src': jax.random.randint(ks[1], (N_EDGES,), 0, N_NODES, dtype=jnp.int32), 'edge_dst': jax.random.randint(ks[2], (N_EDGES,), 0, N_NODES, dtype=jnp.int32), 'W_self0': jax.random.normal(ks[3], (D, D), dtype=jnp.float32) * s, 'W_neigh0': jax.random.normal(ks[4], (D, D), dtype=jnp.float32) * s, 'b0': jnp.zeros((D,), dtype=jnp.float32), 'W_self1': jax.random.normal(ks[5], (D, D), dtype=jnp.float32) * s, 'W_neigh1': jax.random.normal(ks[6], (D, D), dtype=jnp.float32) * s, 'b1': jnp.zeros((D,), dtype=jnp.float32)}
    _L2_gnn_all = _L2_gnn_setup()
    _L2_gnn_in = {k: v for k, v in _L2_gnn_all.items() if k in ('W_self0', 'W_neigh0', 'b0', 'W_self1', 'W_neigh1', 'b1')}
    del _L2_gnn_all

    def _L3_gnn_setup():
        import jax, jax.numpy as jnp
        import numpy as np
        INDIM = 1024
        OUTDIM = 1024
        NNZ = 8192
        N = 6250
        key = jax.random.key(seed)
        k1, k2, k3, k4, k5 = jax.random.split(key, 5)
        x = jax.random.normal(k1, (N, INDIM), dtype=jnp.float32)
        stdv = np.sqrt(6.0 / (INDIM + OUTDIM))
        nnz_weight = jax.random.uniform(k2, (NNZ,), dtype=jnp.float32, minval=-stdv, maxval=stdv)
        bias = jax.random.normal(k3, (OUTDIM,), dtype=jnp.float32) * 0.02
        row = jax.random.randint(k4, (NNZ,), 0, OUTDIM, dtype=jnp.int64)
        col = jax.random.randint(k5, (NNZ,), 0, INDIM, dtype=jnp.int64)
        edge_index = jnp.stack([row, col])
        return {'x': x, 'nnz_weight': nnz_weight, 'bias': bias, 'edge_index': edge_index}
    _L3_gnn_all = _L3_gnn_setup()
    _L3_gnn_in = {k: v for k, v in _L3_gnn_all.items() if k in ('bias',)}
    del _L3_gnn_all
    return {'x': x, 'src': src, 'dst': dst, 'edge_type_5': edge_type_5, 'edge_weight': edge_weight, 'L0_gnn_edge_type_weights': _L0_gnn_in['edge_type_weights'], 'L0_gnn_wq': _L0_gnn_in['wq'], 'L0_gnn_bq': _L0_gnn_in['bq'], 'L0_gnn_wk': _L0_gnn_in['wk'], 'L0_gnn_bk': _L0_gnn_in['bk'], 'L0_gnn_wv': _L0_gnn_in['wv'], 'L0_gnn_bv': _L0_gnn_in['bv'], 'L0_gnn_wiq': _L0_gnn_in['wiq'], 'L0_gnn_biq': _L0_gnn_in['biq'], 'L0_gnn_wik': _L0_gnn_in['wik'], 'L0_gnn_bik': _L0_gnn_in['bik'], 'L0_gnn_wiv': _L0_gnn_in['wiv'], 'L0_gnn_biv': _L0_gnn_in['biv'], 'L0_gnn_wo': _L0_gnn_in['wo'], 'L0_gnn_bo': _L0_gnn_in['bo'], 'L1_gnn_W1': _L1_gnn_in['W1'], 'L1_gnn_b1': _L1_gnn_in['b1'], 'L1_gnn_W2': _L1_gnn_in['W2'], 'L1_gnn_b2': _L1_gnn_in['b2'], 'L2_gnn_W_self0': _L2_gnn_in['W_self0'], 'L2_gnn_W_neigh0': _L2_gnn_in['W_neigh0'], 'L2_gnn_b0': _L2_gnn_in['b0'], 'L2_gnn_W_self1': _L2_gnn_in['W_self1'], 'L2_gnn_W_neigh1': _L2_gnn_in['W_neigh1'], 'L2_gnn_b1': _L2_gnn_in['b1'], 'L3_gnn_bias': _L3_gnn_in['bias']}

def reference(x, src, dst, edge_type_5, edge_weight, L0_gnn_edge_type_weights, L0_gnn_wq, L0_gnn_bq, L0_gnn_wk, L0_gnn_bk, L0_gnn_wv, L0_gnn_bv, L0_gnn_wiq, L0_gnn_biq, L0_gnn_wik, L0_gnn_bik, L0_gnn_wiv, L0_gnn_biv, L0_gnn_wo, L0_gnn_bo, L1_gnn_W1, L1_gnn_b1, L1_gnn_W2, L1_gnn_b2, L2_gnn_W_self0, L2_gnn_W_neigh0, L2_gnn_b0, L2_gnn_W_self1, L2_gnn_W_neigh1, L2_gnn_b1, L3_gnn_bias):
    import jax
    import jax.numpy as jnp

    def _L0_gnn_ref(x, edge_index, edge_type, edge_type_weights, wq, bq, wk, bk, wv, bv, wiq, biq, wik, bik, wiv, biv, wo, bo):
        import jax, jax.numpy as jnp
        import numpy as np
        N = 384
        E = 12288
        IN_F = 1024
        OUT_F = 1024
        H = 16
        D = OUT_F // H
        NUM_ETYPES = 4

        def _build_mask(edge_index, edge_type, edge_type_weights, dtype):
            src, dst = (edge_index[0], edge_index[1])
            w = jax.nn.softplus(edge_type_weights)
            mask = jnp.full((N, N), -jnp.inf, dtype=dtype)
            mask = mask.at[src, dst].set(w[edge_type - 1])
            diag = jnp.diagonal(mask)
            idx = jnp.arange(N)
            mask = mask.at[idx, idx].set(jnp.where(jnp.isneginf(diag), w[3], diag))
            return mask
        q = x @ wq.T + bq
        k = x @ wk.T + bk
        v = x @ wv.T + bv
        q2 = (q @ wiq.T + biq).reshape(N, H, D).transpose(1, 0, 2)
        k2 = (k @ wik.T + bik).reshape(N, H, D).transpose(1, 0, 2)
        v2 = (v @ wiv.T + biv).reshape(N, H, D).transpose(1, 0, 2)
        mask = _build_mask(edge_index, edge_type, edge_type_weights, x.dtype)
        scale = 1.0 / np.sqrt(D).astype(np.float32)
        scores = jnp.einsum('hnd,hmd->hnm', q2, k2) * scale + mask[None]
        attn = jax.nn.softmax(scores, axis=-1)
        out = jnp.einsum('hnm,hmd->hnd', attn, v2)
        out = out.transpose(1, 0, 2).reshape(N, OUT_F)
        return out @ wo.T + bo

    def _L1_gnn_ref(x, edge_index, W1, b1, W2, b2):
        import jax, jax.numpy as jnp
        import numpy as np
        N_NODES = 2048
        HID_IN = 1024
        HID_MID = 1500
        N_EDGES = 16384

        def _gcn_conv(x, W, b, src, dst, inv_sqrt_deg, n_nodes):
            h = x @ W
            norm = inv_sqrt_deg[src] * inv_sqrt_deg[dst]
            msg = h[src] * norm[:, None]
            out = jax.ops.segment_sum(msg, dst, num_segments=n_nodes)
            return out + b
        n = x.shape[0]
        loops = jnp.arange(n, dtype=edge_index.dtype)
        src = jnp.concatenate([edge_index[0], loops])
        dst = jnp.concatenate([edge_index[1], loops])
        deg = jax.ops.segment_sum(jnp.ones_like(dst, dtype=x.dtype), dst, num_segments=n)
        inv_sqrt_deg = jnp.where(deg > 0, jax.lax.rsqrt(jnp.maximum(deg, 1.0)), 0.0)
        h = _gcn_conv(x, W1, b1, src, dst, inv_sqrt_deg, n)
        h = jax.nn.relu(h)
        out = _gcn_conv(h, W2, b2, src, dst, inv_sqrt_deg, n)
        return out

    def _L2_gnn_ref(x, edge_src, edge_dst, W_self0, W_neigh0, b0, W_self1, W_neigh1, b1):
        import jax, jax.numpy as jnp
        import numpy as np
        N_NODES = 3125
        N_EDGES = 50000
        D = 1024

        def _sage_layer(h, edge_src, edge_dst, deg_inv, W_self, W_neigh, b):
            msg = h[edge_src]
            agg = jax.ops.segment_sum(msg, edge_dst, num_segments=h.shape[0])
            mean = agg * deg_inv[:, None]
            return h @ W_self + mean @ W_neigh + b
        N = x.shape[0]
        deg = jax.ops.segment_sum(jnp.ones_like(edge_dst, dtype=x.dtype), edge_dst, num_segments=N)
        deg_inv = 1.0 / jnp.maximum(deg, 1.0)
        h = jax.nn.relu(_sage_layer(x, edge_src, edge_dst, deg_inv, W_self0, W_neigh0, b0))
        out = _sage_layer(h, edge_src, edge_dst, deg_inv, W_self1, W_neigh1, b1)
        return out

    def _L3_gnn_ref(x, nnz_weight, bias, edge_index):
        import jax, jax.numpy as jnp
        import numpy as np
        INDIM = 1024
        OUTDIM = 1024
        NNZ = 8192
        N = 6250
        row, col = (edge_index[0], edge_index[1])
        W = jnp.zeros((OUTDIM, INDIM), dtype=nnz_weight.dtype).at[row, col].add(nnz_weight)
        return x @ W.T + bias
    edge_index = jnp.stack([src, dst])
    h = jnp.maximum(_layernorm(x, axis=-1), 0.0)
    x = x + _L0_gnn_ref(h, edge_index, edge_type_5, L0_gnn_edge_type_weights, L0_gnn_wq, L0_gnn_bq, L0_gnn_wk, L0_gnn_bk, L0_gnn_wv, L0_gnn_bv, L0_gnn_wiq, L0_gnn_biq, L0_gnn_wik, L0_gnn_bik, L0_gnn_wiv, L0_gnn_biv, L0_gnn_wo, L0_gnn_bo)
    h = jnp.maximum(_layernorm(x, axis=-1), 0.0)
    x = x + _L1_gnn_ref(h, edge_index, L1_gnn_W1, L1_gnn_b1, L1_gnn_W2, L1_gnn_b2)
    h = jnp.maximum(_layernorm(x, axis=-1), 0.0)
    x = x + _L2_gnn_ref(h, src, dst, L2_gnn_W_self0, L2_gnn_W_neigh0, L2_gnn_b0, L2_gnn_W_self1, L2_gnn_W_neigh1, L2_gnn_b1)
    h = jnp.maximum(_layernorm(x, axis=-1), 0.0)
    x = x + _L3_gnn_ref(h, edge_weight, L3_gnn_bias, edge_index)
    return x

_drawn_inputs = setup_inputs


def setup_inputs(seed=0):
    import zlib

    import numpy as np

    out = dict(_drawn_inputs(seed))
    spreads = {'L1_gnn_b1': (0.0, 0.1),
     'L1_gnn_b2': (0.0, 0.1),
     'L2_gnn_b0': (0.0, 0.1),
     'L2_gnn_b1': (0.0, 0.1)}
    factors = {'L0_gnn_edge_type_weights': 64.0,
     'L0_gnn_wq': 8.0,
     'L0_gnn_bq': 8.0,
     'L0_gnn_wk': 8.0,
     'L0_gnn_bk': 64.0,
     'L0_gnn_bv': 7.538,
     'L0_gnn_wiq': 8.0,
     'L0_gnn_biq': 42.075,
     'L0_gnn_wik': 8.0,
     'L0_gnn_bik': 64.0,
     'L0_gnn_biv': 4.761,
     'L0_gnn_bo': 2.953,
     'L3_gnn_bias': 3.803}
    for name, (base, spread) in spreads.items():
        noise = np.random.default_rng([zlib.crc32(name.encode()), seed]).standard_normal(out[name].shape)
        drawn = base * np.exp(spread * noise) if base else spread * noise
        out[name] = jnp.asarray(drawn.astype(out[name].dtype))
    for name, factor in factors.items():
        out[name] = (out[name] * factor).astype(out[name].dtype)
    return out
```

```python
from contextlib import ExitStack

import concourse.bass as bass
from concourse import mybir

ALU = mybir.AluOpType
ACT = mybir.ActivationFunctionType
F32 = mybir.dt.float32
F32R = mybir.dt.float32r
I32 = mybir.dt.int32

P = 128
BANK = 512
EPS = 1e-5
FAR = -3.0e37
ROUND = 12582912.0
ETYPES = 4

GROUP_BITS = 5
LOWEST = 8


def gnn_stack(nc, x, src, dst, etype, eweight, etw, wq, bq, wk, bk, wv, bv, wiq, biq, wik, bik, wiv, biv,
              wo, bo, w1, b1, w2, b2, wself0, wneigh0, sb0, wself1, wneigh1, sb1, b3, out):
    N, F = x.shape
    NT, KT = N // P, F // P
    E = src.shape[0]
    G = E // P
    MID = w1.shape[1]
    MT = -(-MID // P)
    LASTM = MID - (MT - 1) * P
    H = 16
    D = F // H
    SCALE = float(D) ** -0.5
    HALF = F // BANK
    SLOTS = 4
    assert G * GROUP_BITS + LOWEST < 254 and E % P == 0 and N == NT * P and D == 64 and KT == 8

    with ExitStack() as ctx:
        def sb(name, shape, dt=F32):
            return ctx.enter_context(nc.sbuf_tensor(name, shape, dt))

        def sem(name):
            return ctx.enter_context(nc.semaphore(name))

        x_sb = sb("x_sb", [P, NT, F])
        tmp = sb("tmp", [P, NT * F])
        a_hi, a_lo = (sb(f"a_{n}", [P, NT * F], F32R) for n in ("hi", "lo"))
        b_hi, b_lo = (sb(f"b_{n}", [P, NT * F], F32R) for n in ("hi", "lo"))
        c_act = sb("c_act", [P, 2 * NT * F], F32R)
        d_act = sb("d_act", [P, 2 * NT * F], F32R)
        raw = sb("raw", [P, SLOTS, F])
        ring_hi, ring_lo = (sb(f"ring_{n}", [P, SLOTS, F], F32R) for n in ("hi", "lo"))
        adj = sb("adj", [P, NT, N], F32R)
        mask = sb("mask", [P, NT, N])
        wedge = sb("wedge", [P, NT, N])
        row_isd = sb("row_isd", [P, N])
        row_inv = sb("row_inv", [P, N])
        col_isd = sb("col_isd", [P, 4])
        col_inv = sb("col_inv", [P, 4])
        iota_i = sb("iota_i", [P, N], I32)
        iota = sb("iota", [P, N])
        ident = sb("ident", [P, P])
        later = sb("later", [P, P])
        ones = sb("ones", [P, P], F32R)
        ROWS = dict(q=0, iq=8, k=16, ik=24, v=32, iv=40, o=48, mid=56, s0=56 + MT)
        NB = ROWS["s0"] + KT
        bias_rows = sb("bias_rows", [NB, P])
        bias = sb("bias", [P, NB])
        idx = sb("idx", [P, 5, G])
        dup = sb("dup", [P, G])
        pow2_i = sb("pow2_i", [P, G], I32)
        wt_hi = sb("wt_hi", [P, G], F32R)
        wt_lo = sb("wt_lo", [P, G])
        sp = sb("sp", [P, 4, ETYPES])
        stats = sb("stats", [P, NT, 2, 6])
        mv = sb("mv", [P, NT, 2])
        rstd = sb("rstd", [P, NT])
        mx = sb("mx", [P, 2 * NT])
        nmx = sb("nmx", [P, 2 * NT])
        rs = sb("rs", [P, 2 * NT])
        rinv = sb("rinv", [P, 2 * NT])
        deg2 = sb("deg2", [P, 4])
        ones32 = sb("ones32", [P, P])
        part = sb("part", [P, 1])
        ps = ctx.enter_context(nc.psum_tensor("ps", [P, 8, BANK], F32))

        tmp_n = tmp[:, :].rearrange("p (t f) -> p t f", t=NT)
        tmp_t = tmp[:, :].rearrange("p (k n) -> p k n", n=N)
        a_t = [t[:, :].rearrange("p (k n) -> p k n", n=N) for t in (a_hi, a_lo)]
        v_n = [t[:, :].rearrange("p (t f) -> p t f", t=NT) for t in (a_hi, a_lo)]
        b_t = [t[:, :].rearrange("p (k n) -> p k n", n=N) for t in (b_hi, b_lo)]
        b_n = [t[:, :].rearrange("p (t f) -> p t f", t=NT) for t in (b_hi, b_lo)]
        c_n = [c_act[:, j * NT * F:(j + 1) * NT * F].rearrange("p (t f) -> p t f", t=NT) for j in range(2)]
        q2 = [c_act[:, j * NT * F:(j + 1) * NT * F].rearrange("p (k n) -> p k n", n=N) for j in range(2)]
        k2 = [d_act[:, j * NT * F:(j + 1) * NT * F].rearrange("p (k n) -> p k n", n=N) for j in range(2)]
        m_t = [t[:, 0:MT * N].rearrange("p (k n) -> p k n", n=N) for t in (c_act, d_act)]
        stage_i = mask[0:G, :, :].rearrange("p t n -> p (t n)").bitcast(I32)
        stage = wedge[0:G, :, :].rearrange("p t n -> p (t n)")
        mask_i = mask[:, :, :].bitcast(I32)
        keyeq = wedge[:, 2, 0:P]
        code = [wedge[:, 2, P + j * G:P + (j + 1) * G] for j in range(2)]
        hot_b, hot_c = b_t[0][:, SLOTS:2 * SLOTS, :], b_t[1][:, 0:SLOTS, :]
        brow = mask[:, :, :].rearrange("p t n -> p (t n)")[:, 0:F]

        def unit_part(u, buf):
            if u == U_W2 - 1:
                return buf[:, u % SLOTS, :].rearrange("p (k c) -> p k c", c=P)[:, :, 0:LASTM]
            return buf[0:LASTM if u == U_S0 - 1 else P, u % SLOTS, :]

        def as32(ap):
            return ap.bitcast(F32)

        LAYER_IN = [a_t, b_t, a_t, b_t, a_t, b_t, q2]
        LAYER_OUT = [b_t, q2, b_t, k2, b_t]
        BIAS_COL = [ROWS[r] for r in ("q", "iq", "k", "ik", "v", "iv", "o")]
        CONSTS = 9
        TURNED = [wq, wiq, wk, wik, wv, wiv, wo]
        U_W1 = len(TURNED) * KT
        U_W2 = U_W1 + MT
        U_S0 = U_W2 + MT
        U_N1 = U_S0 + 2 * KT
        U_S1 = U_N1 + KT
        U_END = U_S1 + KT
        assert all(u % SLOTS == 0 for u in (U_W1, U_W2, U_S0, U_N1, U_S1, U_END))

        x_in = sem("x_in")
        ids_in = sem("ids_in")
        bias_in = sem("bias_in")
        etw_in = sem("etw_in")
        brow_in = sem("brow_in")
        out_done = sem("out_done")
        landed = [sem(f"landed{s}") for s in range(SLOTS)]
        consts = sem("consts")
        turned_up = sem("turned_up")
        w_hi = sem("w_hi")
        w_lo = sem("w_lo")
        w_used = sem("w_used")
        dve_step = sem("dve_step")
        soft_step = sem("soft_step")
        ids_flat = sem("ids_flat")
        turned_small = sem("turned_small")
        small_read = sem("small_read")
        keys_up = sem("keys_up")
        keys_read = sem("keys_read")
        hot = sem("hot")
        hot_used = sem("hot_used")
        bits_read = sem("bits_read")
        adj_raw = sem("adj_raw")
        adj_ready = sem("adj_ready")
        deg_up = sem("deg_up")
        isd_sq = sem("isd_sq")
        isd_rt = sem("isd_rt")
        deg_ready = sem("deg_ready")
        mask_ready = sem("mask_ready")
        wedge_ready = sem("wedge_ready")
        wedge_hi = sem("wedge_hi")
        wedge_lo = sem("wedge_lo")
        stats_up = sem("stats_up")
        var_up = sem("var_up")
        std_up = sem("std_up")
        normed = sem("normed")
        t_up = sem("t_up")
        t_hi = sem("t_hi")
        t_lo = sem("t_lo")
        acc_hi = sem("acc_hi")
        acc_free = sem("acc_free")
        v_up = sem("v_up")
        v_hi = sem("v_hi")
        v_lo = sem("v_lo")
        sc_up = sem("sc_up")
        sc_read = sem("sc_read")
        nmx_ready = sem("nmx_ready")
        exp_done = sem("exp_done")
        rinv_ready = sem("rinv_ready")
        p_ready = sem("p_ready")
        pt_up = sem("pt_up")
        pt_hi = sem("pt_hi")
        pt_lo = sem("pt_lo")
        pv_up = sem("pv_up")
        o_hi = sem("o_hi")
        o_lo = sem("o_lo")
        y_up = sem("y_up")
        x1_ready = sem("x1_ready")
        x2_ready = sem("x2_ready")
        x3_ready = sem("x3_ready")
        x4_ready = sem("x4_ready")
        xb_ready = sem("xb_ready")
        r_up = sem("r_up")
        n_hi = sem("n_hi")
        n_lo = sem("n_lo")
        g_up = sem("g_up")
        g_m = sem("g_m")
        g_hi = sem("g_hi")
        g_lo = sem("g_lo")
        m_r = sem("m_r")
        m_hi = sem("m_hi")
        m_lo = sem("m_lo")
        z_up = sem("z_up")
        z_hi = sem("z_hi")
        z_lo = sem("z_lo")
        s_up = sem("s_up")
        s_added = sem("s_added")
        h_up = sem("h_up")
        h_added = sem("h_added")
        f_up = sem("f_up")

        block = ctx.enter_context(nc.Block())

        @block.sync
        def _(sp_):
            eng = sp_
            eng.dma_start(x_sb[:, :, :], x.rearrange("(t p) f -> p t f", p=P)).then_inc(x_in, 16)
            for j, v in enumerate((src, dst, etype)):
                eng.dma_start(stage_i[:, j * P:(j + 1) * P], v.rearrange("(g p) -> g p", p=P)).then_inc(ids_in, 16)
            eng.dma_start(stage[:, 3 * P:4 * P], eweight.rearrange("(g p) -> g p", p=P)).then_inc(ids_in, 16)
            for s in range(SLOTS):
                eng.dma_start(raw[:, s, :], TURNED[0][s * P:(s + 1) * P, :]).then_inc(landed[s], 16)
            eng.wait_ge(consts, 1)
            for name, v in (("q", bq), ("iq", biq), ("k", bk), ("ik", bik), ("v", bv), ("iv", biv), ("o", bo),
                            ("s0", sb0)):
                eng.dma_start(bias_rows[ROWS[name]:ROWS[name] + KT, :], v.rearrange("(k p) -> k p", p=P)).then_inc(bias_in, 16)
            full = (MT - 1) * P
            eng.dma_start(bias_rows[ROWS["mid"]:ROWS["mid"] + MT - 1, :],
                          b1[0:full].rearrange("(k p) -> k p", p=P)).then_inc(bias_in, 16)
            r = ROWS["mid"] + MT - 1
            eng.dma_start(bias_rows[r:r + 1, 0:LASTM], b1[full:MID].rearrange("(a n) -> a n", a=1)).then_inc(bias_in, 16)
            eng.dma_start(sp[:, 0, :], etw.partition_broadcast(P)).then_inc(etw_in, 16)

            def free_raw(u):
                if isinstance(u, int) and u >= U_W1 + SLOTS:
                    eng.wait_ge(w_hi, u - 3)
                    eng.wait_ge(w_lo, u - 3)
                else:
                    eng.wait_ge(turned_up, u - 3)

            for s in range(SLOTS):
                free_raw(SLOTS + s)
                eng.dma_start(raw[:, s, :], TURNED[0][(SLOTS + s) * P:(SLOTS + s + 1) * P, :]).then_inc(landed[s], 16)
            for L in range(1, len(TURNED)):
                with eng.Fori(0, KT // SLOTS) as i:
                    for s in range(SLOTS):
                        eng.wait_ge(turned_up, i * SLOTS + (L * KT + s - 3))
                        eng.dma_start(raw[:, s, :], TURNED[L][bass.ds(i * (SLOTS * P) + s * P, P), :]).then_inc(landed[s], 16)

            def load_cols(w, o, u):
                s = u % SLOTS
                width = min(P, w.shape[1] - o * P)
                free_raw(u)
                eng.dma_start(raw[:, s, :].rearrange("p (k c) -> p k c", c=P)[:, :, 0:width],
                              w[:, o * P:o * P + width].rearrange("(k p) c -> p k c", p=P)).then_inc(landed[s], 16)

            def load_rows(w, k, u):
                s = u % SLOTS
                rows = min(P, w.shape[0] - k * P)
                free_raw(u)
                eng.dma_start(raw[0:rows, s, :], w[k * P:k * P + rows, :]).then_inc(landed[s], 16)

            for o in range(MT):
                load_cols(w1, o, U_W1 + o)
            for k in range(MT):
                load_rows(w2, k, U_W2 + k)
                if k == 0:
                    eng.wait_ge(sc_read, NT * H)
                    eng.dma_start(brow, b2.partition_broadcast(P)).then_inc(brow_in, 16)
            for o in range(KT):
                load_cols(wself0, o, U_S0 + 2 * o)
                load_cols(wneigh0, o, U_S0 + 2 * o + 1)
            for k in range(KT):
                load_rows(wneigh1, k, U_N1 + k)
            eng.wait_ge(xb_ready, NT)
            eng.dma_start(brow, sb1.partition_broadcast(P)).then_inc(brow_in, 16)
            for k in range(KT):
                load_rows(wself1, k, U_S1 + k)
            eng.wait_ge(xb_ready, 2 * NT)
            eng.dma_start(brow, b3.partition_broadcast(P)).then_inc(brow_in, 16)
            for t in range(NT):
                eng.wait_ge(x4_ready, t + 1)
                eng.dma_start(out[t * P:(t + 1) * P, :], x_sb[:, t, :]).then_inc(out_done, 16)
            eng.wait_ge(out_done, 16 * NT)

        @block.gpsimd
        def _(eng):
            eng.memset(bias_rows[:, :], 0.0).then_inc(consts, 1)
            eng.iota(iota_i[:, :], pattern=[[1, N]], base=0, channel_multiplier=0).then_inc(consts, 1)
            eng.memset(ones32[:, :], 1.0).then_inc(consts, 1)
            eng.wait_ge(consts, 3)
            eng.tensor_copy(iota[:, :], iota_i[:, :]).then_inc(consts, 1)
            eng.tensor_copy(ones[:, :], ones32[:, :]).then_inc(consts, 1)
            eng.wait_ge(consts, 5)
            eng.iota(iota_i[:, 0:P], pattern=[[1, P]], base=0, channel_multiplier=-1).then_inc(consts, 1)
            eng.wait_ge(consts, 6)
            eng.tensor_scalar(ident[:, :], iota_i[:, 0:P], 0.0, None, ALU.is_equal).then_inc(consts, 1)
            eng.tensor_scalar(later[:, :], iota_i[:, 0:P], 0.0, None, ALU.is_gt).then_inc(consts, 1)
            eng.tensor_scalar(part[:, :], iota_i[:, 0:1], -1.0, 1.0, ALU.mult, ALU.mult).then_inc(consts, 1)
            eng.wait_ge(consts, CONSTS)
            def norm_rows(h, par):
                for t in range(NT):
                    eng.wait_ge(rinv_ready, h + 1)
                    p = tmp[:, (par * NT + t) * N:(par * NT + t + 1) * N]
                    eng.tensor_scalar(p, p, rinv[:, par * NT + t:par * NT + t + 1], 1.0, ALU.mult,
                                      ALU.mult).then_inc(p_ready, 1)
            for h in range(H):
                norm_rows(h, h % 2)
            eng.wait_ge(deg_ready, 1)
            for t in range(NT):
                d = adj[:, t, t * P:(t + 1) * P]
                eng.tensor_tensor(d, as32(d), ident[:, :], ALU.add).then_inc(adj_ready, 1)
            def add_row(n, seen):
                eng.wait_ge(brow_in, 16 * n)
                for t in range(NT):
                    eng.wait_ge(normed, seen + t + 1)
                    eng.tensor_tensor(x_sb[:, t, :], x_sb[:, t, :], brow, ALU.add).then_inc(xb_ready, 1)
            add_row(1, NT)
            eng.wait_ge(h_up, HALF * NT)
            for t in range(NT):
                d = adj[:, t, t * P:(t + 1) * P]
                eng.tensor_tensor(d, as32(d), ident[:, :], ALU.subtract).then_inc(adj_ready, 1)
            add_row(2, 2 * NT)
            add_row(3, 3 * NT)

        @block.scalar
        def _(eng):
            def hi_of_unit(u, s, slot_free=True):
                if isinstance(u, int) and u >= U_W1:
                    if slot_free:
                        eng.wait_ge(w_used, u - 3)
                    eng.wait_ge(landed[s], 16 * (u // SLOTS + 1))
                    d, r = unit_part(u, ring_hi), unit_part(u, raw)
                    eng.activation(d, r, ACT.Copy).then_inc(w_hi, 1)
                else:
                    eng.wait_ge(turned_up, u + 1)
                    tp = 2 * (s % 2)
                    eng.activation(ring_hi[:, s, :], ps[:, tp:tp + 2, :].rearrange("p b c -> p (b c)"),
                                   ACT.Copy).then_inc(w_hi, 1)

            def roots(n):
                for t in range(NT):
                    eng.wait_ge(var_up, n * NT + t + 1)
                    eng.activation(rstd[:, t:t + 1], mv[:, t, 1:2], ACT.Sqrt).then_inc(std_up, 1)

            def turn_hi(n, tiles, func, dst):
                for k in range(tiles):
                    eng.wait_ge(t_up, n + k + 1)
                    eng.activation(dst[0][:, k:k + 1, :], ps[:, 6 + k % 2:7 + k % 2, 0:N], func).then_inc(t_hi, 1)

            eng.wait_ge(etw_in, 16)
            eng.wait_ge(soft_step, 1)
            eng.activation(sp[:, 1, :], sp[:, 1, :], ACT.Exp, scale=-1.0).then_inc(soft_step, 1)
            eng.wait_ge(soft_step, 2)
            eng.activation(sp[:, 2, :], sp[:, 1, :], ACT.Ln, bias=1.0).then_inc(soft_step, 1)
            roots(0)
            turn_hi(0, KT, ACT.Relu, a_t)
            eng.wait_ge(hot_used, G)
            for t in range(NT):
                eng.activation(adj[:, t, :], ps[:, 3 + t, 0:N], ACT.Copy).then_inc(adj_raw, 1)
            eng.wait_ge(isd_sq, 1)
            eng.activation(row_isd[:, :], row_isd[:, :], ACT.Sqrt).then_inc(isd_rt, 1)
            eng.activation(col_isd[:, 0:NT], col_isd[:, 0:NT], ACT.Sqrt).then_inc(isd_rt, 1)

            hi_of_unit(0, 0)
            hi_of_unit(1, 1)

            def turned_out(L, u, o, s):
                eng.wait_ge(w_used, u + 1)
                src_ = ps[:, 4 + s % 2:5 + s % 2, 0:N]
                row = bass.ds(o + BIAS_COL[L], 1)
                if L < 5:
                    eng.activation(LAYER_OUT[L][0][:, bass.ds(o, 1), :], src_, ACT.Identity,
                                   bias=bias[:, row]).then_inc(acc_hi, 1)
                else:
                    eng.activation(tmp_t[:, bass.ds(o, 1), :], src_, ACT.Identity,
                                   bias=bias[:, row]).then_inc(acc_free, 1)

            def exps(h, par):
                for t in range(NT):
                    p = tmp[:, (par * NT + t) * N:(par * NT + t + 1) * N]
                    c = slice(par * NT + t, par * NT + t + 1)
                    eng.wait_ge(nmx_ready, h + 1)
                    eng.activation(p, p, ACT.Exp, bias=nmx[:, c], accum_out=rs[:, c]).then_inc(exp_done, 1)

            def probs_hi(h, par):
                for j in range(NT):
                    eng.wait_ge(pt_up, h * NT + j + 1)
                    eng.activation(b_t[0][:, par * NT + j, :], ps[:, 3 + j, 0:N], ACT.Copy).then_inc(pt_hi, 1)

            def heads_hi(h, pair, par):
                r = slice(D * par, D * par + D)
                eng.wait_ge(pv_up, h + 1)
                eng.activation(q2[0][r, bass.ds(pair, 1), :], ps[r, 6 + par:7 + par, 0:N],
                               ACT.Copy).then_inc(o_hi, 1)

            for L in range(len(TURNED)):
                if L == 6:
                    exps(0, 0)
                    exps(1, 1)
                    probs_hi(0, 0)
                    for h in range(H):
                        if h + 1 < H:
                            probs_hi(h + 1, (h + 1) % 2)
                        if h + 2 < H:
                            exps(h + 2, h % 2)
                        heads_hi(h, h // 2, h % 2)
                if L < 6:
                    with eng.Fori(0, KT // SLOTS) as i:
                        for s in range(SLOTS):
                            turned_out(L, i * SLOTS + (L * KT + s), i * SLOTS + s, s)
                            hi_of_unit(i * SLOTS + (L * KT + s + 2), (s + 2) % SLOTS)
                else:
                    for o in range(KT):
                        turned_out(L, L * KT + o, o, o % SLOTS)
                        hi_of_unit(L * KT + o + 2, (o + 2) % SLOTS)
                if L == 5:
                    for t in range(NT):
                        eng.wait_ge(v_up, t + 1)
                        tp = 2 * (t % 2)
                        eng.activation(v_n[0][:, t, :], ps[:, tp:tp + 2, :].rearrange("p b c -> p (b c)"),
                                       ACT.Copy).then_inc(v_hi, 1)

            def relu_tile(n, o, u, dst, rows=P):
                eng.wait_ge(w_used, u + 1)
                if n >= SLOTS:
                    eng.wait_ge(m_lo, n - SLOTS + 1)
                b = ROWS["mid"] + o if n < MT else ROWS["s0"] + o
                t = tmp_t[0:rows, n % SLOTS, :]
                eng.activation(t, ps[0:rows, 4 + n % 2, 0:N], ACT.Relu, bias=bias[0:rows, b:b + 1]).then_inc(m_r, 1)
                eng.wait_ge(m_r, n + 1)
                eng.activation(dst[0][0:rows, o, :], t, ACT.Copy).then_inc(m_hi, 1)

            def aggregated_hi(n, dst):
                for k in range(KT):
                    eng.wait_ge(g_m, n + k + 1)
                    eng.activation(dst[0][:, k, :], tmp_t[:, k, :], ACT.Copy).then_inc(g_hi, 1)

            roots(1)
            for t in range(NT):
                eng.wait_ge(r_up, t + 1)
                eng.activation(b_n[0][:, t, :], tmp_n[:, t, :], ACT.Copy).then_inc(n_hi, 1)
            aggregated_hi(0, a_t)
            for o in range(MT):
                relu_tile(o, o, U_W1 + o, m_t, P if o < MT - 1 else LASTM)
                hi_of_unit(U_W1 + o + 2, (o + 2) % SLOTS)
            for k in range(MT):
                hi_of_unit(U_W2 + k + 2, (k + 2) % SLOTS)

            def rows_hi(n, u_last, dst, scaled):
                for half in range(HALF):
                    for t in range(NT):
                        if half * NT + t < HALF * NT - 1:
                            eng.wait_ge(z_up, n + half * NT + t + 1)
                        else:
                            eng.wait_ge(w_used, u_last + 1)
                        d = dst[0][:, t, half * BANK:(half + 1) * BANK]
                        q = ps[:, 2 * t + half, :]
                        scale = col_isd[:, t:t + 1] if scaled else 1.0
                        eng.activation(d, q, ACT.Copy, scale=scale).then_inc(z_hi, 1)

            rows_hi(0, U_S0 - 1, b_n, True)
            roots(2)
            for t in range(NT):
                eng.wait_ge(normed, 2 * NT + t + 1)
                eng.activation(c_n[0][:, t, :], tmp_n[:, t, :], ACT.Relu).then_inc(n_hi, 1)
            turn_hi(KT, KT, ACT.Relu, a_t)
            aggregated_hi(KT, b_t)
            for o in range(KT):
                relu_tile(MT + o, o, U_S0 + 2 * o + 1, k2)
                for j in range(2):
                    hi_of_unit(U_S0 + 2 * o + 2 + j, (2 * o + 2 + j) % SLOTS)
            for k in range(NT):
                eng.activation(b_t[0][:, k, :], wedge[:, k, :], ACT.Copy).then_inc(wedge_hi, 1)
            for k in range(KT):
                hi_of_unit(U_N1 + k + 2, (k + 2) % SLOTS)
            rows_hi(HALF * NT - 1, U_S1 - 1, c_n, False)
            for k in range(KT - 2):
                hi_of_unit(U_S1 + k + 2, (k + 2) % SLOTS)
            roots(3)
            turn_hi(2 * KT, NT, ACT.Relu, a_t)

        @block.vector
        def _(eng):
            steps = [0]

            def link(ins):
                steps[0] += 1
                ins.then_inc(dve_step, 1)
                eng.wait_ge(dve_step, steps[0])

            def lo_of_unit(u, s):
                eng.wait_ge(w_hi, u + 1)
                if isinstance(u, int) and u >= U_W1:
                    d, r, h = (unit_part(u, b) for b in (ring_lo, raw, ring_hi))
                    eng.tensor_tensor(d, r, as32(h), ALU.subtract).then_inc(w_lo, 1)
                else:
                    tp = 2 * (s % 2)
                    eng.tensor_tensor(ring_lo[:, s, :], ps[:, tp:tp + 2, :].rearrange("p b c -> p (b c)"),
                                      as32(ring_hi[:, s, :]), ALU.subtract).then_inc(w_lo, 1)

            def layer_norm(n, ready, first, each, cols=F):
                for t in range(NT):
                    eng.wait_ge(ready, first + each * t)
                    for half in range(HALF):
                        eng.bn_stats(stats[:, t, half, :], x_sb[:, t, half * BANK:(half + 1) * BANK])\
                           .then_inc(stats_up, 1)
                    eng.wait_ge(stats_up, (n * NT + t + 1) * HALF)
                    link(eng.bn_aggr(mv[:, t, :], stats[:, t, :, :].rearrange("p a b -> p (a b)")))
                    eng.tensor_scalar(mv[:, t, 1:2], mv[:, t, 1:2], EPS, None, ALU.add).then_inc(var_up, 1)
                for t in range(NT):
                    eng.wait_ge(std_up, n * NT + t + 1)
                    link(eng.reciprocal(rstd[:, t:t + 1], rstd[:, t:t + 1]))
                    eng.tensor_scalar(tmp_n[:, t, 0:cols], x_sb[:, t, 0:cols], mv[:, t, 0:1], rstd[:, t:t + 1],
                                      ALU.subtract, ALU.mult).then_inc(normed, 1)

            def turn_lo(n, tiles, dst):
                for k in range(tiles):
                    eng.wait_ge(t_hi, n + k + 1)
                    eng.scalar_tensor_tensor(dst[1][:, k, :], ps[:, 6 + k % 2, 0:N], 0.0, as32(dst[0][:, k, :]),
                                             ALU.max, ALU.subtract).then_inc(t_lo, 1)

            eng.wait_ge(etw_in, 16)
            eng.scalar_tensor_tensor(sp[:, 1, :], sp[:, 0, :], -1.0, sp[:, 0, :], ALU.mult, ALU.max).then_inc(soft_step, 1)
            eng.wait_ge(ids_in, 16 * 4)
            link(eng.tensor_copy(stage[:, 0:3 * P], stage_i[:, 0:3 * P]))
            eng.scalar_tensor_tensor(stage[:, 4 * P:5 * P], stage[:, 0:P], float(N), stage[:, P:2 * P],
                                     ALU.mult, ALU.add).then_inc(ids_flat, 1)
            eng.wait_ge(turned_small, 1)
            link(eng.tensor_copy(idx[:, :, :], ps[:, 6, 0:5 * G].rearrange("p (a g) -> p a g", a=5)))
            eng.tensor_copy(bias[:, :], ps[:, 7, 0:NB]).then_inc(small_read, 1)
            layer_norm(0, x_in, 16, 0)
            eng.wait_ge(consts, CONSTS)
            for g in range(G):
                if g % 4 == 0:
                    eng.wait_ge(keys_up, g // 4 + 1)
                if g:
                    eng.wait_ge(keys_read, g)
                eng.scalar_tensor_tensor(keyeq, ps[:, 6 + (g // 4) % 2, (g % 4) * P:(g % 4 + 1) * P],
                                         idx[:, 4, g:g + 1], later[:, :], ALU.is_equal, ALU.mult,
                                         accum_out=dup[:, g:g + 1]).then_inc(keys_read, 1)
            eng.wait_ge(keys_read, G)
            et = idx[:, 2, :]
            c0, c1 = code
            link(eng.tensor_scalar(c0, et, 0.0, float(ETYPES), ALU.is_equal, ALU.mult))
            link(eng.scalar_tensor_tensor(c0, et, -1.0, c0, ALU.add, ALU.add))
            link(eng.tensor_scalar(c1, iota[:, 0:G], float(GROUP_BITS), float(LOWEST), ALU.mult, ALU.add))
            link(eng.tensor_tensor(c0, c0, c1, ALU.add))
            link(eng.tensor_scalar(c1, dup[:, :], 0.0, float(2 ** 23), ALU.is_equal, ALU.mult))
            link(eng.tensor_tensor(pow2_i[:, :], c0, c1, ALU.mult))
            link(eng.tensor_copy(wt_hi[:, :], idx[:, 3, :]))
            link(eng.tensor_tensor(wt_lo[:, :], idx[:, 3, :], as32(wt_hi[:, :]), ALU.subtract))
            turn_lo(0, KT, a_t)

            def hot_rows(n, col, s, plain, weighted):
                g1 = bass.ds(col, 1)
                last = eng.tensor_scalar(b_t[0][:, s, :], iota[:, :], idx[:, plain, g1], None, ALU.is_equal)
                for dst_, index, weight in weighted:
                    last = eng.tensor_scalar(dst_[:, s, :], iota[:, :], idx[:, index, g1],
                                             None if weight is None else weight[:, g1], ALU.is_equal,
                                             *(() if weight is None else (ALU.mult,)))
                last.then_inc(hot, 1)

            for n0, plain, weighted in ((0, 0, ((hot_b, 1, pow2_i[:, :].bitcast(F32)), (hot_c, 1, None))),
                                        (G, 1, ((hot_b, 0, as32(wt_hi[:, :])), (hot_c, 0, wt_lo)))):
                if n0:
                    for t in range(NT):
                        if t == 0:
                            eng.wait_ge(hot_used, G)
                        eng.tensor_scalar(mask_i[:, t, :], ps[:, t, 0:N].bitcast(I32), 23, None,
                                          ALU.logical_shift_right).then_inc(bits_read, 1)
                for s in range(SLOTS):
                    if n0:
                        eng.wait_ge(hot_used, n0 + s - 3)
                    hot_rows(n0 + s, s, s, plain, weighted)
                with eng.Fori(1, G // SLOTS) as i:
                    for s in range(SLOTS):
                        eng.wait_ge(hot_used, i * SLOTS + (n0 + s - 3))
                        hot_rows(None, i * SLOTS + s, s, plain, weighted)

            eng.wait_ge(soft_step, 3)
            link(eng.scalar_tensor_tensor(sp[:, 3, :], sp[:, 0, :], 0.0, sp[:, 2, :], ALU.max, ALU.add))
            link(eng.tensor_scalar(sp[:, 3, :], sp[:, 3, :], 1.0 / SCALE, None, ALU.mult))
            for t in range(NT):
                ex, t1, t2, t3 = mask_i[:, t, :], tmp[:, 0:N], tmp[:, N:2 * N], tmp[:, 2 * N:3 * N]
                g1 = 1.0 / GROUP_BITS
                if t == 0:
                    eng.wait_ge(bits_read, NT)
                link(eng.tensor_scalar(t1, ex, -(LOWEST + 1.5), g1, ALU.add, ALU.mult))
                link(eng.tensor_scalar(t1, t1, ROUND, -ROUND, ALU.add, ALU.add))
                link(eng.scalar_tensor_tensor(t1, t1, -float(GROUP_BITS), ex, ALU.mult, ALU.add))
                link(eng.tensor_scalar(t2, t1, float(LOWEST), sp[:, 3, 0:1], ALU.is_equal, ALU.mult))
                for c in range(1, ETYPES):
                    link(eng.tensor_scalar(t3, t1, float(LOWEST + c), sp[:, 3, c:c + 1], ALU.is_equal, ALU.mult))
                    link(eng.tensor_tensor(t2, t2, t3, ALU.add))
                link(eng.tensor_scalar(t1, iota[:, :], -float(t * P), part[:, 0:1], ALU.add, ALU.is_equal))
                link(eng.tensor_scalar(t3, t1, -1.0, -FAR, ALU.add, ALU.mult))
                link(eng.scalar_tensor_tensor(t1, t1, sp[:, 3, ETYPES - 1:ETYPES], t3, ALU.mult, ALU.add))
                link(eng.copy_predicated(t1, ex, t2))
                link(eng.tensor_copy(mask[:, t, :], t1))
            eng.tensor_copy(part[:, :], part[:, :]).then_inc(mask_ready, 1)
            eng.wait_ge(deg_up, 1)
            dcol = ps[:, 7, 0:2 * NT].rearrange("p (t a) -> p t a", a=2)[:, :, 0]
            drow = ps[:, 6, 0:N]
            eng.tensor_scalar(row_isd[:, :], drow, 1.0, None, ALU.add)
            eng.tensor_scalar(col_isd[:, 0:NT], dcol, 1.0, None, ALU.add).then_inc(isd_sq, 1)
            link(eng.tensor_scalar(row_inv[:, :], drow, 1.0, None, ALU.max))
            link(eng.tensor_scalar(col_inv[:, 0:NT], dcol, 1.0, None, ALU.max))
            eng.reciprocal(row_inv[:, :], row_inv[:, :])
            eng.reciprocal(col_inv[:, 0:NT], col_inv[:, 0:NT])
            eng.wait_ge(isd_rt, 2)
            eng.reciprocal(row_isd[:, :], row_isd[:, :])
            eng.reciprocal(col_isd[:, 0:NT], col_isd[:, 0:NT]).then_inc(deg_ready, 1)
            eng.wait_ge(deg_ready, 1)
            for t in range(NT):
                eng.tensor_copy(wedge[:, t, :], ps[:, t, 0:N]).then_inc(wedge_ready, 1)

            lo_of_unit(0, 0)
            lo_of_unit(1, 1)

            def turned_out(L, u, o, s):
                if L >= 5:
                    return
                eng.wait_ge(acc_hi, u + 1)
                hi, lo = (LAYER_OUT[L][j][:, bass.ds(o, 1), :] for j in range(2))
                src_ = ps[:, 4 + s % 2:5 + s % 2, 0:N]
                eng.scalar_tensor_tensor(lo, src_, bias[:, bass.ds(o + BIAS_COL[L], 1)], as32(hi), ALU.add,
                                         ALU.subtract).then_inc(acc_free, 1)

            def mask_scores(h, par):
                for t in range(NT):
                    p = tmp[:, (par * NT + t) * N:(par * NT + t + 1) * N]
                    eng.wait_ge(sc_up, h * NT + t + 1)
                    eng.tensor_tensor_reduce(p, ps[:, t, 0:N], mask[:, t, :], SCALE, FAR, ALU.add, ALU.max,
                                             mx[:, par * NT + t:par * NT + t + 1]).then_inc(sc_read, 1)
                eng.wait_ge(sc_read, h * NT + NT)
                c = slice(par * NT, par * NT + NT)
                eng.tensor_scalar(nmx[:, c], mx[:, c], -1.0, None, ALU.mult).then_inc(nmx_ready, 1)

            def row_sums(h, par):
                eng.wait_ge(exp_done, h * NT + NT)
                c = slice(par * NT, par * NT + NT)
                eng.reciprocal(rinv[:, c], rs[:, c]).then_inc(rinv_ready, 1)

            def probs_lo(h, par):
                for j in range(NT):
                    eng.wait_ge(pt_hi, h * NT + j + 1)
                    eng.tensor_tensor(b_t[1][:, par * NT + j, :], ps[:, 3 + j, 0:N],
                                      as32(b_t[0][:, par * NT + j, :]), ALU.subtract).then_inc(pt_lo, 1)

            def heads_lo(h, pair, par):
                r = slice(D * par, D * par + D)
                eng.wait_ge(o_hi, h + 1)
                eng.tensor_tensor(q2[1][r, bass.ds(pair, 1), :], ps[r, 6 + par:7 + par, 0:N],
                                  as32(q2[0][r, bass.ds(pair, 1), :]), ALU.subtract).then_inc(o_lo, 1)

            for L in range(len(TURNED)):
                if L == 6:
                    mask_scores(0, 0)
                    row_sums(0, 0)
                    mask_scores(1, 1)
                    row_sums(1, 1)
                    probs_lo(0, 0)
                    for h in range(H):
                        if h + 2 < H:
                            mask_scores(h + 2, h % 2)
                        if h + 1 < H:
                            probs_lo(h + 1, (h + 1) % 2)
                        if h + 2 < H:
                            row_sums(h + 2, h % 2)
                        heads_lo(h, h // 2, h % 2)
                if L < 6:
                    with eng.Fori(0, KT // SLOTS) as i:
                        for s in range(SLOTS):
                            turned_out(L, i * SLOTS + (L * KT + s), i * SLOTS + s, s)
                            lo_of_unit(i * SLOTS + (L * KT + s + 2), (s + 2) % SLOTS)
                else:
                    for o in range(KT):
                        lo_of_unit(L * KT + o + 2, (o + 2) % SLOTS)
                if L == 5:
                    for t in range(NT):
                        eng.wait_ge(v_hi, t + 1)
                        tp = 2 * (t % 2)
                        eng.tensor_tensor(v_n[1][:, t, :], ps[:, tp:tp + 2, :].rearrange("p b c -> p (b c)"),
                                          as32(v_n[0][:, t, :]), ALU.subtract).then_inc(v_lo, 1)
            for t in range(NT):
                eng.wait_ge(y_up, t + 1)
                tp = 2 * (t % 2)
                eng.tensor_tensor(x_sb[:, t, :], ps[:, tp:tp + 2, :].rearrange("p b c -> p (b c)"),
                                  x_sb[:, t, :], ALU.add).then_inc(x1_ready, 1)

            def aggregated_lo(n, row, dst):
                for k in range(KT):
                    eng.wait_ge(g_up, n + k + 1)
                    eng.tensor_tensor(tmp_t[:, k, :], ps[:, 6 + k % 2, 0:N], row[:, :], ALU.mult).then_inc(g_m, 1)
                    eng.wait_ge(g_hi, n + k + 1)
                    eng.tensor_tensor(dst[1][:, k, :], tmp_t[:, k, :], as32(dst[0][:, k, :]),
                                      ALU.subtract).then_inc(g_lo, 1)

            def relu_lo(n, o, dst, rows=P):
                eng.wait_ge(m_hi, n + 1)
                eng.tensor_tensor(dst[1][0:rows, o, :], tmp_t[0:rows, n % SLOTS, :], as32(dst[0][0:rows, o, :]),
                                  ALU.subtract).then_inc(m_lo, 1)

            layer_norm(1, x1_ready, 1, 1)
            for t in range(NT):
                eng.wait_ge(normed, NT + t + 1)
                eng.tensor_scalar(tmp_n[:, t, :], tmp_n[:, t, :], 0.0, col_isd[:, t:t + 1], ALU.max,
                                  ALU.mult).then_inc(r_up, 1)
            for t in range(NT):
                eng.wait_ge(n_hi, t + 1)
                eng.tensor_tensor(b_n[1][:, t, :], tmp_n[:, t, :], as32(b_n[0][:, t, :]),
                                  ALU.subtract).then_inc(n_lo, 1)
            aggregated_lo(0, row_isd, a_t)
            for o in range(MT):
                relu_lo(o, o, m_t, P if o < MT - 1 else LASTM)
                lo_of_unit(U_W1 + o + 2, (o + 2) % SLOTS)
            for k in range(MT):
                lo_of_unit(U_W2 + k + 2, (k + 2) % SLOTS)

            def rows_lo(n, dst, scaled):
                for half in range(HALF):
                    for t in range(NT):
                        n += 1
                        eng.wait_ge(z_hi, n)
                        hi, lo = (dst[j][:, t, half * BANK:(half + 1) * BANK] for j in range(2))
                        q = ps[:, 2 * t + half, :]
                        if scaled:
                            last = eng.scalar_tensor_tensor(lo, q, col_isd[:, t:t + 1], as32(hi), ALU.mult,
                                                            ALU.subtract)
                        else:
                            last = eng.tensor_tensor(lo, q, as32(hi), ALU.subtract)
                        last.then_inc(z_lo, 1)

            def add_aggregated(n, col, ready):
                for half in range(HALF):
                    for t in range(NT):
                        eng.wait_ge(h_up, n + half * NT + t + 1)
                        xs = x_sb[:, t, half * BANK:(half + 1) * BANK]
                        eng.scalar_tensor_tensor(xs, ps[:, 6 + (half * NT + t) % 2, :], col[:, t:t + 1], xs,
                                                 ALU.mult, ALU.add).then_inc(ready, 1)

            rows_lo(0, b_n, True)
            eng.wait_ge(xb_ready, NT)
            add_aggregated(0, col_isd, x2_ready)
            layer_norm(2, x2_ready, NT + 1, 1)
            for t in range(NT):
                eng.wait_ge(n_hi, NT + t + 1)
                eng.scalar_tensor_tensor(c_n[1][:, t, :], tmp_n[:, t, :], 0.0, as32(c_n[0][:, t, :]), ALU.max,
                                         ALU.subtract).then_inc(n_lo, 1)
            turn_lo(KT, KT, a_t)
            aggregated_lo(KT, row_inv, b_t)
            for o in range(KT):
                relu_lo(MT + o, o, k2)
                for j in range(2):
                    lo_of_unit(U_S0 + 2 * o + 2 + j, (2 * o + 2 + j) % SLOTS)
            eng.wait_ge(wedge_hi, NT)
            for k in range(NT):
                eng.tensor_tensor(b_t[1][:, k, :], wedge[:, k, :], as32(b_t[0][:, k, :]),
                                  ALU.subtract).then_inc(wedge_lo, 1)
            for k in range(KT):
                lo_of_unit(U_N1 + k + 2, (k + 2) % SLOTS)
            rows_lo(HALF * NT, c_n, False)
            for k in range(KT - 2):
                lo_of_unit(U_S1 + k + 2, (k + 2) % SLOTS)
            eng.wait_ge(xb_ready, 2 * NT)
            for half in range(HALF):
                for t in range(NT):
                    if half * NT + t < HALF * NT - 1:
                        eng.wait_ge(s_up, half * NT + t + 1)
                    else:
                        eng.wait_ge(w_used, U_END)
                    xs = x_sb[:, t, half * BANK:(half + 1) * BANK]
                    eng.tensor_tensor(xs, ps[:, 2 * t + half, :], xs, ALU.add).then_inc(s_added, 1)
            eng.wait_ge(s_added, HALF * NT)
            add_aggregated(HALF * NT, col_inv, x3_ready)
            layer_norm(3, x3_ready, NT + 1, 1, N)
            turn_lo(2 * KT, NT, a_t)
            eng.wait_ge(xb_ready, 3 * NT)
            for t in range(NT):
                eng.wait_ge(f_up, t + 1)
                eng.tensor_tensor(x_sb[:, t, 0:N], ps[:, t, 0:N], x_sb[:, t, 0:N], ALU.add).then_inc(x4_ready, 1)

        @block.tensor
        def _(eng):
            def mm3(out_, l, r, first, last):
                eng.matmul(out_, l[0], r[0], start=first, stop=False)
                eng.matmul(out_, l[1], r[0], start=False, stop=False)
                return eng.matmul(out_, l[0], r[1], start=False, stop=last)

            eng.wait_ge(consts, CONSTS)
            eng.wait_ge(ids_flat, 1)
            for j in range(5):
                eng.transpose(ps[:, 6, j * G:(j + 1) * G], stage[:, j * P:(j + 1) * P], ident[0:G, 0:G])
            eng.wait_ge(bias_in, 16 * 10)
            eng.transpose(ps[:, 7, 0:NB], bias_rows[:, :], ident[0:NB, 0:NB]).then_inc(turned_small, 1)
            eng.wait_ge(small_read, 1)
            for g in range(G):
                if g % 4 == 0 and g >= 8:
                    eng.wait_ge(keys_read, g - 4)
                tr = eng.transpose(ps[:, 6 + (g // 4) % 2, (g % 4) * P:(g % 4 + 1) * P],
                                   idx[:, 4, g:g + 1].to_broadcast([P, P]), ident[:, :])
                if g % 4 == 3:
                    tr.then_inc(keys_up, 1)
            eng.wait_ge(keys_read, G)

            def turn(n, tiles, ready):
                for k in range(tiles):
                    if k >= 2:
                        eng.wait_ge(t_lo, n + k - 1)
                    for t in range(NT):
                        if k == 0:
                            eng.wait_ge(normed, ready + t + 1)
                        tr = eng.transpose(ps[:, 6 + k % 2, t * P:(t + 1) * P], tmp_n[:, t, k * P:(k + 1) * P],
                                           ident[:, :])
                    tr.then_inc(t_up, 1)

            turn(0, KT, 0)

            def edge_pass1(g, s, first, last):
                eng.wait_ge(hot, g + 1)
                for m in range(NT):
                    l = b_t[0][:, s, m * P:(m + 1) * P]
                    eng.matmul(ps[:, m, 0:N], l, hot_b[:, s, :], start=first, stop=last)
                    mm = eng.matmul(ps[:, NT + m, 0:N], l, hot_c[:, s, :], start=first, stop=last)
                mm.then_inc(hot_used, 1)

            def edge_pass2(g, s, first, last):
                eng.wait_ge(hot, g + 1)
                for m in range(NT):
                    l = b_t[0][:, s, m * P:(m + 1) * P]
                    eng.matmul(ps[:, m, 0:N], l, hot_b[:, s, :], start=first, stop=False)
                    mm = eng.matmul(ps[:, m, 0:N], l, hot_c[:, s, :], start=False, stop=last)
                mm.then_inc(hot_used, 1)

            for base, edge_pass in ((0, edge_pass1), (G, edge_pass2)):
                if base:
                    eng.wait_ge(bits_read, NT)
                for s in range(SLOTS):
                    edge_pass(base + s, s, s == 0, False)
                with eng.Fori(1, G // SLOTS - 1) as i:
                    for s in range(SLOTS):
                        edge_pass(i * SLOTS + (base + s), s, False, False)
                for s in range(SLOTS):
                    edge_pass(base + G - SLOTS + s, s, False, s == SLOTS - 1)
            eng.wait_ge(adj_raw, NT)
            eng.wait_ge(t_lo, KT)
            for s in range(NT):
                eng.matmul(ps[:, 6, 0:N], ones[:, :], adj[:, s, :], start=s == 0, stop=s == NT - 1)
            for t in range(NT):
                for s in range(NT):
                    mm = eng.matmul(ps[:, 7, 2 * t:2 * t + 2], adj[:, s, t * P:(t + 1) * P], ones[:, 0:2],
                                    start=s == 0, stop=s == NT - 1)
            mm.then_inc(deg_up, 1)

            def turn_unit(landed_value, s):
                eng.wait_ge(landed[s], landed_value)
                for k in range(KT):
                    tr = eng.transpose(ps[:, 2 * (s % 2) + k // 4, (k % 4) * P:(k % 4 + 1) * P],
                                       raw[:, s, k * P:(k + 1) * P], ident[:, :])
                tr.then_inc(turned_up, 1)

            eng.wait_ge(wedge_ready, NT)
            turn_unit(16, 0)
            turn_unit(16, 1)

            def ring(s, k, m=P):
                return [b[:, s, k * P:k * P + m] for b in (ring_hi, ring_lo)]

            def turned_unit(L, u, s, landed_value, bank_free=True):
                eng.wait_ge(w_lo, u + 1)
                if bank_free:
                    eng.wait_ge(acc_free, u - 1)
                if L in (1, 3, 5):
                    eng.wait_ge(acc_free, L * KT - 1)
                for k in range(KT):
                    if k == KT - 1 and L in (1, 3, 5):
                        eng.wait_ge(acc_free, L * KT)
                    mm = mm3(ps[:, 4 + s % 2, 0:N], ring(s, k), [b[:, k, :] for b in LAYER_IN[L]], k == 0, k == KT - 1)
                mm.then_inc(w_used, 1)
                if landed_value is not None:
                    turn_unit(landed_value, (s + 2) % SLOTS)

            def scores(h, par):
                r = slice(D * par, D * par + D)
                for t in range(NT):
                    if h >= 1:
                        eng.wait_ge(sc_read, (h - 1) * NT + t + 1)
                    mm3(ps[:, t, 0:N], [q[r, h // 2, t * P:(t + 1) * P] for q in q2], [k[r, h // 2, :] for k in k2],
                        True, True).then_inc(sc_up, 1)

            def turn_probs(h, par):
                for j in range(NT):
                    if h >= 1:
                        eng.wait_ge(pt_lo, (h - 1) * NT + j + 1)
                    for t in range(NT):
                        if j == 0:
                            eng.wait_ge(p_ready, h * NT + t + 1)
                        o = (par * NT + t) * N + j * P
                        tr = eng.transpose(ps[:, 3 + j, t * P:(t + 1) * P], tmp[:, o:o + P], ident[:, :])
                    tr.then_inc(pt_up, 1)

            def attend(h, par):
                if h >= 2:
                    eng.wait_ge(o_lo, h - 1)
                for j in range(NT):
                    eng.wait_ge(pt_lo, h * NT + j + 1)
                    mm = mm3(ps[:, 6 + par, 0:N], [v[:, j, (h // 2) * P:(h // 2 + 1) * P] for v in v_n],
                             [q[:, par * NT + j, :] for q in b_t], j == 0, j == NT - 1)
                mm.then_inc(pv_up, 1)

            for L in range(len(TURNED)):
                if L == 0:
                    for s in range(SLOTS):
                        turned_unit(0, s, s, 16 * ((s + 2) // SLOTS + 1), s >= 2)
                    with eng.Fori(1, KT // SLOTS) as i:
                        for s in range(SLOTS):
                            turned_unit(0, i * SLOTS + s, s, i * 16 + 16 * ((s + 2) // SLOTS + 1))
                elif L < 6:
                    with eng.Fori(0, KT // SLOTS) as i:
                        for s in range(SLOTS):
                            v = L * KT + s + 2
                            turned_unit(L, i * SLOTS + (L * KT + s), s, i * 16 + 16 * (v // SLOTS + 1))
                if L == 5:
                    eng.wait_ge(acc_free, 6 * KT)
                    eng.wait_ge(w_lo, 6 * KT + 2)
                    for t in range(NT):
                        if t == 2:
                            eng.wait_ge(v_lo, 1)
                        for o in range(KT):
                            tr = eng.transpose(ps[:, 2 * (t % 2) + o // 4, (o % 4) * P:(o % 4 + 1) * P],
                                               tmp_t[:, o, t * P:(t + 1) * P], ident[:, :])
                        tr.then_inc(v_up, 1)
                    eng.wait_ge(v_lo, NT)
                    eng.wait_ge(mask_ready, 1)
                    scores(0, 0)
                    scores(1, 1)
                    turn_probs(0, 0)
                    for h in range(H):
                        if h + 2 < H:
                            scores(h + 2, h % 2)
                        if h + 1 < H:
                            turn_probs(h + 1, (h + 1) % 2)
                        attend(h, h % 2)
                    eng.wait_ge(o_lo, H)
                if L == 6:
                    for o in range(KT):
                        u = L * KT + o
                        more = 16 * ((u + 2) // SLOTS + 1) if o + 2 < KT else None
                        turned_unit(6, u, o % SLOTS, more)
            eng.wait_ge(acc_free, 7 * KT)
            for t in range(NT):
                if t == 2:
                    eng.wait_ge(x1_ready, 1)
                for o in range(KT):
                    tr = eng.transpose(ps[:, 2 * (t % 2) + o // 4, (o % 4) * P:(o % 4 + 1) * P],
                                       tmp_t[:, o, t * P:(t + 1) * P], ident[:, :])
                tr.then_inc(y_up, 1)

            def aggregate(n, act):
                for k in range(KT):
                    if k >= 2:
                        eng.wait_ge(g_m, n + k - 1)
                    for s in range(NT):
                        for j in range(2):
                            mm = eng.matmul(ps[:, 6 + k % 2, 0:N], act[j][:, s, k * P:(k + 1) * P], adj[:, s, :],
                                            start=s == 0 and j == 0, stop=s == NT - 1 and j == 1)
                    mm.then_inc(g_up, 1)

            def relu_unit(n, u, act, first, last, m=P, counts=None):
                s = u % SLOTS
                eng.wait_ge(w_lo, u + 1)
                if first and n >= 2:
                    eng.wait_ge(m_r, n - 1)
                for k in range(KT):
                    if counts is not None:
                        eng.wait_ge(counts[0], counts[1] + k + 1)
                    mm = mm3(ps[0:m, 4 + n % 2, 0:N], ring(s, k, m), [b[:, k, :] for b in act],
                             first and k == 0, last and k == KT - 1)
                mm.then_inc(w_used, 1)

            def rows_layer(act, u0, tiles, lastrows, ready, up, bank_free):
                for k in range(tiles):
                    u = u0 + k
                    r = P if k < tiles - 1 else lastrows
                    eng.wait_ge(w_lo, u + 1)
                    eng.wait_ge(m_lo, ready + k + 1)
                    for half in range(HALF):
                        for t in range(NT):
                            if k == 0:
                                bank_free(half * NT + t)
                            mm = mm3(ps[:, 2 * t + half, :], [a[0:r, k, t * P:(t + 1) * P] for a in act],
                                     [b[0:r, u % SLOTS, half * BANK:(half + 1) * BANK] for b in (ring_hi, ring_lo)],
                                     k == 0, k == tiles - 1)
                            if half * NT + t == HALF * NT - 1:
                                mm.then_inc(w_used, 1)
                            elif k == tiles - 1:
                                mm.then_inc(up, 1)

            def aggregate_rows(n, zs, act):
                for half in range(HALF):
                    eng.wait_ge(z_lo, zs + (half + 1) * NT)
                    for t in range(NT):
                        b = half * NT + t
                        if n + b >= 2 and b >= 2:
                            eng.wait_ge(x2_ready if n == 0 else x3_ready, b - 1)
                        for s in range(NT):
                            for j in range(2):
                                mm = eng.matmul(ps[:, 6 + b % 2, :], adj[:, s, t * P:(t + 1) * P],
                                                act[j][:, s, half * BANK:(half + 1) * BANK],
                                                start=s == 0 and j == 0, stop=s == NT - 1 and j == 1)
                        mm.then_inc(h_up, 1)

            eng.wait_ge(adj_ready, NT)
            eng.wait_ge(n_lo, NT)
            aggregate(0, b_n)
            for o in range(MT):
                relu_unit(o, U_W1 + o, a_t, True, True, P if o < MT - 1 else LASTM,
                          (g_lo, 0) if o == 0 else None)
            rows_layer(m_t, U_W2, MT, LASTM, 0, z_up, lambda b: eng.wait_ge(m_r, MT) if b == 0 else None)
            aggregate_rows(0, 0, b_n)
            turn(KT, KT, 2 * NT)
            eng.wait_ge(adj_ready, 2 * NT)
            eng.wait_ge(n_lo, 2 * NT)
            eng.wait_ge(t_lo, 2 * KT)
            aggregate(KT, c_n)
            for o in range(KT):
                relu_unit(MT + o, U_S0 + 2 * o, a_t, True, False)
                relu_unit(MT + o, U_S0 + 2 * o + 1, b_t, False, True, P, (g_lo, KT) if o == 0 else None)
            rows_layer(k2, U_N1, KT, P, MT, z_up, lambda b: eng.wait_ge(m_r, MT + KT) if b == 0 else None)
            rows_layer(k2, U_S1, KT, P, MT, s_up, lambda b: eng.wait_ge(z_lo, HALF * NT + b + 1))
            aggregate_rows(HALF * NT, HALF * NT, c_n)
            turn(2 * KT, NT, 3 * NT)
            eng.wait_ge(t_lo, 2 * KT + NT)
            eng.wait_ge(wedge_lo, NT)
            for t in range(NT):
                for k in range(NT):
                    mm = mm3(ps[:, t, 0:N], [a[:, k, t * P:(t + 1) * P] for a in a_t], [b[:, k, :] for b in b_t],
                             k == 0, k == NT - 1)
                mm.then_inc(f_up, 1)


_INS = ['x', 'src', 'dst', 'edge_type_5', 'edge_weight', 'L0_gnn_edge_type_weights', 'L0_gnn_wq', 'L0_gnn_bq',
        'L0_gnn_wk', 'L0_gnn_bk', 'L0_gnn_wv', 'L0_gnn_bv', 'L0_gnn_wiq', 'L0_gnn_biq', 'L0_gnn_wik', 'L0_gnn_bik',
        'L0_gnn_wiv', 'L0_gnn_biv', 'L0_gnn_wo', 'L0_gnn_bo', 'L1_gnn_W1', 'L1_gnn_b1', 'L1_gnn_W2', 'L1_gnn_b2',
        'L2_gnn_W_self0', 'L2_gnn_W_neigh0', 'L2_gnn_b0', 'L2_gnn_W_self1', 'L2_gnn_W_neigh1', 'L2_gnn_b1',
        'L3_gnn_bias']


def kernel(**inputs):
    import numpy as _np
    import concourse.bacc as _bacc
    from concourse import mybir as _mybir
    from concourse.bass_utils import run_bass_kernel_spmd as _run

    nc = _bacc.Bacc("TRN2", target_bir_lowering=False, num_devices=1)
    arrays, args = {}, []
    for name in _INS:
        a = _np.ascontiguousarray(inputs[name])
        arrays[f"in_{name}_dram"] = a
        args.append(nc.dram_tensor(f"in_{name}_dram", a.shape, _mybir.dt.from_np(a.dtype), kind="ExternalInput").ap())
    shape = arrays["in_x_dram"].shape
    args.append(nc.dram_tensor("out_0_dram", shape, _mybir.dt.float32, kind="ExternalOutput").ap())
    gnn_stack(nc, *args)
    r = _run(nc, [arrays], core_ids=[0])
    return r.results[0]["out_0_dram"]
```

```python
from contextlib import ExitStack

import concourse.bass as bass
from concourse import mybir

ALU = mybir.AluOpType
ACT = mybir.ActivationFunctionType
F32 = mybir.dt.float32
F32R = mybir.dt.float32r
I32 = mybir.dt.int32
BF16 = mybir.dt.bfloat16
F16 = mybir.dt.float16

P = 128
BANK = 512
EPS = 1e-5
FAR = -3.0e37
ROUND = 12582912.0
ETYPES = 4

GROUP_BITS = 5
LOWEST = 6


def gnn_stack(nc, x, src, dst, etype, eweight, etw, wq, bq, wk, bk, wv, bv, wiq, biq, wik, bik, wiv, biv,
              wo, bo, w1, b1, w2, b2, wself0, wneigh0, sb0, wself1, wneigh1, sb1, b3, out):
    N, F = x.shape
    NT, KT = N // P, F // P
    E = src.shape[0]
    G = E // P
    MID = w1.shape[1]
    MT = -(-MID // P)
    LASTM = MID - (MT - 1) * P
    H = 16
    D = F // H
    SCALE = float(D) ** -0.5
    HALF = F // BANK
    SLOTS = 4
    AHEAD = 3
    assert G * GROUP_BITS + LOWEST < 254 and E % P == 0 and N == NT * P and D == 64 and KT == 8

    with ExitStack() as ctx:
        def sb(name, shape, dt=F32):
            return ctx.enter_context(nc.sbuf_tensor(name, shape, dt))

        def sem(name):
            return ctx.enter_context(nc.semaphore(name))

        x_sb = sb("x_sb", [P, NT, F])
        tmp = sb("tmp", [P, NT * F])
        a_hi, a_lo = (sb(f"a_{n}", [P, NT * F], F32R) for n in ("hi", "lo"))
        b_hi, b_lo = (sb(f"b_{n}", [P, NT * F], F32R) for n in ("hi", "lo"))
        c_act = sb("c_act", [P, 2 * NT * F], F32R)
        d_act = sb("d_act", [P, 2 * NT * F], F32R)
        raw = sb("raw", [P, SLOTS, F])
        ring_hi, ring_lo = (sb(f"ring_{n}", [P, SLOTS, F], F32R) for n in ("hi", "lo"))
        adj = sb("adj", [P, NT, N], F32R)
        mask = sb("mask", [P, NT, N])
        wedge = sb("wedge", [P, NT, N])
        row_isd = sb("row_isd", [P, N])
        row_inv = sb("row_inv", [P, N])
        col_isd = sb("col_isd", [P, 4])
        col_inv = sb("col_inv", [P, 4])
        iota_i = sb("iota_i", [P, N], I32)
        iota = sb("iota", [P, N])
        iota_h = sb("iota_h", [P, N], F16)
        hot = sb("hot", [P, SLOTS, 3, N], BF16)
        ident = sb("ident", [P, P])
        later = sb("later", [P, P])
        ones = sb("ones", [P, P], F32R)
        ROWS = dict(q=0, iq=8, k=16, ik=24, v=32, iv=40, o=48, mid=56, s0=56 + MT)
        NB = ROWS["s0"] + KT
        bias_rows = sb("bias_rows", [NB, P])
        bias = sb("bias", [P, NB])
        idx = sb("idx", [P, 5, G])
        dup = sb("dup", [P, G])
        pow2_i = sb("pow2_i", [P, G], I32)
        wt_hi = sb("wt_hi", [P, G], F32R)
        wt_lo = sb("wt_lo", [P, G])
        sp = sb("sp", [P, 4, ETYPES])
        stats = sb("stats", [P, NT, 2, 6])
        mv = sb("mv", [P, NT, 2])
        rstd = sb("rstd", [P, NT])
        mx = sb("mx", [P, AHEAD * NT])
        nmx = sb("nmx", [P, AHEAD * NT])
        rs = sb("rs", [P, AHEAD * NT])
        rinv = sb("rinv", [P, AHEAD * NT])
        deg2 = sb("deg2", [P, 4])
        ones32 = sb("ones32", [P, P])
        part = sb("part", [P, 1])
        ps = ctx.enter_context(nc.psum_tensor("ps", [P, 8, BANK], F32))

        tmp_n = tmp[:, :].rearrange("p (t f) -> p t f", t=NT)
        tmp_t = tmp[:, :].rearrange("p (k n) -> p k n", n=N)
        a_t = [t[:, :].rearrange("p (k n) -> p k n", n=N) for t in (a_hi, a_lo)]
        v_n = [t[:, :].rearrange("p (t f) -> p t f", t=NT) for t in (a_hi, a_lo)]
        b_t = [t[:, :].rearrange("p (k n) -> p k n", n=N) for t in (b_hi, b_lo)]
        b_n = [t[:, :].rearrange("p (t f) -> p t f", t=NT) for t in (b_hi, b_lo)]
        c_n = [c_act[:, j * NT * F:(j + 1) * NT * F].rearrange("p (t f) -> p t f", t=NT) for j in range(2)]
        q2 = [c_act[:, j * NT * F:(j + 1) * NT * F].rearrange("p (k n) -> p k n", n=N) for j in range(2)]
        k2 = [d_act[:, j * NT * F:(j + 1) * NT * F].rearrange("p (k n) -> p k n", n=N) for j in range(2)]
        m_t = [t[:, 0:MT * N].rearrange("p (k n) -> p k n", n=N) for t in (c_act, d_act)]
        stage_i = mask[0:G, :, :].rearrange("p t n -> p (t n)").bitcast(I32)
        stage = wedge[0:G, :, :].rearrange("p t n -> p (t n)")
        prob_tiles = [tmp[:, j * NT * N:(j + 1) * NT * N] for j in range(2)] + [
            hot[:, :, :, :].rearrange("p s j n -> p (s j n)")[:, 0:2 * NT * N].bitcast(F32)]
        mask_i = mask[:, :, :].bitcast(I32)
        keyeq = wedge[:, 2, 0:P]
        code = [wedge[:, 2, P + j * G:P + (j + 1) * G] for j in range(2)]
        hot_dst, hot_wh, hot_wl = k2[0][:, 0:SLOTS, :], k2[0][:, SLOTS:2 * SLOTS, :], k2[1][:, 0:SLOTS, :]
        brow = mask[:, :, :].rearrange("p t n -> p (t n)")[:, 0:F]

        def unit_part(u, buf):
            if u == U_W2 - 1:
                return buf[:, u % SLOTS, :].rearrange("p (k c) -> p k c", c=P)[:, :, 0:LASTM]
            return buf[0:LASTM if u == U_S0 - 1 else P, u % SLOTS, :]

        def prob(h, t, c=slice(0, N)):
            return prob_tiles[h % AHEAD][:, t * N + c.start:t * N + c.stop]

        def stat(buf, h, t=None):
            c = h % AHEAD * NT
            return buf[:, c:c + NT] if t is None else buf[:, c + t:c + t + 1]

        def as32(ap):
            return ap.bitcast(F32)

        LAYER_IN = [a_t, b_t, a_t, b_t, a_t, b_t, q2]
        LAYER_OUT = [b_t, q2, b_t, k2, b_t]
        BIAS_COL = [ROWS[r] for r in ("q", "iq", "k", "ik", "v", "iv", "o")]
        CONSTS = 10
        GU = G // (2 * KT)
        BITS, COUNTS, WEIGHTS = (6, 7, 0), (1, 2, 3), (4, 5, 6)
        assert GU * 2 * KT == G
        TURNED = [wq, wiq, wk, wik, wv, wiv, wo]
        U_W1 = len(TURNED) * KT
        U_W2 = U_W1 + MT
        U_S0 = U_W2 + MT
        U_N1 = U_S0 + 2 * KT
        U_S1 = U_N1 + KT
        U_END = U_S1 + KT
        assert all(u % SLOTS == 0 for u in (U_W1, U_W2, U_S0, U_N1, U_S1, U_END))

        x_in = [sem(f"x_in{t}") for t in range(NT)]
        ids_in = sem("ids_in")
        bias_in = sem("bias_in")
        etw_in = sem("etw_in")
        brow_in = sem("brow_in")
        out_done = sem("out_done")
        landed = [sem(f"landed{s}") for s in range(SLOTS)]
        consts = sem("consts")
        turned_up = sem("turned_up")
        w_hi = sem("w_hi")
        w_lo = sem("w_lo")
        w_used = sem("w_used")
        dve_step = sem("dve_step")
        pool_step = sem("pool_step")
        soft_step = sem("soft_step")
        ids_flat = sem("ids_flat")
        turned_small = sem("turned_small")
        small_read = sem("small_read")
        keys_up = sem("keys_up")
        keys_read = sem("keys_read")
        hot_ready = sem("hot_ready")
        weighed = sem("weighed")
        hot_used = sem("hot_used")
        bits_read = sem("bits_read")
        adj_raw = sem("adj_raw")
        adj_ready = sem("adj_ready")
        deg_up = sem("deg_up")
        isd_sq = sem("isd_sq")
        isd_rt = sem("isd_rt")
        deg_ready = sem("deg_ready")
        mask_ready = sem("mask_ready")
        wedge_ready = sem("wedge_ready")
        wedge_hi = sem("wedge_hi")
        wedge_lo = sem("wedge_lo")
        stats_up = sem("stats_up")
        var_up = sem("var_up")
        std_up = sem("std_up")
        normed = sem("normed")
        t_up = sem("t_up")
        t_hi = sem("t_hi")
        t_lo = sem("t_lo")
        acc_hi = sem("acc_hi")
        acc_free = sem("acc_free")
        v_up = sem("v_up")
        v_hi = sem("v_hi")
        v_lo = sem("v_lo")
        sc_up = sem("sc_up")
        sc_read = sem("sc_read")
        nmx_ready = sem("nmx_ready")
        exp_done = sem("exp_done")
        rinv_ready = sem("rinv_ready")
        p_ready = sem("p_ready")
        pt_up = sem("pt_up")
        pt_hi = sem("pt_hi")
        pt_lo = sem("pt_lo")
        pv_up = sem("pv_up")
        o_hi = sem("o_hi")
        o_lo = sem("o_lo")
        y_up = sem("y_up")
        x1_ready = sem("x1_ready")
        x2_ready = sem("x2_ready")
        x3_ready = sem("x3_ready")
        x4_ready = sem("x4_ready")
        xb_ready = sem("xb_ready")
        r_up = sem("r_up")
        n_hi = sem("n_hi")
        n_lo = sem("n_lo")
        g_up = sem("g_up")
        g_m = sem("g_m")
        g_hi = sem("g_hi")
        g_lo = sem("g_lo")
        m_r = sem("m_r")
        m_hi = sem("m_hi")
        m_lo = sem("m_lo")
        z_up = sem("z_up")
        z_hi = sem("z_hi")
        z_lo = sem("z_lo")
        s_up = sem("s_up")
        s_added = sem("s_added")
        h_up = sem("h_up")
        h_added = sem("h_added")
        f_up = sem("f_up")

        block = ctx.enter_context(nc.Block())

        @block.sync
        def _(sp_):
            eng = sp_
            for j, v in enumerate((src, dst, etype)):
                eng.dma_start(stage_i[:, j * P:(j + 1) * P], v.rearrange("(g p) -> g p", p=P)).then_inc(ids_in, 16)
            eng.dma_start(stage[:, 3 * P:4 * P], eweight.rearrange("(g p) -> g p", p=P)).then_inc(ids_in, 16)
            for t in range(NT):
                eng.dma_start(x_sb[:, t, :], x[t * P:(t + 1) * P, :]).then_inc(x_in[t], 16)
            for s in range(2):
                eng.dma_start(raw[:, s, :], TURNED[0][s * P:(s + 1) * P, :]).then_inc(landed[s], 16)
            eng.wait_ge(consts, 1)
            for name, v in (("q", bq), ("iq", biq), ("k", bk), ("ik", bik), ("v", bv), ("iv", biv), ("o", bo),
                            ("s0", sb0)):
                eng.dma_start(bias_rows[ROWS[name]:ROWS[name] + KT, :], v.rearrange("(k p) -> k p", p=P)).then_inc(bias_in, 16)
            full = (MT - 1) * P
            eng.dma_start(bias_rows[ROWS["mid"]:ROWS["mid"] + MT - 1, :],
                          b1[0:full].rearrange("(k p) -> k p", p=P)).then_inc(bias_in, 16)
            r = ROWS["mid"] + MT - 1
            eng.dma_start(bias_rows[r:r + 1, 0:LASTM], b1[full:MID].rearrange("(a n) -> a n", a=1)).then_inc(bias_in, 16)
            for s in range(2, SLOTS):
                eng.dma_start(raw[:, s, :], TURNED[0][s * P:(s + 1) * P, :]).then_inc(landed[s], 16)
            eng.dma_start(sp[:, 0, :], etw.partition_broadcast(P)).then_inc(etw_in, 16)

            def free_raw(u):
                if isinstance(u, int) and u >= U_W1 + SLOTS:
                    eng.wait_ge(w_hi, u - 3)
                    eng.wait_ge(w_lo, u - 3)
                else:
                    eng.wait_ge(turned_up, u - 3)

            for s in range(SLOTS):
                free_raw(SLOTS + s)
                eng.dma_start(raw[:, s, :], TURNED[0][(SLOTS + s) * P:(SLOTS + s + 1) * P, :]).then_inc(landed[s], 16)
            for L in range(1, len(TURNED)):
                with eng.Fori(0, KT // SLOTS) as i:
                    for s in range(SLOTS):
                        eng.wait_ge(turned_up, i * SLOTS + (L * KT + s - 3))
                        eng.dma_start(raw[:, s, :], TURNED[L][bass.ds(i * (SLOTS * P) + s * P, P), :]).then_inc(landed[s], 16)

            def load_cols(w, o, u):
                s = u % SLOTS
                width = min(P, w.shape[1] - o * P)
                free_raw(u)
                eng.dma_start(raw[:, s, :].rearrange("p (k c) -> p k c", c=P)[:, :, 0:width],
                              w[:, o * P:o * P + width].rearrange("(k p) c -> p k c", p=P)).then_inc(landed[s], 16)

            def load_rows(w, k, u):
                s = u % SLOTS
                rows = min(P, w.shape[0] - k * P)
                free_raw(u)
                eng.dma_start(raw[0:rows, s, :], w[k * P:k * P + rows, :]).then_inc(landed[s], 16)

            for o in range(MT):
                load_cols(w1, o, U_W1 + o)
            for k in range(MT):
                load_rows(w2, k, U_W2 + k)
                if k == 0:
                    eng.wait_ge(sc_read, NT * H)
                    eng.dma_start(brow, b2.partition_broadcast(P)).then_inc(brow_in, 16)
            for o in range(KT):
                load_cols(wself0, o, U_S0 + 2 * o)
                load_cols(wneigh0, o, U_S0 + 2 * o + 1)
            for k in range(KT):
                load_rows(wneigh1, k, U_N1 + k)
            eng.wait_ge(xb_ready, NT)
            eng.dma_start(brow, sb1.partition_broadcast(P)).then_inc(brow_in, 16)
            for k in range(KT):
                load_rows(wself1, k, U_S1 + k)
            eng.wait_ge(xb_ready, 2 * NT)
            eng.dma_start(brow, b3.partition_broadcast(P)).then_inc(brow_in, 16)
            for t in range(NT):
                eng.wait_ge(x4_ready, t + 1)
                eng.dma_start(out[t * P:(t + 1) * P, :], x_sb[:, t, :]).then_inc(out_done, 16)
            eng.wait_ge(out_done, 16 * NT)

        @block.gpsimd
        def _(eng):
            eng.memset(bias_rows[:, :], 0.0).then_inc(consts, 1)
            eng.iota(iota_i[:, 0:P], pattern=[[1, P]], base=0, channel_multiplier=-1).then_inc(consts, 1)
            eng.wait_ge(consts, 2)
            eng.tensor_scalar(ident[:, :], iota_i[:, 0:P], 0.0, None, ALU.is_equal).then_inc(consts, 1)
            eng.tensor_scalar(later[:, :], iota_i[:, 0:P], 0.0, None, ALU.is_gt).then_inc(consts, 1)
            eng.tensor_scalar(part[:, :], iota_i[:, 0:1], -1.0, 1.0, ALU.mult, ALU.mult).then_inc(consts, 1)
            eng.memset(ones32[:, :], 1.0).then_inc(consts, 1)
            eng.wait_ge(consts, 6)
            eng.iota(iota_i[:, :], pattern=[[1, N]], base=0, channel_multiplier=0).then_inc(consts, 1)
            eng.tensor_copy(ones[:, :], ones32[:, :]).then_inc(consts, 1)
            eng.wait_ge(consts, 8)
            eng.tensor_copy(iota[:, :], iota_i[:, :]).then_inc(consts, 1)
            eng.tensor_copy(iota_h[:, :], iota_i[:, :]).then_inc(consts, 1)
            eng.wait_ge(consts, CONSTS)

            steps = [0]

            def link(ins):
                steps[0] += 1
                ins.then_inc(pool_step, 1)
                eng.wait_ge(pool_step, steps[0])

            eng.wait_ge(etw_in, 16)
            link(eng.tensor_scalar(sp[:, 3, :], sp[:, 0, :], 0.0, None, ALU.max))
            link(eng.tensor_scalar(sp[:, 1, :], sp[:, 0, :], 0.0, None, ALU.min))
            eng.tensor_tensor(sp[:, 1, :], sp[:, 3, :], sp[:, 1, :], ALU.subtract).then_inc(soft_step, 1)
            eng.wait_ge(soft_step, 3)
            link(eng.tensor_tensor(sp[:, 3, :], sp[:, 3, :], sp[:, 2, :], ALU.add))
            link(eng.tensor_scalar(sp[:, 3, :], sp[:, 3, :], 1.0 / SCALE, None, ALU.mult))
            for t in range(NT):
                ex, t1, t2, t3 = mask_i[:, t, :], tmp[:, 0:N], tmp[:, N:2 * N], tmp[:, 2 * N:3 * N]
                g1 = 1.0 / GROUP_BITS
                if t == 0:
                    eng.wait_ge(bits_read, NT)
                link(eng.tensor_copy(t2, ex))
                link(eng.tensor_scalar(t1, t2, -(LOWEST + 1.5), g1, ALU.add, ALU.mult))
                link(eng.tensor_scalar(t1, t1, ROUND, -ROUND, ALU.add, ALU.add))
                link(eng.tensor_scalar(t1, t1, -float(GROUP_BITS), None, ALU.mult))
                link(eng.tensor_tensor(t1, t1, t2, ALU.add))
                link(eng.tensor_scalar(t2, t1, float(LOWEST), sp[:, 3, 0:1], ALU.is_equal, ALU.mult))
                for c in range(1, ETYPES):
                    link(eng.tensor_scalar(t3, t1, float(LOWEST + c), sp[:, 3, c:c + 1], ALU.is_equal, ALU.mult))
                    link(eng.tensor_tensor(t2, t2, t3, ALU.add))
                link(eng.tensor_scalar(t1, iota[:, :], -float(t * P), part[:, 0:1], ALU.add, ALU.is_equal))
                link(eng.tensor_scalar(t3, t1, -1.0, -FAR, ALU.add, ALU.mult))
                link(eng.tensor_scalar(t1, t1, sp[:, 3, ETYPES - 1:ETYPES], None, ALU.mult))
                link(eng.tensor_tensor(t1, t1, t3, ALU.add))
                link(eng.tensor_scalar(t3, ex, 0.0, None, ALU.is_equal))
                link(eng.tensor_tensor(t1, t1, t3, ALU.mult))
                eng.tensor_tensor(mask[:, t, :], t1, t2, ALU.add).then_inc(mask_ready, 1)
                eng.wait_ge(mask_ready, t + 1)
            for h in range(H):
                for t in range(NT):
                    eng.wait_ge(rinv_ready, h + 1)
                    eng.tensor_scalar(prob(h, t), prob(h, t), stat(rinv, h, t), 1.0, ALU.mult,
                                      ALU.mult).then_inc(p_ready, 1)
            eng.wait_ge(deg_ready, 1)
            for t in range(NT):
                d = adj[:, t, t * P:(t + 1) * P]
                eng.tensor_tensor(d, as32(d), ident[:, :], ALU.add).then_inc(adj_ready, 1)
            def add_row(n, seen):
                eng.wait_ge(brow_in, 16 * n)
                for t in range(NT):
                    eng.wait_ge(normed, seen + t + 1)
                    eng.tensor_tensor(x_sb[:, t, :], x_sb[:, t, :], brow, ALU.add).then_inc(xb_ready, 1)
            add_row(1, NT)
            eng.wait_ge(h_up, HALF * NT)
            for t in range(NT):
                d = adj[:, t, t * P:(t + 1) * P]
                eng.tensor_tensor(d, as32(d), ident[:, :], ALU.subtract).then_inc(adj_ready, 1)
            add_row(2, 2 * NT)
            add_row(3, 3 * NT)

        @block.scalar
        def _(eng):
            def hi_of_unit(u, s, slot_free=True):
                if isinstance(u, int) and u >= U_W1:
                    if slot_free:
                        eng.wait_ge(w_used, u - 3)
                    eng.wait_ge(landed[s], 16 * (u // SLOTS + 1))
                    d, r = unit_part(u, ring_hi), unit_part(u, raw)
                    eng.activation(d, r, ACT.Copy).then_inc(w_hi, 1)
                else:
                    eng.wait_ge(turned_up, u + 1)
                    tp = 2 * (s % 2)
                    eng.activation(ring_hi[:, s, :], ps[:, tp:tp + 2, :].rearrange("p b c -> p (b c)"),
                                   ACT.Copy).then_inc(w_hi, 1)

            def roots(n):
                for t in range(NT):
                    eng.wait_ge(var_up, n * NT + t + 1)
                    eng.activation(rstd[:, t:t + 1], mv[:, t, 1:2], ACT.Sqrt).then_inc(std_up, 1)

            def turn_hi(n, tiles, func, dst):
                for k in range(tiles):
                    eng.wait_ge(t_up, n + k + 1)
                    eng.activation(dst[0][:, k:k + 1, :], ps[:, 6 + k % 2:7 + k % 2, 0:N], func).then_inc(t_hi, 1)

            eng.wait_ge(turned_small, 1)
            eng.activation(idx[:, :, :], ps[:, 6, 0:5 * G].rearrange("p (a g) -> p a g", a=5), ACT.Copy)\
               .then_inc(small_read, 1)
            eng.wait_ge(turned_small, 2)
            eng.activation(bias[:, :], ps[:, 7, 0:NB], ACT.Copy).then_inc(small_read, 1)
            roots(0)
            hi_of_unit(0, 0)
            hi_of_unit(1, 1)
            turn_hi(0, KT, ACT.Relu, a_t)

            def weigh(n, s):
                g1 = bass.ds(n, 1)
                eng.activation(hot_wh[:, s, :], hot[:, s, 2, :], ACT.Copy, scale=as32(wt_hi[:, g1]))
                eng.activation(hot_wl[:, s, :], hot[:, s, 2, :], ACT.Copy, scale=wt_lo[:, g1]).then_inc(weighed, 1)

            def edges_out():
                eng.wait_ge(hot_used, G)
                for t in range(NT):
                    eng.activation(adj[:, t, :], ps[:, COUNTS[t], 0:N], ACT.Copy).then_inc(adj_raw, 1)
                for s in range(SLOTS):
                    eng.wait_ge(hot_ready, G + s + 1)
                    weigh(s, s)
                with eng.Fori(1, G // SLOTS) as i:
                    for s in range(SLOTS):
                        eng.wait_ge(hot_ready, i * SLOTS + (G + s + 1))
                        eng.wait_ge(hot_used, i * SLOTS + (G + s - 3))
                        weigh(i * SLOTS + s, s)
                eng.wait_ge(hot_used, 2 * G)
                eng.activation(wedge[:, 1, :], ps[:, WEIGHTS[1], 0:N], ACT.Copy).then_inc(wedge_ready, 1)

            def isd_roots():
                eng.wait_ge(isd_sq, 1)
                eng.activation(row_isd[:, :], row_isd[:, :], ACT.Sqrt).then_inc(isd_rt, 1)
                eng.activation(col_isd[:, 0:NT], col_isd[:, 0:NT], ACT.Sqrt).then_inc(isd_rt, 1)

            def softplus_steps():
                eng.wait_ge(soft_step, 1)
                eng.activation(sp[:, 1, :], sp[:, 1, :], ACT.Exp, scale=-1.0).then_inc(soft_step, 1)
                eng.wait_ge(soft_step, 2)
                eng.activation(sp[:, 2, :], sp[:, 1, :], ACT.Ln, bias=1.0).then_inc(soft_step, 1)


            def turned_out(L, u, o, s):
                eng.wait_ge(w_used, u + 1)
                src_ = ps[:, 4 + s % 2:5 + s % 2, 0:N]
                row = bass.ds(o + BIAS_COL[L], 1)
                if L < 5:
                    eng.activation(LAYER_OUT[L][0][:, bass.ds(o, 1), :], src_, ACT.Identity,
                                   bias=bias[:, row]).then_inc(acc_hi, 1)
                else:
                    eng.activation(tmp_t[:, bass.ds(o, 1), :], src_, ACT.Identity,
                                   bias=bias[:, row]).then_inc(acc_free, 1)

            def exps(h):
                for t in range(NT):
                    eng.wait_ge(nmx_ready, h + 1)
                    eng.activation(prob(h, t), prob(h, t), ACT.Exp, bias=stat(nmx, h, t),
                                   accum_out=stat(rs, h, t)).then_inc(exp_done, 1)

            def probs_hi(h, par):
                for j in range(NT):
                    eng.wait_ge(pt_up, h * NT + j + 1)
                    eng.activation(b_t[0][:, par * NT + j, :], ps[:, 3 + j, 0:N], ACT.Copy).then_inc(pt_hi, 1)

            def heads_hi(h, pair, par):
                r = slice(D * par, D * par + D)
                eng.wait_ge(pv_up, h + 1)
                eng.activation(q2[0][r, bass.ds(pair, 1), :], ps[r, 6 + par:7 + par, 0:N],
                               ACT.Copy).then_inc(o_hi, 1)

            for L in range(len(TURNED)):
                if L == 6:
                    for h in range(AHEAD):
                        exps(h)
                    probs_hi(0, 0)
                    for h in range(H):
                        if h:
                            heads_hi(h - 1, (h - 1) // 2, (h - 1) % 2)
                        if h + 1 < H:
                            probs_hi(h + 1, (h + 1) % 2)
                        if h + AHEAD < H:
                            exps(h + AHEAD)
                    heads_hi(H - 1, (H - 1) // 2, (H - 1) % 2)
                if L == 2:
                    edges_out()
                    softplus_steps()
                if L == 3:
                    isd_roots()
                if L == 5:
                    eng.wait_ge(mask_ready, NT)
                if L < 6:
                    with eng.Fori(0, KT // SLOTS) as i:
                        for s in range(SLOTS):
                            turned_out(L, i * SLOTS + (L * KT + s), i * SLOTS + s, s)
                            hi_of_unit(i * SLOTS + (L * KT + s + 2), (s + 2) % SLOTS)
                else:
                    for o in range(KT):
                        turned_out(L, L * KT + o, o, o % SLOTS)
                        hi_of_unit(L * KT + o + 2, (o + 2) % SLOTS)
                if L == 5:
                    for t in range(NT):
                        eng.wait_ge(v_up, t + 1)
                        tp = 2 * (t % 2)
                        eng.activation(v_n[0][:, t, :], ps[:, tp:tp + 2, :].rearrange("p b c -> p (b c)"),
                                       ACT.Copy).then_inc(v_hi, 1)

            def relu_tile(n, o, u, dst, rows=P):
                eng.wait_ge(w_used, u + 1)
                if n >= SLOTS:
                    eng.wait_ge(m_lo, n - SLOTS + 1)
                b = ROWS["mid"] + o if n < MT else ROWS["s0"] + o
                t = tmp_t[0:rows, n % SLOTS, :]
                eng.activation(t, ps[0:rows, 4 + n % 2, 0:N], ACT.Relu, bias=bias[0:rows, b:b + 1]).then_inc(m_r, 1)
                eng.wait_ge(m_r, n + 1)
                eng.activation(dst[0][0:rows, o, :], t, ACT.Copy).then_inc(m_hi, 1)

            def aggregated_hi(n, dst):
                for k in range(KT):
                    eng.wait_ge(g_m, n + k + 1)
                    eng.activation(dst[0][:, k, :], tmp_t[:, k, :], ACT.Copy).then_inc(g_hi, 1)

            roots(1)
            for t in range(NT):
                eng.wait_ge(r_up, t + 1)
                eng.activation(b_n[0][:, t, :], tmp_n[:, t, :], ACT.Copy).then_inc(n_hi, 1)
            aggregated_hi(0, a_t)
            for o in range(MT):
                relu_tile(o, o, U_W1 + o, m_t, P if o < MT - 1 else LASTM)
                hi_of_unit(U_W1 + o + 2, (o + 2) % SLOTS)
            for k in range(MT):
                hi_of_unit(U_W2 + k + 2, (k + 2) % SLOTS)

            def rows_hi(n, u_last, dst, scaled):
                for half in range(HALF):
                    for t in range(NT):
                        if half * NT + t < HALF * NT - 1:
                            eng.wait_ge(z_up, n + half * NT + t + 1)
                        else:
                            eng.wait_ge(w_used, u_last + 1)
                        d = dst[0][:, t, half * BANK:(half + 1) * BANK]
                        q = ps[:, 2 * t + half, :]
                        scale = col_isd[:, t:t + 1] if scaled else 1.0
                        eng.activation(d, q, ACT.Copy, scale=scale).then_inc(z_hi, 1)

            rows_hi(0, U_S0 - 1, b_n, True)
            roots(2)
            for t in range(NT):
                eng.wait_ge(normed, 2 * NT + t + 1)
                eng.activation(c_n[0][:, t, :], tmp_n[:, t, :], ACT.Relu).then_inc(n_hi, 1)
            turn_hi(KT, KT, ACT.Relu, a_t)
            aggregated_hi(KT, b_t)
            for o in range(KT):
                hi_of_unit(U_S0 + 2 * o + 2, (2 * o + 2) % SLOTS)
                relu_tile(MT + o, o, U_S0 + 2 * o + 1, k2)
                hi_of_unit(U_S0 + 2 * o + 3, (2 * o + 3) % SLOTS)
            for k in range(NT):
                eng.activation(b_t[0][:, k, :], wedge[:, k, :], ACT.Copy).then_inc(wedge_hi, 1)
            for k in range(KT):
                hi_of_unit(U_N1 + k + 2, (k + 2) % SLOTS)
            rows_hi(HALF * NT - 1, U_S1 - 1, c_n, False)
            for k in range(KT - 2):
                hi_of_unit(U_S1 + k + 2, (k + 2) % SLOTS)
            roots(3)
            turn_hi(2 * KT, NT, ACT.Relu, a_t)

        @block.vector
        def _(eng):
            steps = [0]

            def link(ins):
                steps[0] += 1
                ins.then_inc(dve_step, 1)
                eng.wait_ge(dve_step, steps[0])

            def lo_of_unit(u, s):
                eng.wait_ge(w_hi, u + 1)
                if isinstance(u, int) and u >= U_W1:
                    d, r, h = (unit_part(u, b) for b in (ring_lo, raw, ring_hi))
                    eng.tensor_tensor(d, r, as32(h), ALU.subtract).then_inc(w_lo, 1)
                else:
                    tp = 2 * (s % 2)
                    eng.tensor_tensor(ring_lo[:, s, :], ps[:, tp:tp + 2, :].rearrange("p b c -> p (b c)"),
                                      as32(ring_hi[:, s, :]), ALU.subtract).then_inc(w_lo, 1)

            def layer_norm(n, ready, cols=F):
                for t in range(NT):
                    eng.wait_ge(*ready[t])
                    for half in range(HALF):
                        eng.bn_stats(stats[:, t, half, :], x_sb[:, t, half * BANK:(half + 1) * BANK])\
                           .then_inc(stats_up, 1)
                    eng.wait_ge(stats_up, (n * NT + t + 1) * HALF)
                    link(eng.bn_aggr(mv[:, t, :], stats[:, t, :, :].rearrange("p a b -> p (a b)")))
                    eng.tensor_scalar(mv[:, t, 1:2], mv[:, t, 1:2], EPS, None, ALU.add).then_inc(var_up, 1)
                for t in range(NT):
                    eng.wait_ge(std_up, n * NT + t + 1)
                    link(eng.reciprocal(rstd[:, t:t + 1], rstd[:, t:t + 1]))
                    eng.tensor_scalar(tmp_n[:, t, 0:cols], x_sb[:, t, 0:cols], mv[:, t, 0:1], rstd[:, t:t + 1],
                                      ALU.subtract, ALU.mult).then_inc(normed, 1)

            def turn_lo(n, tiles, dst):
                for k in range(tiles):
                    eng.wait_ge(t_hi, n + k + 1)
                    eng.scalar_tensor_tensor(dst[1][:, k, :], ps[:, 6 + k % 2, 0:N], 0.0, as32(dst[0][:, k, :]),
                                             ALU.max, ALU.subtract).then_inc(t_lo, 1)

            eng.wait_ge(ids_in, 16 * 4)
            link(eng.tensor_copy(stage[:, 0:3 * P], stage_i[:, 0:3 * P]))
            eng.scalar_tensor_tensor(stage[:, 4 * P:5 * P], stage[:, 0:P], float(N), stage[:, P:2 * P],
                                     ALU.mult, ALU.add).then_inc(ids_flat, 1)
            layer_norm(0, [(q, 16) for q in x_in])
            lo_of_unit(0, 0)
            lo_of_unit(1, 1)
            turn_lo(0, KT, a_t)

            def find_dups(u):
                for g in range(GU * u, GU * (u + 1)):
                    if g:
                        eng.wait_ge(keys_read, g)
                    else:
                        eng.wait_ge(small_read, 1)
                        eng.wait_ge(consts, CONSTS)
                    if g % GU == 0:
                        eng.wait_ge(keys_up, u + 1)
                    j = g % GU
                    eng.scalar_tensor_tensor(keyeq, ps[:, 6 + u % 2, j * P:(j + 1) * P],
                                             idx[:, 4, g:g + 1], later[:, :], ALU.is_equal, ALU.mult,
                                             accum_out=dup[:, g:g + 1]).then_inc(keys_read, 1)

            def powers():
                eng.wait_ge(keys_read, G)
                et = idx[:, 2, :]
                c0, c1 = code
                link(eng.tensor_scalar(c0, et, 0.0, float(ETYPES), ALU.is_equal, ALU.mult))
                link(eng.scalar_tensor_tensor(c0, et, -1.0, c0, ALU.add, ALU.add))
                link(eng.tensor_scalar(c1, iota[:, 0:G], float(GROUP_BITS), float(LOWEST), ALU.mult, ALU.add))
                link(eng.tensor_tensor(c0, c0, c1, ALU.add))
                link(eng.tensor_scalar(c1, dup[:, :], 0.0, float(2 ** 23), ALU.is_equal, ALU.mult))
                link(eng.tensor_tensor(pow2_i[:, :], c0, c1, ALU.mult))
                link(eng.tensor_copy(wt_hi[:, :], idx[:, 3, :]))
                link(eng.tensor_tensor(wt_lo[:, :], idx[:, 3, :], as32(wt_hi[:, :]), ALU.subtract))

            def hot_rows1(g, s):
                g1 = bass.ds(g, 1)
                eng.tensor_scalar(hot[:, s, 0, :], iota_h[:, :], idx[:, 0, g1], None, ALU.is_equal)
                eng.tensor_scalar(hot[:, s, 1, :], iota_h[:, :], idx[:, 1, g1], pow2_i[:, g1].bitcast(F32),
                                  ALU.is_equal, ALU.mult)
                eng.tensor_scalar(hot[:, s, 2, :], iota_h[:, :], idx[:, 1, g1], None,
                                  ALU.is_equal).then_inc(hot_ready, 1)

            def hot_rows2(g, s):
                g1 = bass.ds(g, 1)
                eng.tensor_scalar(hot_dst[:, s, :], iota[:, :], idx[:, 1, g1], None, ALU.is_equal)
                eng.tensor_scalar(hot[:, s, 2, :], iota_h[:, :], idx[:, 0, g1], None,
                                  ALU.is_equal).then_inc(hot_ready, 1)

            def edges_out():
                powers()
                for s in range(SLOTS):
                    hot_rows1(s, s)
                with eng.Fori(1, G // SLOTS) as i:
                    for s in range(SLOTS):
                        eng.wait_ge(hot_used, i * SLOTS + (s - 3))
                        hot_rows1(i * SLOTS + s, s)
                for s in range(SLOTS):
                    eng.wait_ge(hot_used, G + s - 3)
                    hot_rows2(s, s)
                for t in range(NT):
                    eng.tensor_scalar(mask_i[:, t, :], ps[:, BITS[t], 0:N].bitcast(I32), 23, None,
                                      ALU.logical_shift_right).then_inc(bits_read, 1)
                with eng.Fori(1, G // SLOTS) as i:
                    for s in range(SLOTS):
                        eng.wait_ge(hot_used, i * SLOTS + (G + s - 3))
                        eng.wait_ge(weighed, i * SLOTS + (s - 3))
                        hot_rows2(i * SLOTS + s, s)
                eng.wait_ge(hot_used, 2 * G)
                for t in (0, 2):
                    eng.tensor_copy(wedge[:, t, :], ps[:, WEIGHTS[t], 0:N]).then_inc(wedge_ready, 1)

            def degrees():
                eng.wait_ge(deg_up, 1)
                dcol = ps[:, 7, N:N + 2 * NT].rearrange("p (t a) -> p t a", a=2)[:, :, 0]
                drow = ps[:, 7, 0:N]
                eng.tensor_scalar(row_isd[:, :], drow, 1.0, None, ALU.add)
                eng.tensor_scalar(col_isd[:, 0:NT], dcol, 1.0, None, ALU.add).then_inc(isd_sq, 1)
                link(eng.tensor_scalar(row_inv[:, :], drow, 1.0, None, ALU.max))
                link(eng.tensor_scalar(col_inv[:, 0:NT], dcol, 1.0, None, ALU.max))
                eng.reciprocal(row_inv[:, :], row_inv[:, :])
                eng.reciprocal(col_inv[:, 0:NT], col_inv[:, 0:NT])
                eng.wait_ge(isd_rt, 2)
                eng.reciprocal(row_isd[:, :], row_isd[:, :])
                eng.reciprocal(col_isd[:, 0:NT], col_isd[:, 0:NT]).then_inc(deg_ready, 1)
                eng.wait_ge(deg_ready, 1)

            def turned_out(L, u, o, s):
                if L >= 5:
                    return
                eng.wait_ge(acc_hi, u + 1)
                hi, lo = (LAYER_OUT[L][j][:, bass.ds(o, 1), :] for j in range(2))
                src_ = ps[:, 4 + s % 2:5 + s % 2, 0:N]
                eng.scalar_tensor_tensor(lo, src_, bias[:, bass.ds(o + BIAS_COL[L], 1)], as32(hi), ALU.add,
                                         ALU.subtract).then_inc(acc_free, 1)

            def mask_scores(h):
                for t in range(NT):
                    eng.wait_ge(sc_up, h * NT + t + 1)
                    eng.tensor_tensor_reduce(prob(h, t), ps[:, t, 0:N], mask[:, t, :], SCALE, FAR, ALU.add, ALU.max,
                                             stat(mx, h, t)).then_inc(sc_read, 1)
                eng.wait_ge(sc_read, h * NT + NT)
                eng.tensor_scalar(stat(nmx, h), stat(mx, h), -1.0, None, ALU.mult).then_inc(nmx_ready, 1)

            def row_sums(h):
                eng.wait_ge(exp_done, h * NT + NT)
                eng.reciprocal(stat(rinv, h), stat(rs, h)).then_inc(rinv_ready, 1)

            def probs_lo(h, par):
                for j in range(NT):
                    eng.wait_ge(pt_hi, h * NT + j + 1)
                    eng.tensor_tensor(b_t[1][:, par * NT + j, :], ps[:, 3 + j, 0:N],
                                      as32(b_t[0][:, par * NT + j, :]), ALU.subtract).then_inc(pt_lo, 1)

            def heads_lo(h, pair, par):
                r = slice(D * par, D * par + D)
                eng.wait_ge(o_hi, h + 1)
                eng.tensor_tensor(q2[1][r, bass.ds(pair, 1), :], ps[r, 6 + par:7 + par, 0:N],
                                  as32(q2[0][r, bass.ds(pair, 1), :]), ALU.subtract).then_inc(o_lo, 1)

            for L in range(len(TURNED)):
                if L == 2:
                    edges_out()
                if L == 3:
                    degrees()
                if L == 6:
                    eng.wait_ge(mask_ready, NT)
                    mask_scores(0)
                    mask_scores(1)
                    row_sums(0)
                    mask_scores(2)
                    row_sums(1)
                    probs_lo(0, 0)
                    for h in range(H):
                        if h + 2 < H:
                            row_sums(h + 2)
                        if h + AHEAD < H:
                            mask_scores(h + AHEAD)
                        if h:
                            heads_lo(h - 1, (h - 1) // 2, (h - 1) % 2)
                        if h + 1 < H:
                            probs_lo(h + 1, (h + 1) % 2)
                    heads_lo(H - 1, (H - 1) // 2, (H - 1) % 2)
                if L < 2:
                    for o in range(KT):
                        u = L * KT + o
                        turned_out(L, u, o, o % SLOTS)
                        lo_of_unit(u + 2, (u + 2) % SLOTS)
                        find_dups(u)
                elif L < 6:
                    with eng.Fori(0, KT // SLOTS) as i:
                        for s in range(SLOTS):
                            turned_out(L, i * SLOTS + (L * KT + s), i * SLOTS + s, s)
                            lo_of_unit(i * SLOTS + (L * KT + s + 2), (s + 2) % SLOTS)
                else:
                    for o in range(KT):
                        lo_of_unit(L * KT + o + 2, (o + 2) % SLOTS)
                if L == 5:
                    for t in range(NT):
                        eng.wait_ge(v_hi, t + 1)
                        tp = 2 * (t % 2)
                        eng.tensor_tensor(v_n[1][:, t, :], ps[:, tp:tp + 2, :].rearrange("p b c -> p (b c)"),
                                          as32(v_n[0][:, t, :]), ALU.subtract).then_inc(v_lo, 1)
            for t in range(NT):
                eng.wait_ge(y_up, t + 1)
                tp = 2 * (t % 2)
                eng.tensor_tensor(x_sb[:, t, :], ps[:, tp:tp + 2, :].rearrange("p b c -> p (b c)"),
                                  x_sb[:, t, :], ALU.add).then_inc(x1_ready, 1)

            def aggregated_lo(n, row, dst):
                for k in range(KT):
                    eng.wait_ge(g_up, n + k + 1)
                    eng.tensor_tensor(tmp_t[:, k, :], ps[:, 6 + k % 2, 0:N], row[:, :], ALU.mult).then_inc(g_m, 1)
                    eng.wait_ge(g_hi, n + k + 1)
                    eng.tensor_tensor(dst[1][:, k, :], tmp_t[:, k, :], as32(dst[0][:, k, :]),
                                      ALU.subtract).then_inc(g_lo, 1)

            def relu_lo(n, o, dst, rows=P):
                eng.wait_ge(m_hi, n + 1)
                eng.tensor_tensor(dst[1][0:rows, o, :], tmp_t[0:rows, n % SLOTS, :], as32(dst[0][0:rows, o, :]),
                                  ALU.subtract).then_inc(m_lo, 1)

            layer_norm(1, [(x1_ready, t + 1) for t in range(NT)])
            for t in range(NT):
                eng.wait_ge(normed, NT + t + 1)
                eng.tensor_scalar(tmp_n[:, t, :], tmp_n[:, t, :], 0.0, col_isd[:, t:t + 1], ALU.max,
                                  ALU.mult).then_inc(r_up, 1)
            for t in range(NT):
                eng.wait_ge(n_hi, t + 1)
                eng.tensor_tensor(b_n[1][:, t, :], tmp_n[:, t, :], as32(b_n[0][:, t, :]),
                                  ALU.subtract).then_inc(n_lo, 1)
            aggregated_lo(0, row_isd, a_t)
            for o in range(MT):
                relu_lo(o, o, m_t, P if o < MT - 1 else LASTM)
                lo_of_unit(U_W1 + o + 2, (o + 2) % SLOTS)
            for k in range(MT):
                lo_of_unit(U_W2 + k + 2, (k + 2) % SLOTS)

            def rows_lo(n, dst, scaled):
                for half in range(HALF):
                    for t in range(NT):
                        n += 1
                        eng.wait_ge(z_hi, n)
                        hi, lo = (dst[j][:, t, half * BANK:(half + 1) * BANK] for j in range(2))
                        q = ps[:, 2 * t + half, :]
                        if scaled:
                            last = eng.scalar_tensor_tensor(lo, q, col_isd[:, t:t + 1], as32(hi), ALU.mult,
                                                            ALU.subtract)
                        else:
                            last = eng.tensor_tensor(lo, q, as32(hi), ALU.subtract)
                        last.then_inc(z_lo, 1)

            def add_aggregated(n, col, ready):
                for half in range(HALF):
                    for t in range(NT):
                        eng.wait_ge(h_up, n + half * NT + t + 1)
                        xs = x_sb[:, t, half * BANK:(half + 1) * BANK]
                        eng.scalar_tensor_tensor(xs, ps[:, 6 + (half * NT + t) % 2, :], col[:, t:t + 1], xs,
                                                 ALU.mult, ALU.add).then_inc(ready, 1)

            rows_lo(0, b_n, True)
            eng.wait_ge(xb_ready, NT)
            add_aggregated(0, col_isd, x2_ready)
            layer_norm(2, [(x2_ready, NT + t + 1) for t in range(NT)])
            for t in range(NT):
                eng.wait_ge(n_hi, NT + t + 1)
                eng.scalar_tensor_tensor(c_n[1][:, t, :], tmp_n[:, t, :], 0.0, as32(c_n[0][:, t, :]), ALU.max,
                                         ALU.subtract).then_inc(n_lo, 1)
            turn_lo(KT, KT, a_t)
            aggregated_lo(KT, row_inv, b_t)
            for o in range(KT):
                lo_of_unit(U_S0 + 2 * o + 2, (2 * o + 2) % SLOTS)
                relu_lo(MT + o, o, k2)
                lo_of_unit(U_S0 + 2 * o + 3, (2 * o + 3) % SLOTS)
            eng.wait_ge(wedge_hi, NT)
            for k in range(NT):
                eng.tensor_tensor(b_t[1][:, k, :], wedge[:, k, :], as32(b_t[0][:, k, :]),
                                  ALU.subtract).then_inc(wedge_lo, 1)
            for k in range(KT):
                lo_of_unit(U_N1 + k + 2, (k + 2) % SLOTS)
            rows_lo(HALF * NT, c_n, False)
            for k in range(KT - 2):
                lo_of_unit(U_S1 + k + 2, (k + 2) % SLOTS)
            eng.wait_ge(xb_ready, 2 * NT)
            for half in range(HALF):
                for t in range(NT):
                    if half * NT + t < HALF * NT - 1:
                        eng.wait_ge(s_up, half * NT + t + 1)
                    else:
                        eng.wait_ge(w_used, U_END)
                    xs = x_sb[:, t, half * BANK:(half + 1) * BANK]
                    eng.tensor_tensor(xs, ps[:, 2 * t + half, :], xs, ALU.add).then_inc(s_added, 1)
            eng.wait_ge(s_added, HALF * NT)
            add_aggregated(HALF * NT, col_inv, x3_ready)
            layer_norm(3, [(x3_ready, NT + t + 1) for t in range(NT)], N)
            turn_lo(2 * KT, NT, a_t)
            eng.wait_ge(xb_ready, 3 * NT)
            for t in range(NT):
                eng.wait_ge(f_up, t + 1)
                eng.tensor_tensor(x_sb[:, t, 0:N], ps[:, t, 0:N], x_sb[:, t, 0:N], ALU.add).then_inc(x4_ready, 1)

        @block.tensor
        def _(eng):
            def mm3(out_, l, r, first, last):
                eng.matmul(out_, l[0], r[0], start=first, stop=False)
                eng.matmul(out_, l[1], r[0], start=False, stop=False)
                return eng.matmul(out_, l[0], r[1], start=False, stop=last)

            def turn_unit(landed_value, s):
                eng.wait_ge(landed[s], landed_value)
                for k in range(KT):
                    tr = eng.transpose(ps[:, 2 * (s % 2) + k // 4, (k % 4) * P:(k % 4 + 1) * P],
                                       raw[:, s, k * P:(k + 1) * P], ident[:, :])
                tr.then_inc(turned_up, 1)

            eng.wait_ge(consts, 3)
            eng.wait_ge(ids_flat, 1)
            for j in range(5):
                tr = eng.transpose(ps[:, 6, j * G:(j + 1) * G], stage[:, j * P:(j + 1) * P], ident[0:G, 0:G])
            tr.then_inc(turned_small, 1)
            eng.wait_ge(bias_in, 16 * 10)
            eng.transpose(ps[:, 7, 0:NB], bias_rows[:, :], ident[0:NB, 0:NB]).then_inc(turned_small, 1)
            turn_unit(16, 0)
            turn_unit(16, 1)

            def turn(n, tiles, ready):
                for k in range(tiles):
                    if k >= 2:
                        eng.wait_ge(t_lo, n + k - 1)
                    for t in range(NT):
                        if k == 0:
                            eng.wait_ge(normed, ready + t + 1)
                        tr = eng.transpose(ps[:, 6 + k % 2, t * P:(t + 1) * P], tmp_n[:, t, k * P:(k + 1) * P],
                                           ident[:, :])
                    tr.then_inc(t_up, 1)

            eng.wait_ge(small_read, 2)
            turn(0, KT, 0)

            def keys(u):
                if u >= 2:
                    eng.wait_ge(keys_read, GU * (u - 1))
                for j in range(GU):
                    g = GU * u + j
                    tr = eng.transpose(ps[:, 6 + u % 2, j * P:(j + 1) * P],
                                       idx[:, 4, g:g + 1].to_broadcast([P, P]), ident[:, :])
                tr.then_inc(keys_up, 1)

            def edge_pass1(g, s, first, last):
                eng.wait_ge(hot_ready, g + 1)
                for m in range(NT):
                    l = hot[:, s, 0, m * P:(m + 1) * P]
                    eng.matmul(ps[:, BITS[m], 0:N], l, hot[:, s, 1, :], start=first, stop=last)
                    mm = eng.matmul(ps[:, COUNTS[m], 0:N], l, hot[:, s, 2, :], start=first, stop=last)
                mm.then_inc(hot_used, 1)

            def edge_pass2(g, s, first, last):
                eng.wait_ge(weighed, g - G + 1)
                for m in range(NT):
                    if first and m == 2:
                        eng.wait_ge(bits_read, 1)
                    l = hot_dst[:, s, m * P:(m + 1) * P]
                    eng.matmul(ps[:, WEIGHTS[m], 0:N], l, hot_wh[:, s, :], start=first, stop=False)
                    mm = eng.matmul(ps[:, WEIGHTS[m], 0:N], l, hot_wl[:, s, :], start=False, stop=last)
                mm.then_inc(hot_used, 1)

            def edges_in():
                eng.wait_ge(w_lo, 2 * KT + 2)
                for base, edge_pass in ((0, edge_pass1), (G, edge_pass2)):
                    if base:
                        eng.wait_ge(acc_free, 2 * KT)
                    for s in range(SLOTS):
                        edge_pass(base + s, s, s == 0, False)
                    with eng.Fori(1, G // SLOTS - 1) as i:
                        for s in range(SLOTS):
                            edge_pass(i * SLOTS + (base + s), s, False, False)
                    for s in range(SLOTS):
                        edge_pass(base + G - SLOTS + s, s, False, s == SLOTS - 1)
                eng.wait_ge(adj_raw, NT)
                eng.wait_ge(bits_read, NT)
                for s in range(NT):
                    eng.matmul(ps[:, 7, 0:N], ones[:, :], adj[:, s, :], start=s == 0, stop=s == NT - 1)
                for t in range(NT):
                    for s in range(NT):
                        mm = eng.matmul(ps[:, 7, N + 2 * t:N + 2 * t + 2], adj[:, s, t * P:(t + 1) * P], ones[:, 0:2],
                                        start=s == 0, stop=s == NT - 1)
                mm.then_inc(deg_up, 1)
                eng.wait_ge(wedge_ready, NT)

            def ring(s, k, m=P):
                return [b[:, s, k * P:k * P + m] for b in (ring_hi, ring_lo)]

            def turned_unit(L, u, s, landed_value, bank_free=True, x_split=False):
                eng.wait_ge(w_lo, u + 1)
                if bank_free:
                    eng.wait_ge(acc_free, u - 1)
                if L in (1, 3, 5):
                    eng.wait_ge(acc_free, L * KT - 1)
                if landed_value is not None:
                    turn_unit(landed_value, (s + 2) % SLOTS)
                for k in range(KT):
                    if k == KT - 1 and L in (1, 3, 5):
                        eng.wait_ge(acc_free, L * KT)
                    if x_split:
                        eng.wait_ge(t_lo, k + 1)
                    mm = mm3(ps[:, 4 + s % 2, 0:N], ring(s, k), [b[:, k, :] for b in LAYER_IN[L]], k == 0, k == KT - 1)
                mm.then_inc(w_used, 1)

            def scores(h):
                r = slice(D * (h % 2), D * (h % 2) + D)
                for t in range(NT):
                    if h >= 1:
                        eng.wait_ge(sc_read, (h - 1) * NT + t + 1)
                    mm3(ps[:, t, 0:N], [q[r, h // 2, t * P:(t + 1) * P] for q in q2], [k[r, h // 2, :] for k in k2],
                        True, True).then_inc(sc_up, 1)

            def turn_probs(h):
                for j in range(NT):
                    if h >= 1:
                        eng.wait_ge(pt_lo, (h - 1) * NT + j + 1)
                    for t in range(NT):
                        if j == 0:
                            eng.wait_ge(p_ready, h * NT + t + 1)
                        tr = eng.transpose(ps[:, 3 + j, t * P:(t + 1) * P], prob(h, t, slice(j * P, (j + 1) * P)),
                                           ident[:, :])
                    tr.then_inc(pt_up, 1)

            def attend(h, par):
                if h >= 2:
                    eng.wait_ge(o_lo, h - 1)
                for j in range(NT):
                    eng.wait_ge(pt_lo, h * NT + j + 1)
                    mm = mm3(ps[:, 6 + par, 0:N], [v[:, j, (h // 2) * P:(h // 2 + 1) * P] for v in v_n],
                             [q[:, par * NT + j, :] for q in b_t], j == 0, j == NT - 1)
                mm.then_inc(pv_up, 1)

            for L in range(len(TURNED)):
                if L == 2:
                    edges_in()
                if L < 2:
                    for o in range(KT):
                        u = L * KT + o
                        turned_unit(L, u, u % SLOTS, 16 * ((u + 2) // SLOTS + 1), u >= 2, u == 0)
                        keys(u)
                elif L < 6:
                    with eng.Fori(0, KT // SLOTS) as i:
                        for s in range(SLOTS):
                            v = L * KT + s + 2
                            turned_unit(L, i * SLOTS + (L * KT + s), s, i * 16 + 16 * (v // SLOTS + 1))
                if L == 5:
                    eng.wait_ge(acc_free, 6 * KT)
                    eng.wait_ge(w_lo, 6 * KT + 2)
                    for t in range(NT):
                        if t == 2:
                            eng.wait_ge(v_lo, 1)
                        for o in range(KT):
                            tr = eng.transpose(ps[:, 2 * (t % 2) + o // 4, (o % 4) * P:(o % 4 + 1) * P],
                                               tmp_t[:, o, t * P:(t + 1) * P], ident[:, :])
                        tr.then_inc(v_up, 1)
                    eng.wait_ge(v_lo, NT)
                    for h in range(AHEAD):
                        scores(h)
                    turn_probs(0)
                    for h in range(H):
                        if h + AHEAD < H:
                            scores(h + AHEAD)
                        if h + 1 < H:
                            turn_probs(h + 1)
                        attend(h, h % 2)
                    eng.wait_ge(o_lo, H)
                if L == 6:
                    for o in range(KT):
                        u = L * KT + o
                        more = 16 * ((u + 2) // SLOTS + 1) if o + 2 < KT else None
                        turned_unit(6, u, o % SLOTS, more)
            eng.wait_ge(acc_free, 7 * KT)
            for t in range(NT):
                if t == 2:
                    eng.wait_ge(x1_ready, 1)
                for o in range(KT):
                    tr = eng.transpose(ps[:, 2 * (t % 2) + o // 4, (o % 4) * P:(o % 4 + 1) * P],
                                       tmp_t[:, o, t * P:(t + 1) * P], ident[:, :])
                tr.then_inc(y_up, 1)

            def aggregate(n, act):
                for k in range(KT):
                    if k >= 2:
                        eng.wait_ge(g_m, n + k - 1)
                    for s in range(NT):
                        for j in range(2):
                            mm = eng.matmul(ps[:, 6 + k % 2, 0:N], act[j][:, s, k * P:(k + 1) * P], adj[:, s, :],
                                            start=s == 0 and j == 0, stop=s == NT - 1 and j == 1)
                    mm.then_inc(g_up, 1)

            def relu_unit(n, u, act, first, last, m=P, counts=None):
                s = u % SLOTS
                eng.wait_ge(w_lo, u + 1)
                if first and n >= 2:
                    eng.wait_ge(m_r, n - 1)
                for k in range(KT):
                    if counts is not None:
                        eng.wait_ge(counts[0], counts[1] + k + 1)
                    mm = mm3(ps[0:m, 4 + n % 2, 0:N], ring(s, k, m), [b[:, k, :] for b in act],
                             first and k == 0, last and k == KT - 1)
                mm.then_inc(w_used, 1)

            def rows_layer(act, u0, tiles, lastrows, ready, up, bank_free):
                for k in range(tiles):
                    u = u0 + k
                    r = P if k < tiles - 1 else lastrows
                    eng.wait_ge(w_lo, u + 1)
                    eng.wait_ge(m_lo, ready + k + 1)
                    for half in range(HALF):
                        for t in range(NT):
                            if k == 0:
                                bank_free(half * NT + t)
                            mm = mm3(ps[:, 2 * t + half, :], [a[0:r, k, t * P:(t + 1) * P] for a in act],
                                     [b[0:r, u % SLOTS, half * BANK:(half + 1) * BANK] for b in (ring_hi, ring_lo)],
                                     k == 0, k == tiles - 1)
                            if half * NT + t == HALF * NT - 1:
                                mm.then_inc(w_used, 1)
                            elif k == tiles - 1:
                                mm.then_inc(up, 1)

            def aggregate_rows(n, zs, act):
                for half in range(HALF):
                    eng.wait_ge(z_lo, zs + (half + 1) * NT)
                    for t in range(NT):
                        b = half * NT + t
                        if n + b >= 2 and b >= 2:
                            eng.wait_ge(x2_ready if n == 0 else x3_ready, b - 1)
                        for s in range(NT):
                            for j in range(2):
                                mm = eng.matmul(ps[:, 6 + b % 2, :], adj[:, s, t * P:(t + 1) * P],
                                                act[j][:, s, half * BANK:(half + 1) * BANK],
                                                start=s == 0 and j == 0, stop=s == NT - 1 and j == 1)
                        mm.then_inc(h_up, 1)

            eng.wait_ge(adj_ready, NT)
            eng.wait_ge(n_lo, NT)
            aggregate(0, b_n)
            for o in range(MT):
                relu_unit(o, U_W1 + o, a_t, True, True, P if o < MT - 1 else LASTM,
                          (g_lo, 0) if o == 0 else None)
            rows_layer(m_t, U_W2, MT, LASTM, 0, z_up, lambda b: eng.wait_ge(m_r, MT) if b == 0 else None)
            aggregate_rows(0, 0, b_n)
            turn(KT, KT, 2 * NT)
            eng.wait_ge(adj_ready, 2 * NT)
            eng.wait_ge(n_lo, 2 * NT)
            eng.wait_ge(t_lo, 2 * KT)
            aggregate(KT, c_n)
            for o in range(KT):
                relu_unit(MT + o, U_S0 + 2 * o, a_t, True, False)
                relu_unit(MT + o, U_S0 + 2 * o + 1, b_t, False, True, P, (g_lo, KT) if o == 0 else None)
            rows_layer(k2, U_N1, KT, P, MT, z_up, lambda b: eng.wait_ge(m_r, MT + KT) if b == 0 else None)
            rows_layer(k2, U_S1, KT, P, MT, s_up, lambda b: eng.wait_ge(z_lo, HALF * NT + b + 1))
            aggregate_rows(HALF * NT, HALF * NT, c_n)
            turn(2 * KT, NT, 3 * NT)
            eng.wait_ge(t_lo, 2 * KT + NT)
            eng.wait_ge(wedge_lo, NT)
            for t in range(NT):
                for k in range(NT):
                    mm = mm3(ps[:, t, 0:N], [a[:, k, t * P:(t + 1) * P] for a in a_t], [b[:, k, :] for b in b_t],
                             k == 0, k == NT - 1)
                mm.then_inc(f_up, 1)


_INS = ['x', 'src', 'dst', 'edge_type_5', 'edge_weight', 'L0_gnn_edge_type_weights', 'L0_gnn_wq', 'L0_gnn_bq',
        'L0_gnn_wk', 'L0_gnn_bk', 'L0_gnn_wv', 'L0_gnn_bv', 'L0_gnn_wiq', 'L0_gnn_biq', 'L0_gnn_wik', 'L0_gnn_bik',
        'L0_gnn_wiv', 'L0_gnn_biv', 'L0_gnn_wo', 'L0_gnn_bo', 'L1_gnn_W1', 'L1_gnn_b1', 'L1_gnn_W2', 'L1_gnn_b2',
        'L2_gnn_W_self0', 'L2_gnn_W_neigh0', 'L2_gnn_b0', 'L2_gnn_W_self1', 'L2_gnn_W_neigh1', 'L2_gnn_b1',
        'L3_gnn_bias']


def kernel(**inputs):
    import numpy as _np
    import concourse.bacc as _bacc
    from concourse import mybir as _mybir
    from concourse.bass_utils import run_bass_kernel_spmd as _run

    nc = _bacc.Bacc("TRN2", target_bir_lowering=False, num_devices=1)
    arrays, args = {}, []
    for name in _INS:
        a = _np.ascontiguousarray(inputs[name])
        arrays[f"in_{name}_dram"] = a
        args.append(nc.dram_tensor(f"in_{name}_dram", a.shape, _mybir.dt.from_np(a.dtype), kind="ExternalInput").ap())
    shape = arrays["in_x_dram"].shape
    args.append(nc.dram_tensor("out_0_dram", shape, _mybir.dt.float32, kind="ExternalOutput").ap())
    gnn_stack(nc, *args)
    r = _run(nc, [arrays], core_ids=[0])
    return r.results[0]["out_0_dram"]
```

```python
from contextlib import ExitStack

import concourse.bass as bass
from concourse import mybir

ALU = mybir.AluOpType
ACT = mybir.ActivationFunctionType
F32 = mybir.dt.float32
F32R = mybir.dt.float32r
I32 = mybir.dt.int32
BF16 = mybir.dt.bfloat16
F16 = mybir.dt.float16

P = 128
BANK = 512
EPS = 1e-5
FAR = -3.0e37
ROUND = 12582912.0
ETYPES = 4

GROUP_BITS = 5
LOWEST = 6


def gnn_stack(nc, x, src, dst, etype, eweight, etw, wq, bq, wk, bk, wv, bv, wiq, biq, wik, bik, wiv, biv,
              wo, bo, w1, b1, w2, b2, wself0, wneigh0, sb0, wself1, wneigh1, sb1, b3, out):
    N, F = x.shape
    NT, KT = N // P, F // P
    E = src.shape[0]
    G = E // P
    MID = w1.shape[1]
    MT = -(-MID // P)
    LASTM = MID - (MT - 1) * P
    H = 16
    D = F // H
    SCALE = float(D) ** -0.5
    HALF = F // BANK
    SLOTS = 4
    AHEAD = 3
    assert G * GROUP_BITS + LOWEST < 254 and E % P == 0 and N == NT * P and D == 64 and KT == 8

    with ExitStack() as ctx:
        def sb(name, shape, dt=F32):
            return ctx.enter_context(nc.sbuf_tensor(name, shape, dt))

        def sem(name):
            return ctx.enter_context(nc.semaphore(name))

        x_sb = sb("x_sb", [P, NT, F])
        tmp = sb("tmp", [P, NT * F])
        a_hi, a_lo = (sb(f"a_{n}", [P, NT * F], F32R) for n in ("hi", "lo"))
        b_hi, b_lo = (sb(f"b_{n}", [P, NT * F], F32R) for n in ("hi", "lo"))
        c_act = sb("c_act", [P, 2 * NT * F], F32R)
        d_act = sb("d_act", [P, 2 * NT * F], F32R)
        raw = sb("raw", [P, SLOTS, F])
        ring_hi, ring_lo = (sb(f"ring_{n}", [P, SLOTS, F], F32R) for n in ("hi", "lo"))
        adj = sb("adj", [P, NT, N], F32R)
        mask = sb("mask", [P, NT, N])
        wedge = sb("wedge", [P, NT, N])
        row_isd = sb("row_isd", [P, N])
        row_inv = sb("row_inv", [P, N])
        col_isd = sb("col_isd", [P, 4])
        col_inv = sb("col_inv", [P, 4])
        iota_i = sb("iota_i", [P, N], I32)
        iota = sb("iota", [P, N])
        iota_h = sb("iota_h", [P, N], F16)
        spare = sb("spare", [P, 2 * N], F32R)
        hot = sb("hot", [P, SLOTS, 3, N], BF16)
        ident = sb("ident", [P, P])
        later = sb("later", [P, P])
        ones = sb("ones", [P, P], F32R)
        ROWS = dict(q=0, iq=8, k=16, ik=24, v=32, iv=40, mid=48, s0=48 + MT)
        NB = ROWS["s0"] + KT
        bias_rows = sb("bias_rows", [NB, P])
        bias = sb("bias", [P, NB])
        idx = sb("idx", [P, 5, G])
        dup = sb("dup", [P, G])
        pow2_i = sb("pow2_i", [P, G], I32)
        wt_hi = sb("wt_hi", [P, G], F32R)
        wt_lo = sb("wt_lo", [P, G])
        sp = sb("sp", [P, 4, ETYPES])
        stats = sb("stats", [P, NT, KT // 2, 6])
        mv = sb("mv", [P, NT, 2])
        rstd = sb("rstd", [P, NT])
        nshift = sb("nshift", [P, NT])
        mx = sb("mx", [P, AHEAD * NT])
        nmx = sb("nmx", [P, AHEAD * NT])
        rs = sb("rs", [P, AHEAD * NT])
        rinv = sb("rinv", [P, AHEAD * NT])
        ones32 = sb("ones32", [P, P])
        part = sb("part", [P, 1])
        ps = ctx.enter_context(nc.psum_tensor("ps", [P, 8, BANK], F32))

        tmp_n = tmp[:, :].rearrange("p (t f) -> p t f", t=NT)
        tmp_t = tmp[:, :].rearrange("p (k n) -> p k n", n=N)
        a_t = [t[:, :].rearrange("p (k n) -> p k n", n=N) for t in (a_hi, a_lo)]
        v_n = [t[:, :].rearrange("p (t f) -> p t f", t=NT) for t in (a_hi, a_lo)]
        b_t = [t[:, :].rearrange("p (k n) -> p k n", n=N) for t in (b_hi, b_lo)]
        b_n = [t[:, :].rearrange("p (t f) -> p t f", t=NT) for t in (b_hi, b_lo)]
        c_n = [c_act[:, j * NT * F:(j + 1) * NT * F].rearrange("p (t f) -> p t f", t=NT) for j in range(2)]
        q2 = [c_act[:, j * NT * F:(j + 1) * NT * F].rearrange("p (k n) -> p k n", n=N) for j in range(2)]
        k2 = [d_act[:, j * NT * F:(j + 1) * NT * F].rearrange("p (k n) -> p k n", n=N) for j in range(2)]
        m_t = [t[:, 0:MT * N].rearrange("p (k n) -> p k n", n=N) for t in (c_act, d_act)]
        stage_i = mask[0:G, :, :].rearrange("p t n -> p (t n)").bitcast(I32)
        stage = wedge[0:G, :, :].rearrange("p t n -> p (t n)")
        prob_tiles = [tmp[:, j * NT * N:(j + 1) * NT * N] for j in range(2)] + [
            hot[:, :, :, :].rearrange("p s j n -> p (s j n)")[:, 0:2 * NT * N].bitcast(F32)]
        FILL_TILES = [[b[:, j * N:(j + 1) * N] for b in bufs for j in range(n)] + [spare[:, 0:N], spare[:, N:2 * N]]
                      for bufs, n in (((d_act,), 2 * KT), ((a_hi, a_lo), KT))]
        mask_i = mask[:, :, :].bitcast(I32)
        keyeq = wedge[:, 2, 0:P]
        code = [wedge[:, 2, P + j * G:P + (j + 1) * G] for j in range(2)]
        hot_dst, hot_wh, hot_wl = k2[0][:, 0:SLOTS, :], k2[0][:, SLOTS:2 * SLOTS, :], k2[1][:, 0:SLOTS, :]
        brow = mask[:, :, :].rearrange("p t n -> p (t n)")[:, 0:F]

        def unit_part(u, buf):
            if u == U_W2 - 1:
                return buf[:, u % SLOTS, :].rearrange("p (k c) -> p k c", c=P)[:, :, 0:LASTM]
            return buf[0:LASTM if u == U_S0 - 1 else P, u % SLOTS, :]

        def prob(h, t, c=slice(0, N)):
            return prob_tiles[h % AHEAD][:, t * N + c.start:t * N + c.stop]

        def stat(buf, h, t=None):
            c = h % AHEAD * NT
            return buf[:, c:c + NT] if t is None else buf[:, c + t:c + t + 1]

        def wait_normed(eng, n, t):
            if t < NORM_ACT[n]:
                eng.wait_ge(normed_act, sum(NORM_ACT[:n]) + t + 1)
            else:
                eng.wait_ge(normed_dve, n * NT - sum(NORM_ACT[:n + 1]) + t + 1)

        def pair_out(i, t):
            return ps[:, 4 + (i * NT + t) % 4, 0:PAIR]

        def last_turn(t):
            return ps[:, NT + t, 0:N].rearrange("p (k n) -> p k n", n=P)

        def as32(ap):
            return ap.bitcast(F32)

        LAYER_IN = [a_t, b_t, a_t, b_t, a_t, b_t, q2]
        LAYER_OUT = [b_t, q2, b_t, k2, b_t]
        BIAS_COL = [ROWS[r] for r in ("q", "iq", "k", "ik", "v")]
        CONSTS = 10
        PARTS = [(t, slice(c, c + BANK)) for c in range(0, F, BANK) for t in range(NT)]
        PAIR = 2 * P
        PAIRS = KT // 2
        TURN_BANKS = ((6, 7, 5), (5, 3, 7))
        NORM_ACT = (2, 1, 2, NT)
        FILL = 6
        G2 = G - 2 * FILL
        assert G % SLOTS == 0 and G2 % SLOTS == 0
        GU = BANK // P
        U_DUPS = G // GU
        BITS, COUNTS, WEIGHTS = (6, 7, 0), (1, 2, 3), (4, 5, 6)
        assert U_DUPS * GU == G and U_DUPS + 2 <= 2 * KT
        TURNED = [wq, wiq, wk, wik, wv, wiv, wo]
        U_W1 = len(TURNED) * KT
        U_W2 = U_W1 + MT
        U_S0 = U_W2 + MT
        U_N1 = U_S0 + 2 * KT
        U_S1 = U_N1 + KT
        U_END = U_S1 + KT
        assert all(u % SLOTS == 0 for u in (U_W1, U_W2, U_S0, U_N1, U_S1, U_END))

        x_in = [sem(f"x_in{t}") for t in range(NT)]
        ids_in = sem("ids_in")
        bias_in = sem("bias_in")
        etw_in = sem("etw_in")
        brow_in = sem("brow_in")
        out_done = sem("out_done")
        landed = [sem(f"landed{s}") for s in range(SLOTS)]
        consts = sem("consts")
        turned_up = sem("turned_up")
        w_hi = sem("w_hi")
        w_lo = sem("w_lo")
        w_used = sem("w_used")
        dve_step = sem("dve_step")
        pool_step = sem("pool_step")
        soft_step = sem("soft_step")
        ids_flat = sem("ids_flat")
        turned_small = sem("turned_small")
        small_read = sem("small_read")
        keys_up = sem("keys_up")
        keys_read = sem("keys_read")
        hot_ready = sem("hot_ready")
        weighed = sem("weighed")
        hot_used = sem("hot_used")
        bits_read = sem("bits_read")
        adj_raw = sem("adj_raw")
        adj_ready = sem("adj_ready")
        deg_up = sem("deg_up")
        isd_sq = sem("isd_sq")
        deg_ready = sem("deg_ready")
        mask_ready = sem("mask_ready")
        wedge_ready = sem("wedge_ready")
        fill_ready = sem("fill_ready")
        fill_up = sem("fill_up")
        wedge_added = sem("wedge_added")
        wedge_hi = sem("wedge_hi")
        wedge_lo = sem("wedge_lo")
        stats_up = sem("stats_up")
        var_up = sem("var_up")
        std_up = sem("std_up")
        coef_up = sem("coef_up")
        normed_act = sem("normed_act")
        normed_dve = sem("normed_dve")
        t_up = sem("t_up")
        t_hi = sem("t_hi")
        t_lo = sem("t_lo")
        acc_hi = sem("acc_hi")
        acc_free = sem("acc_free")
        v_up = sem("v_up")
        v_hi = sem("v_hi")
        v_lo = sem("v_lo")
        sc_up = sem("sc_up")
        sc_read = sem("sc_read")
        nmx_ready = sem("nmx_ready")
        exp_done = sem("exp_done")
        rinv_ready = sem("rinv_ready")
        p_ready = sem("p_ready")
        pt_up = sem("pt_up")
        pt_hi = sem("pt_hi")
        pt_lo = sem("pt_lo")
        pv_up = sem("pv_up")
        o_hi = sem("o_hi")
        o_lo = sem("o_lo")
        y_up = sem("y_up")
        x1_ready = sem("x1_ready")
        x2_ready = sem("x2_ready")
        x3_ready = sem("x3_ready")
        x4_ready = sem("x4_ready")
        xb_ready = sem("xb_ready")
        n_hi = sem("n_hi")
        n_lo = sem("n_lo")
        g_up = sem("g_up")
        g_m = sem("g_m")
        g_hi = sem("g_hi")
        g_lo = sem("g_lo")
        m_r = sem("m_r")
        m_hi = sem("m_hi")
        m_lo = sem("m_lo")
        z_up = sem("z_up")
        z_hi = sem("z_hi")
        z_lo = sem("z_lo")
        s_up = sem("s_up")
        s_added = sem("s_added")
        h_up = sem("h_up")
        f_up = sem("f_up")

        block = ctx.enter_context(nc.Block())

        @block.sync
        def _(sp_):
            eng = sp_
            for t in range(NT):
                eng.dma_start(x_sb[:, t, :], x[t * P:(t + 1) * P, :]).then_inc(x_in[t], 16)
            for s in range(2):
                eng.dma_start(raw[:, s, :], TURNED[0][s * P:(s + 1) * P, :]).then_inc(landed[s], 16)
            for j, v in enumerate((src, dst, etype)):
                eng.dma_start(stage_i[:, j * P:(j + 1) * P], v.rearrange("(g p) -> g p", p=P)).then_inc(ids_in, 16)
            eng.dma_start(stage[:, 3 * P:4 * P], eweight.rearrange("(g p) -> g p", p=P)).then_inc(ids_in, 16)
            eng.wait_ge(consts, 1)
            for name, v in (("q", bq), ("iq", biq), ("k", bk), ("ik", bik), ("v", bv), ("iv", biv), ("s0", sb0)):
                eng.dma_start(bias_rows[ROWS[name]:ROWS[name] + KT, :], v.rearrange("(k p) -> k p", p=P)).then_inc(bias_in, 16)
            full = (MT - 1) * P
            eng.dma_start(bias_rows[ROWS["mid"]:ROWS["mid"] + MT - 1, :],
                          b1[0:full].rearrange("(k p) -> k p", p=P)).then_inc(bias_in, 16)
            r = ROWS["mid"] + MT - 1
            eng.dma_start(bias_rows[r:r + 1, 0:LASTM], b1[full:MID].rearrange("(a n) -> a n", a=1)).then_inc(bias_in, 16)
            for s in range(2, SLOTS):
                eng.dma_start(raw[:, s, :], TURNED[0][s * P:(s + 1) * P, :]).then_inc(landed[s], 16)
            eng.dma_start(sp[:, 0, :], etw.partition_broadcast(P)).then_inc(etw_in, 16)
            eng.wait_ge(ids_flat, 1)
            eng.dma_start(brow, bo.partition_broadcast(P)).then_inc(brow_in, 16)

            def free_raw(u):
                if isinstance(u, int) and u >= U_W1 + SLOTS:
                    eng.wait_ge(w_hi, u - 3)
                    eng.wait_ge(w_lo, u - 3)
                else:
                    eng.wait_ge(turned_up, u - 3)

            for s in range(SLOTS):
                free_raw(SLOTS + s)
                eng.dma_start(raw[:, s, :], TURNED[0][(SLOTS + s) * P:(SLOTS + s + 1) * P, :]).then_inc(landed[s], 16)
            for L in range(1, len(TURNED)):
                with eng.Fori(0, KT // SLOTS) as i:
                    for s in range(SLOTS):
                        eng.wait_ge(turned_up, i * SLOTS + (L * KT + s - 3))
                        eng.dma_start(raw[:, s, :], TURNED[L][bass.ds(i * (SLOTS * P) + s * P, P), :]).then_inc(landed[s], 16)

            def load_cols(w, o, u):
                s = u % SLOTS
                width = min(P, w.shape[1] - o * P)
                free_raw(u)
                eng.dma_start(raw[:, s, :].rearrange("p (k c) -> p k c", c=P)[:, :, 0:width],
                              w[:, o * P:o * P + width].rearrange("(k p) c -> p k c", p=P)).then_inc(landed[s], 16)

            def load_rows(w, k, u):
                s = u % SLOTS
                rows = min(P, w.shape[0] - k * P)
                free_raw(u)
                eng.dma_start(raw[0:rows, s, :], w[k * P:k * P + rows, :]).then_inc(landed[s], 16)

            for o in range(MT):
                load_cols(w1, o, U_W1 + o)
            for k in range(MT):
                load_rows(w2, k, U_W2 + k)
                if k == 0:
                    eng.wait_ge(sc_read, NT * H)
                    eng.dma_start(brow, b2.partition_broadcast(P)).then_inc(brow_in, 16)
            for o in range(KT):
                load_cols(wself0, o, U_S0 + 2 * o)
                load_cols(wneigh0, o, U_S0 + 2 * o + 1)
            for k in range(KT):
                load_rows(wneigh1, k, U_N1 + k)
            eng.wait_ge(xb_ready, 2 * NT)
            eng.dma_start(brow, sb1.partition_broadcast(P)).then_inc(brow_in, 16)
            for k in range(KT):
                load_rows(wself1, k, U_S1 + k)
            eng.wait_ge(xb_ready, 3 * NT)
            eng.dma_start(brow, b3.partition_broadcast(P)).then_inc(brow_in, 16)
            for t in range(NT):
                eng.wait_ge(xb_ready, 3 * NT + 2 * t + 2)
                eng.dma_start(out[t * P:(t + 1) * P, N:F], x_sb[:, t, N:F]).then_inc(out_done, 16)
            for t in range(NT):
                eng.wait_ge(x4_ready, t + 1)
                eng.dma_start(out[t * P:(t + 1) * P, 0:N], x_sb[:, t, 0:N]).then_inc(out_done, 16)
            eng.wait_ge(out_done, 2 * 16 * NT)

        @block.gpsimd
        def _(eng):
            eng.memset(bias_rows[:, :], 0.0).then_inc(consts, 1)
            eng.iota(iota_i[:, 0:P], pattern=[[1, P]], base=0, channel_multiplier=-1).then_inc(consts, 1)
            eng.wait_ge(consts, 2)
            eng.tensor_scalar(ident[:, :], iota_i[:, 0:P], 0.0, None, ALU.is_equal).then_inc(consts, 1)
            eng.tensor_scalar(later[:, :], iota_i[:, 0:P], 0.0, None, ALU.is_gt).then_inc(consts, 1)
            eng.tensor_scalar(part[:, :], iota_i[:, 0:1], -1.0, 1.0, ALU.mult, ALU.mult).then_inc(consts, 1)
            eng.memset(ones32[:, :], 1.0).then_inc(consts, 1)
            eng.wait_ge(consts, 6)
            eng.iota(iota_i[:, :], pattern=[[1, N]], base=0, channel_multiplier=0).then_inc(consts, 1)
            eng.tensor_copy(ones[:, :], ones32[:, :]).then_inc(consts, 1)
            eng.wait_ge(consts, 8)
            eng.tensor_copy(iota[:, :], iota_i[:, :]).then_inc(consts, 1)
            eng.tensor_copy(iota_h[:, :], iota_i[:, :]).then_inc(consts, 1)
            eng.wait_ge(consts, CONSTS)

            steps = [0]

            def link(ins):
                steps[0] += 1
                ins.then_inc(pool_step, 1)
                eng.wait_ge(pool_step, steps[0])

            def fill_rows(chunk):
                for j in range(FILL):
                    g = G2 + chunk * FILL + j
                    rows = FILL_TILES[chunk][3 * j:3 * j + 3]
                    eng.tensor_scalar(rows[0], iota[:, :], idx[:, 1, g:g + 1], None, ALU.is_equal)
                    eng.tensor_scalar(rows[1], iota[:, :], idx[:, 0, g:g + 1], as32(wt_hi[:, g:g + 1]),
                                      ALU.is_equal, ALU.mult)
                    eng.tensor_scalar(rows[2], iota[:, :], idx[:, 0, g:g + 1], wt_lo[:, g:g + 1],
                                      ALU.is_equal, ALU.mult).then_inc(fill_ready, 1)

            def add_row(n):
                eng.wait_ge(brow_in, 16 * (n + 1))
                for t in range(NT):
                    wait_normed(eng, n, t)
                    eng.tensor_tensor(x_sb[:, t, :], x_sb[:, t, :], brow, ALU.add).then_inc(xb_ready, 1)

            add_row(0)
            eng.wait_ge(etw_in, 16)
            link(eng.tensor_scalar(sp[:, 3, :], sp[:, 0, :], 0.0, None, ALU.max))
            link(eng.tensor_scalar(sp[:, 1, :], sp[:, 0, :], 0.0, None, ALU.min))
            eng.tensor_tensor(sp[:, 1, :], sp[:, 3, :], sp[:, 1, :], ALU.subtract).then_inc(soft_step, 1)
            eng.wait_ge(soft_step, 3)
            link(eng.tensor_tensor(sp[:, 3, :], sp[:, 3, :], sp[:, 2, :], ALU.add))
            link(eng.tensor_scalar(sp[:, 3, :], sp[:, 3, :], 1.0 / SCALE, None, ALU.mult))
            for t in range(NT):
                ex, t1, t2, t3 = mask_i[:, t, :], tmp[:, 0:N], tmp[:, N:2 * N], tmp[:, 2 * N:3 * N]
                g1 = 1.0 / GROUP_BITS
                if t == 0:
                    eng.wait_ge(bits_read, NT)
                link(eng.tensor_copy(t2, ex))
                link(eng.tensor_scalar(t1, t2, -(LOWEST + 1.5), g1, ALU.add, ALU.mult))
                link(eng.tensor_scalar(t1, t1, ROUND, -ROUND, ALU.add, ALU.add))
                link(eng.tensor_scalar(t1, t1, -float(GROUP_BITS), None, ALU.mult))
                link(eng.tensor_tensor(t1, t1, t2, ALU.add))
                link(eng.tensor_scalar(t2, t1, float(LOWEST), sp[:, 3, 0:1], ALU.is_equal, ALU.mult))
                for c in range(1, ETYPES):
                    link(eng.tensor_scalar(t3, t1, float(LOWEST + c), sp[:, 3, c:c + 1], ALU.is_equal, ALU.mult))
                    link(eng.tensor_tensor(t2, t2, t3, ALU.add))
                link(eng.tensor_scalar(t1, iota[:, :], -float(t * P), part[:, 0:1], ALU.add, ALU.is_equal))
                link(eng.tensor_scalar(t3, t1, -1.0, -FAR, ALU.add, ALU.mult))
                link(eng.tensor_scalar(t1, t1, sp[:, 3, ETYPES - 1:ETYPES], None, ALU.mult))
                link(eng.tensor_tensor(t1, t1, t3, ALU.add))
                link(eng.tensor_scalar(t3, ex, 0.0, None, ALU.is_equal))
                link(eng.tensor_tensor(t1, t1, t3, ALU.mult))
                eng.tensor_tensor(mask[:, t, :], t1, t2, ALU.add).then_inc(mask_ready, 1)
                eng.wait_ge(mask_ready, t + 1)
            for h in range(H):
                for t in range(NT):
                    eng.wait_ge(rinv_ready, h + 1)
                    eng.tensor_scalar(prob(h, t), prob(h, t), stat(rinv, h, t), 1.0, ALU.mult,
                                      ALU.mult).then_inc(p_ready, 1)
            eng.wait_ge(deg_ready, 2)
            for t in range(NT):
                d = adj[:, t, t * P:(t + 1) * P]
                eng.tensor_tensor(d, as32(d), ident[:, :], ALU.add).then_inc(adj_ready, 1)
            eng.wait_ge(pv_up, H)
            fill_rows(0)
            add_row(1)
            eng.wait_ge(w_used, U_W2)
            fill_rows(1)
            eng.wait_ge(h_up, HALF * NT)
            for t in range(NT):
                d = adj[:, t, t * P:(t + 1) * P]
                eng.tensor_tensor(d, as32(d), ident[:, :], ALU.subtract).then_inc(adj_ready, 1)
            add_row(2)
            eng.wait_ge(brow_in, 16 * 4)
            for t in range(NT):
                wait_normed(eng, 3, t)
                for c in (slice(0, N), slice(N, F)):
                    eng.tensor_tensor(x_sb[:, t, c], x_sb[:, t, c], brow[:, c], ALU.add).then_inc(xb_ready, 1)

        @block.scalar
        def _(eng):
            def hi_of_unit(u, s, slot_free=True):
                if isinstance(u, int) and u >= U_W1:
                    if slot_free:
                        eng.wait_ge(w_used, u - 3)
                    eng.wait_ge(landed[s], 16 * (u // SLOTS + 1))
                    d, r = unit_part(u, ring_hi), unit_part(u, raw)
                    eng.activation(d, r, ACT.Copy).then_inc(w_hi, 1)
                else:
                    eng.wait_ge(turned_up, u + 1)
                    tp = 2 * (s % 2)
                    eng.activation(ring_hi[:, s, :], ps[:, tp:tp + 2, :].rearrange("p b c -> p (b c)"),
                                   ACT.Copy).then_inc(w_hi, 1)

            def norms(n):
                def root(t):
                    eng.wait_ge(var_up, n * NT + t + 1)
                    eng.activation(rstd[:, t:t + 1], mv[:, t, 1:2], ACT.Sqrt).then_inc(std_up, 1)
                root(0)
                for t in range(NT):
                    if t + 1 < NT:
                        root(t + 1)
                    if t < NORM_ACT[n]:
                        eng.wait_ge(coef_up, n * NT + t + 1)
                        eng.activation(tmp_n[:, t, :], x_sb[:, t, :], ACT.Identity, scale=rstd[:, t:t + 1],
                                       bias=nshift[:, t:t + 1]).then_inc(normed_act, 1)

            def norms_hi(n, dst):
                for t, c in PARTS:
                    wait_normed(eng, n, t)
                    eng.activation(dst[0][:, t, c], tmp_n[:, t, c], ACT.Relu).then_inc(n_hi, 1)

            def turn_hi(n, tiles, dst):
                banks = TURN_BANKS[n // KT]
                for k in range(tiles):
                    eng.wait_ge(t_up, n + k + 1)
                    b = banks[k % 3]
                    eng.activation(dst[0][:, k:k + 1, :], ps[:, b:b + 1, 0:N], ACT.Relu).then_inc(t_hi, 1)

            norms(0)
            hi_of_unit(0, 0)
            turn_hi(0, KT, a_t)
            hi_of_unit(1, 1)
            eng.wait_ge(turned_small, 1)
            eng.activation(bias[:, :], ps[:, 7, 0:NB], ACT.Copy).then_inc(small_read, 1)
            eng.wait_ge(turned_small, 2)
            eng.activation(idx[:, :, :], ps[:, 6, 0:5 * G].rearrange("p (a g) -> p a g", a=5), ACT.Copy)\
               .then_inc(small_read, 1)
            eng.wait_ge(small_read, 1)

            def weigh(n, s):
                g1 = bass.ds(n, 1)
                if s % 2 == 0:
                    eng.activation(hot_wl[:, s, :], hot[:, s, 2, :], ACT.Copy, scale=wt_lo[:, g1])
                eng.activation(hot_wh[:, s, :], hot[:, s, 2, :], ACT.Copy, scale=as32(wt_hi[:, g1])).then_inc(weighed, 1)

            def edges_out():
                for s in range(SLOTS):
                    eng.wait_ge(hot_ready, G + s + 1)
                    weigh(s, s)
                with eng.Fori(1, G2 // SLOTS) as i:
                    for s in range(SLOTS):
                        eng.wait_ge(hot_ready, i * SLOTS + (G + s + 1))
                        eng.wait_ge(hot_used, i * SLOTS + (G + s - 3))
                        weigh(i * SLOTS + s, s)
                eng.wait_ge(hot_used, G + G2)
                eng.activation(wedge[:, 1, :], ps[:, WEIGHTS[1], 0:N], ACT.Copy).then_inc(wedge_ready, 1)

            def isd_roots():
                eng.wait_ge(isd_sq, 1)
                eng.activation(row_isd[:, :], row_isd[:, :], ACT.Sqrt).then_inc(deg_ready, 1)
                eng.activation(col_isd[:, 0:NT], col_isd[:, 0:NT], ACT.Sqrt).then_inc(deg_ready, 1)

            def softplus_steps():
                eng.wait_ge(soft_step, 1)
                eng.activation(sp[:, 1, :], sp[:, 1, :], ACT.Exp, scale=-1.0).then_inc(soft_step, 1)
                eng.wait_ge(soft_step, 2)
                eng.activation(sp[:, 2, :], sp[:, 1, :], ACT.Ln, bias=1.0).then_inc(soft_step, 1)


            def turned_out(L, u, o, s):
                eng.wait_ge(w_used, u + 1)
                src_ = ps[:, 4 + s % 2:5 + s % 2, 0:N]
                row = bass.ds(o + BIAS_COL[L], 1)
                eng.activation(LAYER_OUT[L][0][:, bass.ds(o, 1), :], src_, ACT.Identity,
                               bias=bias[:, row]).then_inc(acc_hi, 1)

            def v_out_hi(i, t):
                if t < NT - 1:
                    eng.wait_ge(v_up, i * (NT - 1) + t + 1)
                else:
                    eng.wait_ge(w_used, 5 * KT + 2 * i + 2)
                eng.activation(v_n[0][:, t, i * PAIR:(i + 1) * PAIR], pair_out(i, t), ACT.Copy).then_inc(v_hi, 1)

            def exps(h):
                for t in range(NT):
                    eng.wait_ge(nmx_ready, h + 1)
                    eng.activation(prob(h, t), prob(h, t), ACT.Exp, bias=stat(nmx, h, t),
                                   accum_out=stat(rs, h, t)).then_inc(exp_done, 1)

            def probs_hi(h, par):
                for j in range(NT):
                    eng.wait_ge(pt_up, h * NT + j + 1)
                    eng.activation(b_t[0][:, par * NT + j, :], ps[:, 3 + j, 0:N], ACT.Copy).then_inc(pt_hi, 1)

            def heads_hi(h, pair, par):
                r = slice(D * par, D * par + D)
                eng.wait_ge(pv_up, h + 1)
                b = ROWS["iv"] + pair
                eng.activation(q2[0][r, bass.ds(pair, 1), :], ps[r, 6 + par:7 + par, 0:N],
                               ACT.Identity, bias=bias[r, b:b + 1]).then_inc(o_hi, 1)

            for L in range(len(TURNED)):
                if L == 6:
                    for h in range(H):
                        if h:
                            heads_hi(h - 1, (h - 1) // 2, (h - 1) % 2)
                        if h + 1 < H:
                            probs_hi(h + 1, (h + 1) % 2)
                        if h + AHEAD < H:
                            exps(h + AHEAD)
                    heads_hi(H - 1, (H - 1) // 2, (H - 1) % 2)
                if L == 2:
                    edges_out()
                    softplus_steps()
                if L == 4:
                    isd_roots()
                if L < 5:
                    with eng.Fori(0, KT // SLOTS) as i:
                        for s in range(SLOTS):
                            hi_of_unit(i * SLOTS + (L * KT + s + 2), (s + 2) % SLOTS)
                            turned_out(L, i * SLOTS + (L * KT + s), i * SLOTS + s, s)
                else:
                    for i in range(PAIRS):
                        for j in range(2):
                            hi_of_unit(L * KT + 2 * i + 2 + j, (2 * i + 2 + j) % SLOTS)
                        if L == 5:
                            for t in range(NT):
                                v_out_hi(i, t)
                                if i == PAIRS - 1:
                                    if t == NT - 1:
                                        probs_hi(0, 0)
                                    exps(t)

            def relu_tile(n, o, u, dst, rows=P):
                eng.wait_ge(w_used, u + 1)
                if n >= SLOTS:
                    eng.wait_ge(m_lo, n - SLOTS + 1)
                b = ROWS["mid"] + o if n < MT else ROWS["s0"] + o
                t = tmp_t[0:rows, n % SLOTS, :]
                eng.activation(t, ps[0:rows, 4 + n % 2, 0:N], ACT.Relu, bias=bias[0:rows, b:b + 1]).then_inc(m_r, 1)
                eng.wait_ge(m_r, n + 1)
                eng.activation(dst[0][0:rows, o, :], t, ACT.Copy).then_inc(m_hi, 1)

            def aggregated_hi(n, dst):
                for k in range(KT):
                    eng.wait_ge(g_m, n + k + 1)
                    eng.activation(dst[0][:, k, :], tmp_t[:, k, :], ACT.Copy).then_inc(g_hi, 1)

            norms(1)
            norms_hi(1, b_n)
            aggregated_hi(0, a_t)
            for o in range(MT):
                relu_tile(o, o, U_W1 + o, m_t, P if o < MT - 1 else LASTM)
                hi_of_unit(U_W1 + o + 2, (o + 2) % SLOTS)
            for k in range(MT):
                hi_of_unit(U_W2 + k + 2, (k + 2) % SLOTS)

            def rows_hi(n, u_last, dst, scaled):
                for half in range(HALF):
                    for t in range(NT):
                        if half * NT + t < HALF * NT - 1:
                            eng.wait_ge(z_up, n + half * NT + t + 1)
                        else:
                            eng.wait_ge(w_used, u_last + 1)
                        d = dst[0][:, t, half * BANK:(half + 1) * BANK]
                        q = ps[:, 2 * t + half, :]
                        scale = col_isd[:, t:t + 1] if scaled else 1.0
                        eng.activation(d, q, ACT.Copy, scale=scale).then_inc(z_hi, 1)

            rows_hi(0, U_S0 - 1, b_n, True)
            norms(2)
            turn_hi(KT, KT, a_t)
            norms_hi(2, c_n)
            aggregated_hi(KT, b_t)
            for o in range(KT):
                hi_of_unit(U_S0 + 2 * o + 2, (2 * o + 2) % SLOTS)
                relu_tile(MT + o, o, U_S0 + 2 * o + 1, k2)
                hi_of_unit(U_S0 + 2 * o + 3, (2 * o + 3) % SLOTS)
            eng.wait_ge(wedge_added, 2 * NT)
            for k in range(NT):
                eng.activation(b_t[0][:, k, :], wedge[:, k, :], ACT.Copy).then_inc(wedge_hi, 1)
            for k in range(KT):
                hi_of_unit(U_N1 + k + 2, (k + 2) % SLOTS)
            rows_hi(HALF * NT - 1, U_S1 - 1, c_n, False)
            for k in range(KT - 2):
                hi_of_unit(U_S1 + k + 2, (k + 2) % SLOTS)
            for t in range(NT):
                n = 3 * NT + t
                eng.wait_ge(var_up, n + 1)
                eng.activation(rstd[:, t:t + 1], mv[:, t, 1:2], ACT.Sqrt).then_inc(std_up, 1)
                eng.wait_ge(coef_up, n + 1)
                eng.activation(tmp_n[:, t, 0:N], x_sb[:, t, 0:N], ACT.Identity, scale=rstd[:, t:t + 1],
                               bias=nshift[:, t:t + 1]).then_inc(normed_act, 1)
                eng.wait_ge(t_up, 2 * KT + t + 1)
                eng.activation(a_t[0][:, 0:NT, t * P:(t + 1) * P], last_turn(t), ACT.Relu).then_inc(t_hi, 1)

        @block.vector
        def _(eng):
            steps = [0]

            def link(ins):
                steps[0] += 1
                ins.then_inc(dve_step, 1)
                eng.wait_ge(dve_step, steps[0])

            def lo_of_unit(u, s):
                eng.wait_ge(w_hi, u + 1)
                if isinstance(u, int) and u >= U_W1:
                    d, r, h = (unit_part(u, b) for b in (ring_lo, raw, ring_hi))
                    eng.tensor_tensor(d, r, as32(h), ALU.subtract).then_inc(w_lo, 1)
                else:
                    tp = 2 * (s % 2)
                    eng.tensor_tensor(ring_lo[:, s, :], ps[:, tp:tp + 2, :].rearrange("p b c -> p (b c)"),
                                      as32(ring_hi[:, s, :]), ALU.subtract).then_inc(w_lo, 1)

            def part_stats(t, part, width=BANK):
                eng.bn_stats(stats[:, t, part, :], x_sb[:, t, part * width:(part + 1) * width]).then_inc(stats_up, 1)

            def variance(t, seen, parts=HALF):
                eng.wait_ge(stats_up, seen)
                link(eng.bn_aggr(mv[:, t, :], stats[:, t, 0:parts, :].rearrange("p a b -> p (a b)")))
                eng.tensor_scalar(mv[:, t, 1:2], mv[:, t, 1:2], EPS, None, ALU.add).then_inc(var_up, 1)

            def coefs(n, t, by=None):
                eng.wait_ge(std_up, n * NT + t + 1)
                r = rstd[:, t:t + 1]
                link(eng.reciprocal(r, r))
                if by is not None:
                    link(eng.tensor_tensor(r, r, by[:, t:t + 1], ALU.mult))
                eng.tensor_scalar(nshift[:, t:t + 1], mv[:, t, 0:1], r, -1.0, ALU.mult, ALU.mult).then_inc(coef_up, 1)

            def norm_tile(n, t, by=None):
                coefs(n, t, by)
                eng.wait_ge(coef_up, n * NT + t + 1)
                eng.tensor_scalar(tmp_n[:, t, :], x_sb[:, t, :], rstd[:, t:t + 1], nshift[:, t:t + 1],
                                  ALU.mult, ALU.add).then_inc(normed_dve, 1)

            def norms_lo(n, dst):
                for j, (t, c) in enumerate(PARTS):
                    eng.wait_ge(n_hi, (n - 1) * len(PARTS) + j + 1)
                    eng.scalar_tensor_tensor(dst[1][:, t, c], tmp_n[:, t, c], 0.0, as32(dst[0][:, t, c]), ALU.max,
                                             ALU.subtract).then_inc(n_lo, 1)

            def turn_lo(n, tiles, dst):
                banks = TURN_BANKS[n // KT]
                for k in range(tiles):
                    eng.wait_ge(t_hi, n + k + 1)
                    eng.scalar_tensor_tensor(dst[1][:, k, :], ps[:, banks[k % 3], 0:N], 0.0, as32(dst[0][:, k, :]),
                                             ALU.max, ALU.subtract).then_inc(t_lo, 1)

            for t in range(NT):
                eng.wait_ge(x_in[t], 16)
                for half in range(HALF):
                    part_stats(t, half)
                variance(t, (t + 1) * HALF)
                if t == 1:
                    coefs(0, 0)
            coefs(0, 1)
            norm_tile(0, 2)
            lo_of_unit(0, 0)
            turn_lo(0, KT, a_t)
            lo_of_unit(1, 1)
            eng.wait_ge(ids_in, 16 * 4)
            link(eng.tensor_copy(stage[:, 0:3 * P], stage_i[:, 0:3 * P]))
            eng.scalar_tensor_tensor(stage[:, 4 * P:5 * P], stage[:, 0:P], float(N), stage[:, P:2 * P],
                                     ALU.mult, ALU.add).then_inc(ids_flat, 1)

            def find_dups(u):
                for g in range(GU * u, GU * (u + 1)):
                    if g:
                        eng.wait_ge(keys_read, g)
                    else:
                        eng.wait_ge(small_read, 2)
                        eng.wait_ge(consts, CONSTS)
                    if g % GU == 0:
                        eng.wait_ge(keys_up, u + 1)
                    j = g % GU
                    eng.scalar_tensor_tensor(keyeq, ps[:, 6 + u % 2, j * P:(j + 1) * P],
                                             idx[:, 4, g:g + 1], later[:, :], ALU.is_equal, ALU.mult,
                                             accum_out=dup[:, g:g + 1]).then_inc(keys_read, 1)

            def powers():
                eng.wait_ge(keys_read, G)
                et = idx[:, 2, :]
                c0, c1 = code
                link(eng.tensor_scalar(c0, et, 0.0, float(ETYPES), ALU.is_equal, ALU.mult))
                link(eng.scalar_tensor_tensor(c0, et, -1.0, c0, ALU.add, ALU.add))
                link(eng.tensor_scalar(c1, iota[:, 0:G], float(GROUP_BITS), float(LOWEST), ALU.mult, ALU.add))
                link(eng.tensor_tensor(c0, c0, c1, ALU.add))
                link(eng.tensor_scalar(c1, dup[:, :], 0.0, float(2 ** 23), ALU.is_equal, ALU.mult))
                link(eng.tensor_tensor(pow2_i[:, :], c0, c1, ALU.mult))
                link(eng.tensor_copy(wt_hi[:, :], idx[:, 3, :]))
                link(eng.tensor_tensor(wt_lo[:, :], idx[:, 3, :], as32(wt_hi[:, :]), ALU.subtract))

            def hot_rows1(g, s):
                g1 = bass.ds(g, 1)
                eng.tensor_scalar(hot[:, s, 0, :], iota_h[:, :], idx[:, 0, g1], None, ALU.is_equal)
                eng.tensor_scalar(hot[:, s, 1, :], iota_h[:, :], idx[:, 1, g1], pow2_i[:, g1].bitcast(F32),
                                  ALU.is_equal, ALU.mult)
                eng.tensor_scalar(hot[:, s, 2, :], iota_h[:, :], idx[:, 1, g1], None,
                                  ALU.is_equal).then_inc(hot_ready, 1)

            def hot_rows2(g, s):
                g1 = bass.ds(g, 1)
                eng.tensor_scalar(hot_dst[:, s, :], iota[:, :], idx[:, 1, g1], None, ALU.is_equal)
                if s % 2 == 1:
                    eng.tensor_scalar(hot_wl[:, s, :], iota[:, :], idx[:, 0, g1], wt_lo[:, g1], ALU.is_equal, ALU.mult)
                eng.tensor_scalar(hot[:, s, 2, :], iota_h[:, :], idx[:, 0, g1], None,
                                  ALU.is_equal).then_inc(hot_ready, 1)

            def edges_out():
                with eng.Fori(1, G // SLOTS) as i:
                    for s in range(SLOTS):
                        eng.wait_ge(hot_used, i * SLOTS + (s - 3))
                        hot_rows1(i * SLOTS + s, s)
                for s in range(SLOTS - 1):
                    eng.wait_ge(hot_used, G + s - 3)
                    hot_rows2(s, s)
                eng.wait_ge(xb_ready, NT)
                eng.wait_ge(hot_used, G)
                for g in range(SLOTS - 1, 3 * SLOTS):
                    s, t = g % SLOTS, g - (SLOTS - 1)
                    if t < NT:
                        eng.tensor_scalar(mask_i[:, t, :], ps[:, BITS[t], 0:N].bitcast(I32), 23, None,
                                          ALU.logical_shift_right).then_inc(bits_read, 1)
                    elif t < 2 * NT:
                        t -= NT
                        eng.tensor_copy(adj[:, t, :], ps[:, COUNTS[t], 0:N]).then_inc(adj_raw, 1)
                    if g >= SLOTS:
                        eng.wait_ge(hot_used, G + g - 3)
                        eng.wait_ge(weighed, g - 3)
                    hot_rows2(g, s)
                with eng.Fori(3, G2 // SLOTS) as i:
                    for s in range(SLOTS):
                        eng.wait_ge(hot_used, i * SLOTS + (G + s - 3))
                        eng.wait_ge(weighed, i * SLOTS + (s - 3))
                        hot_rows2(i * SLOTS + s, s)
                eng.wait_ge(hot_used, G + G2)
                for t in (0, 2):
                    eng.tensor_copy(wedge[:, t, :], ps[:, WEIGHTS[t], 0:N]).then_inc(wedge_ready, 1)

            def degrees():
                eng.wait_ge(deg_up, 1)
                dcol = ps[:, 7, N:N + 2 * NT].rearrange("p (t a) -> p t a", a=2)[:, :, 0]
                drow = ps[:, 7, 0:N]
                link(eng.tensor_scalar(row_isd[:, :], drow, 1.0, None, ALU.add))
                link(eng.tensor_scalar(col_isd[:, 0:NT], dcol, 1.0, None, ALU.add))
                eng.reciprocal(row_isd[:, :], row_isd[:, :])
                eng.reciprocal(col_isd[:, 0:NT], col_isd[:, 0:NT]).then_inc(isd_sq, 1)
                link(eng.tensor_scalar(row_inv[:, :], drow, 1.0, None, ALU.max))
                link(eng.tensor_scalar(col_inv[:, 0:NT], dcol, 1.0, None, ALU.max))
                eng.reciprocal(row_inv[:, :], row_inv[:, :])
                link(eng.reciprocal(col_inv[:, 0:NT], col_inv[:, 0:NT]))

            def turned_out(L, u, o, s):
                eng.wait_ge(acc_hi, u + 1)
                hi, lo = (LAYER_OUT[L][j][:, bass.ds(o, 1), :] for j in range(2))
                src_ = ps[:, 4 + s % 2:5 + s % 2, 0:N]
                eng.scalar_tensor_tensor(lo, src_, bias[:, bass.ds(o + BIAS_COL[L], 1)], as32(hi), ALU.add,
                                         ALU.subtract).then_inc(acc_free, 1)

            def mask_scores(h):
                for t in range(NT):
                    eng.wait_ge(sc_up, h * NT + t + 1)
                    eng.tensor_tensor_reduce(prob(h, t), ps[:, t, 0:N], mask[:, t, :], SCALE, FAR, ALU.add, ALU.max,
                                             stat(mx, h, t)).then_inc(sc_read, 1)
                eng.wait_ge(sc_read, h * NT + NT)
                eng.tensor_scalar(stat(nmx, h), stat(mx, h), -1.0, None, ALU.mult).then_inc(nmx_ready, 1)

            def row_sums(h):
                eng.wait_ge(exp_done, h * NT + NT)
                eng.reciprocal(stat(rinv, h), stat(rs, h)).then_inc(rinv_ready, 1)

            def probs_lo(h, par):
                for j in range(NT):
                    eng.wait_ge(pt_hi, h * NT + j + 1)
                    eng.tensor_tensor(b_t[1][:, par * NT + j, :], ps[:, 3 + j, 0:N],
                                      as32(b_t[0][:, par * NT + j, :]), ALU.subtract).then_inc(pt_lo, 1)

            def heads_lo(h, pair, par):
                r = slice(D * par, D * par + D)
                eng.wait_ge(o_hi, h + 1)
                b = ROWS["iv"] + pair
                eng.scalar_tensor_tensor(q2[1][r, bass.ds(pair, 1), :], ps[r, 6 + par:7 + par, 0:N],
                                         bias[r, b:b + 1], as32(q2[0][r, bass.ds(pair, 1), :]), ALU.add,
                                         ALU.subtract).then_inc(o_lo, 1)

            for L in range(len(TURNED)):
                if L == 2:
                    edges_out()
                if L == 3:
                    degrees()
                if L == 6:
                    row_sums(1)
                    probs_lo(0, 0)
                    for h in range(H):
                        if h + 2 < H:
                            row_sums(h + 2)
                        if h + AHEAD < H:
                            mask_scores(h + AHEAD)
                        if h:
                            heads_lo(h - 1, (h - 1) // 2, (h - 1) % 2)
                        if h + 1 < H:
                            probs_lo(h + 1, (h + 1) % 2)
                    heads_lo(H - 1, (H - 1) // 2, (H - 1) % 2)
                if L < 2:
                    for o in range(KT):
                        u = L * KT + o
                        lo_of_unit(u + 2, (u + 2) % SLOTS)
                        turned_out(L, u, o, o % SLOTS)
                        if u < U_DUPS:
                            find_dups(u)
                        elif u == U_DUPS:
                            powers()
                        elif u == U_DUPS + 1:
                            for s in range(SLOTS):
                                hot_rows1(s, s)
                elif L < 5:
                    with eng.Fori(0, KT // SLOTS) as i:
                        for s in range(SLOTS):
                            lo_of_unit(i * SLOTS + (L * KT + s + 2), (s + 2) % SLOTS)
                            turned_out(L, i * SLOTS + (L * KT + s), i * SLOTS + s, s)
                else:
                    for i in range(PAIRS):
                        for j in range(2):
                            lo_of_unit(L * KT + 2 * i + 2 + j, (2 * i + 2 + j) % SLOTS)
                        for t in range(NT):
                            c = slice(i * PAIR, (i + 1) * PAIR)
                            if L == 5:
                                eng.wait_ge(v_hi, i * NT + t + 1)
                                eng.tensor_tensor(v_n[1][:, t, c], pair_out(i, t), as32(v_n[0][:, t, c]),
                                                  ALU.subtract).then_inc(v_lo, 1)
                                if i == PAIRS - 1:
                                    if t == 0:
                                        eng.wait_ge(mask_ready, NT)
                                    mask_scores(t)
                                    if t == 1:
                                        row_sums(0)
                            else:
                                if t < NT - 1:
                                    eng.wait_ge(y_up, i * (NT - 1) + t + 1)
                                else:
                                    eng.wait_ge(w_used, L * KT + 2 * i + 2)
                                if i == 0 and t == 0:
                                    eng.wait_ge(xb_ready, NT)
                                eng.tensor_tensor(x_sb[:, t, c], pair_out(i, t), x_sb[:, t, c],
                                                  ALU.add).then_inc(x1_ready, 1)
                                eng.wait_ge(x1_ready, i * NT + t + 1)
                                part_stats(t, i, PAIR)
                                if i == PAIRS - 1:
                                    variance(t, NT * HALF + i * NT + t + 1, PAIRS)
                                    if t == 1:
                                        eng.wait_ge(deg_ready, 2)
                                        coefs(1, 0, col_isd)
                                        norm_tile(1, 1, col_isd)
            norm_tile(1, 2, col_isd)

            def add_wedge(chunk):
                for t in range(NT):
                    eng.wait_ge(fill_up, chunk + 1)
                    eng.tensor_tensor(wedge[:, t, :], ps[:, t, 0:N], wedge[:, t, :], ALU.add).then_inc(wedge_added, 1)

            def aggregated_lo(n, row, dst):
                eng.wait_ge(n_lo, (n // KT + 1) * len(PARTS))
                for k in range(KT + 1):
                    if k < KT:
                        eng.wait_ge(g_up, n + k + 1)
                        eng.tensor_tensor(tmp_t[:, k, :], ps[:, 6 + k % 2, 0:N], row[:, :], ALU.mult).then_inc(g_m, 1)
                    if k:
                        eng.wait_ge(g_hi, n + k)
                        eng.tensor_tensor(dst[1][:, k - 1, :], tmp_t[:, k - 1, :], as32(dst[0][:, k - 1, :]),
                                          ALU.subtract).then_inc(g_lo, 1)

            def relu_lo(n, o, dst, rows=P):
                eng.wait_ge(m_hi, n + 1)
                eng.tensor_tensor(dst[1][0:rows, o, :], tmp_t[0:rows, n % SLOTS, :], as32(dst[0][0:rows, o, :]),
                                  ALU.subtract).then_inc(m_lo, 1)

            norms_lo(1, b_n)
            aggregated_lo(0, row_isd, a_t)
            add_wedge(0)
            for o in range(MT):
                relu_lo(o, o, m_t, P if o < MT - 1 else LASTM)
                lo_of_unit(U_W1 + o + 2, (o + 2) % SLOTS)
            for k in range(MT):
                lo_of_unit(U_W2 + k + 2, (k + 2) % SLOTS)

            def rows_lo(n, dst, scaled):
                for half in range(HALF):
                    for t in range(NT):
                        n += 1
                        eng.wait_ge(z_hi, n)
                        hi, lo = (dst[j][:, t, half * BANK:(half + 1) * BANK] for j in range(2))
                        q = ps[:, 2 * t + half, :]
                        if scaled:
                            last = eng.scalar_tensor_tensor(lo, q, col_isd[:, t:t + 1], as32(hi), ALU.mult,
                                                            ALU.subtract)
                        else:
                            last = eng.tensor_tensor(lo, q, as32(hi), ALU.subtract)
                        last.then_inc(z_lo, 1)

            def add_aggregated(b, blocks, half, t, col, ready):
                eng.wait_ge(h_up, blocks + b + 1)
                xs = x_sb[:, t, half * BANK:(half + 1) * BANK]
                eng.scalar_tensor_tensor(xs, ps[:, 6 + b % 2, :], col[:, t:t + 1], xs, ALU.mult,
                                         ALU.add).then_inc(ready, 1)
                eng.wait_ge(ready, b + 1)
                part_stats(t, half)

            rows_lo(0, b_n, True)
            eng.wait_ge(xb_ready, 2 * NT)
            for half in range(HALF):
                for t in range(NT):
                    b = half * NT + t
                    add_aggregated(b, 0, half, t, col_isd, x2_ready)
                    if half == HALF - 1:
                        variance(t, NT * (HALF + PAIRS) + b + 1)
                        if t == 1:
                            coefs(2, 0)
            coefs(2, 1)
            norm_tile(2, 2)
            turn_lo(KT, KT, a_t)
            norms_lo(2, c_n)
            aggregated_lo(KT, row_inv, b_t)
            add_wedge(1)
            for o in range(KT):
                lo_of_unit(U_S0 + 2 * o + 2, (2 * o + 2) % SLOTS)
                relu_lo(MT + o, o, k2)
                lo_of_unit(U_S0 + 2 * o + 3, (2 * o + 3) % SLOTS)
            eng.wait_ge(wedge_hi, NT)
            for k in range(NT):
                eng.tensor_tensor(b_t[1][:, k, :], wedge[:, k, :], as32(b_t[0][:, k, :]),
                                  ALU.subtract).then_inc(wedge_lo, 1)
            for k in range(KT):
                lo_of_unit(U_N1 + k + 2, (k + 2) % SLOTS)
            rows_lo(HALF * NT, c_n, False)
            for k in range(KT - 2):
                lo_of_unit(U_S1 + k + 2, (k + 2) % SLOTS)
            eng.wait_ge(xb_ready, 3 * NT)
            for half in range(HALF):
                for t in range(NT):
                    if half * NT + t < HALF * NT - 1:
                        eng.wait_ge(s_up, half * NT + t + 1)
                    else:
                        eng.wait_ge(w_used, U_END)
                    xs = x_sb[:, t, half * BANK:(half + 1) * BANK]
                    eng.tensor_tensor(xs, ps[:, 2 * t + half, :], xs, ALU.add).then_inc(s_added, 1)
            eng.wait_ge(s_added, HALF * NT)
            def last_lo(t):
                eng.wait_ge(t_hi, 2 * KT + t + 1)
                cols = slice(t * P, (t + 1) * P)
                eng.scalar_tensor_tensor(a_t[1][:, 0:NT, cols], last_turn(t), 0.0, as32(a_t[0][:, 0:NT, cols]),
                                         ALU.max, ALU.subtract).then_inc(t_lo, 1)

            def last_add(t):
                eng.wait_ge(xb_ready, 3 * NT + 2 * t + 1)
                eng.wait_ge(f_up, t + 1)
                eng.tensor_tensor(x_sb[:, t, 0:N], ps[:, t, 0:N], x_sb[:, t, 0:N], ALU.add).then_inc(x4_ready, 1)

            for t in range(NT):
                for half in range(HALF):
                    b = t * HALF + half
                    add_aggregated(b, HALF * NT, half, t, col_inv, x3_ready)
                    if half == 0 and t == 2:
                        last_lo(0)
                    if half == 0 and t:
                        coefs(3, t - 1)
                variance(t, NT * (2 * HALF + PAIRS) + b + 1)
            coefs(3, NT - 1)
            last_lo(1)
            last_lo(2)
            for t in range(NT):
                last_add(t)

        @block.tensor
        def _(eng):
            def mm3(out_, l, r, first, last):
                eng.matmul(out_, l[0], r[0], start=first, stop=False)
                eng.matmul(out_, l[1], r[0], start=False, stop=False)
                return eng.matmul(out_, l[0], r[1], start=False, stop=last)

            def turn_unit(landed_value, s):
                eng.wait_ge(landed[s], landed_value)
                for k in range(KT):
                    tr = eng.transpose(ps[:, 2 * (s % 2) + k // 4, (k % 4) * P:(k % 4 + 1) * P],
                                       raw[:, s, k * P:(k + 1) * P], ident[:, :])
                tr.then_inc(turned_up, 1)

            eng.wait_ge(consts, 3)
            turn_unit(16, 0)
            turn_unit(16, 1)

            def turn(n, tiles, norm):
                banks = TURN_BANKS[n // KT]
                for k in range(tiles):
                    if k >= 3:
                        eng.wait_ge(t_lo, n + k - 2)
                    for t in range(NT):
                        if k == 0:
                            wait_normed(eng, norm, t)
                        tr = eng.transpose(ps[:, banks[k % 3], t * P:(t + 1) * P], tmp_n[:, t, k * P:(k + 1) * P],
                                           ident[:, :])
                    tr.then_inc(t_up, 1)

            turn(0, KT, 0)

            def small():
                eng.wait_ge(bias_in, 16 * 9)
                eng.transpose(ps[:, 7, 0:NB], bias_rows[:, :], ident[0:NB, 0:NB]).then_inc(turned_small, 1)
                eng.wait_ge(ids_flat, 1)
                for j in range(5):
                    tr = eng.transpose(ps[:, 6, j * G:(j + 1) * G], stage[:, j * P:(j + 1) * P], ident[0:G, 0:G])
                tr.then_inc(turned_small, 1)
                eng.wait_ge(small_read, 2)

            def keys(u):
                if u == 0:
                    small()
                if u >= 2:
                    eng.wait_ge(keys_read, GU * (u - 1))
                for j in range(GU):
                    g = GU * u + j
                    tr = eng.transpose(ps[:, 6 + u % 2, j * P:(j + 1) * P],
                                       idx[:, 4, g:g + 1].to_broadcast([P, P]), ident[:, :])
                tr.then_inc(keys_up, 1)

            def edge_pass1(g, s, first, last):
                eng.wait_ge(hot_ready, g + 1)
                for m in range(NT):
                    l = hot[:, s, 0, m * P:(m + 1) * P]
                    eng.matmul(ps[:, BITS[m], 0:N], l, hot[:, s, 1, :], start=first, stop=last)
                    mm = eng.matmul(ps[:, COUNTS[m], 0:N], l, hot[:, s, 2, :], start=first, stop=last)
                mm.then_inc(hot_used, 1)

            def edge_pass2(g, s, first, last):
                eng.wait_ge(weighed, g - G + 1)
                for m in range(NT):
                    if first and m == 2:
                        eng.wait_ge(bits_read, 1)
                    l = hot_dst[:, s, m * P:(m + 1) * P]
                    eng.matmul(ps[:, WEIGHTS[m], 0:N], l, hot_wh[:, s, :], start=first, stop=False)
                    mm = eng.matmul(ps[:, WEIGHTS[m], 0:N], l, hot_wl[:, s, :], start=False, stop=last)
                mm.then_inc(hot_used, 1)

            def edges_in():
                eng.wait_ge(w_lo, 2 * KT + 2)
                for base, groups, edge_pass in ((0, G, edge_pass1), (G, G2, edge_pass2)):
                    if base:
                        eng.wait_ge(acc_free, 2 * KT)
                    for s in range(SLOTS):
                        edge_pass(base + s, s, s == 0, False)
                    with eng.Fori(1, groups // SLOTS - 1) as i:
                        for s in range(SLOTS):
                            edge_pass(i * SLOTS + (base + s), s, False, False)
                    for s in range(SLOTS):
                        edge_pass(base + groups - SLOTS + s, s, False, s == SLOTS - 1)
                eng.wait_ge(adj_raw, NT)
                eng.wait_ge(bits_read, NT)
                for s in range(NT):
                    eng.matmul(ps[:, 7, 0:N], ones[:, :], adj[:, s, :], start=s == 0, stop=s == NT - 1)
                for t in range(NT):
                    for s in range(NT):
                        mm = eng.matmul(ps[:, 7, N + 2 * t:N + 2 * t + 2], adj[:, s, t * P:(t + 1) * P], ones[:, 0:2],
                                        start=s == 0, stop=s == NT - 1)
                mm.then_inc(deg_up, 1)
                eng.wait_ge(wedge_ready, NT)

            def ring(s, k, m=P):
                return [b[:, s, k * P:k * P + m] for b in (ring_hi, ring_lo)]

            def turned_unit(L, u, s, landed_value, bank_free=True, x_split=False):
                eng.wait_ge(w_lo, u + 1)
                if bank_free:
                    eng.wait_ge(acc_free, u - 1)
                if L in (1, 3, 5):
                    eng.wait_ge(acc_free, L * KT - 1)
                if landed_value is not None:
                    turn_unit(landed_value, (s + 2) % SLOTS)
                for k in range(KT):
                    if k == KT - 1 and L in (1, 3, 5):
                        eng.wait_ge(acc_free, L * KT)
                    if x_split:
                        eng.wait_ge(t_lo, k + 1)
                    mm = mm3(ps[:, 4 + s % 2, 0:N], ring(s, k), [b[:, k, :] for b in LAYER_IN[L]], k == 0, k == KT - 1)
                mm.then_inc(w_used, 1)

            def scores(h):
                r = slice(D * (h % 2), D * (h % 2) + D)
                for t in range(NT):
                    if h >= 1:
                        eng.wait_ge(sc_read, (h - 1) * NT + t + 1)
                    mm3(ps[:, t, 0:N], [q[r, h // 2, t * P:(t + 1) * P] for q in q2], [k[r, h // 2, :] for k in k2],
                        True, True).then_inc(sc_up, 1)

            def turn_probs(h):
                for j in range(NT):
                    if h >= 1:
                        eng.wait_ge(pt_lo, (h - 1) * NT + j + 1)
                    for t in range(NT):
                        if j == 0:
                            eng.wait_ge(p_ready, h * NT + t + 1)
                        tr = eng.transpose(ps[:, 3 + j, t * P:(t + 1) * P], prob(h, t, slice(j * P, (j + 1) * P)),
                                           ident[:, :])
                    tr.then_inc(pt_up, 1)

            def attend(h, par):
                if h >= 2:
                    eng.wait_ge(o_lo, h - 1)
                for j in range(NT):
                    eng.wait_ge(pt_lo, h * NT + j + 1)
                    mm = mm3(ps[:, 6 + par, 0:N], [v[:, j, (h // 2) * P:(h // 2 + 1) * P] for v in v_n],
                             [q[:, par * NT + j, :] for q in b_t], j == 0, j == NT - 1)
                mm.then_inc(pv_up, 1)

            def pair(L, i):
                u = L * KT + 2 * i
                eng.wait_ge(w_lo, u + 2)
                for v in (u + 2, u + 3):
                    if v < U_W1:
                        turn_unit(16 * (v // SLOTS + 1), v % SLOTS)
                if i == 0:
                    if L == 5:
                        eng.wait_ge(acc_free, L * KT)
                    else:
                        eng.wait_ge(o_lo, H)
                s = u % SLOTS
                for t in range(NT):
                    if i * NT + t >= 4:
                        eng.wait_ge(v_lo if L == 5 else x1_ready, i * NT + t - 3)
                    for k in range(KT):
                        mm = mm3(pair_out(i, t), [b[:, k, t * P:(t + 1) * P] for b in LAYER_IN[L]],
                                 [b[:, s:s + 2, k * P:(k + 1) * P] for b in (ring_hi, ring_lo)], k == 0, k == KT - 1)
                    if t < NT - 1:
                        mm.then_inc(v_up if L == 5 else y_up, 1)
                    else:
                        mm.then_inc(w_used, 2)
                    if L == 5 and i == PAIRS - 1:
                        if t == 0:
                            eng.wait_ge(w_lo, u + 4)
                        scores(t)

            for L in range(len(TURNED)):
                if L == 2:
                    edges_in()
                if L < 2:
                    for o in range(KT):
                        u = L * KT + o
                        turned_unit(L, u, u % SLOTS, 16 * ((u + 2) // SLOTS + 1), u >= 2, u == 0)
                        if u < U_DUPS:
                            keys(u)
                elif L < 5:
                    with eng.Fori(0, KT // SLOTS) as i:
                        for s in range(SLOTS):
                            v = L * KT + s + 2
                            turned_unit(L, i * SLOTS + (L * KT + s), s, i * 16 + 16 * (v // SLOTS + 1))
                else:
                    for i in range(PAIRS):
                        pair(L, i)
                if L == 5:
                    eng.wait_ge(v_lo, PAIRS * NT)
                    turn_probs(0)
                    for h in range(H):
                        if h + AHEAD < H:
                            scores(h + AHEAD)
                        if h + 1 < H:
                            turn_probs(h + 1)
                        attend(h, h % 2)

            def aggregate(n, act, parts):
                for k in range(KT):
                    if k % (KT // HALF) == 0:
                        eng.wait_ge(n_lo, parts + NT * (k // (KT // HALF) + 1))
                    if k >= 2:
                        eng.wait_ge(g_m, n + k - 1)
                    for s in range(NT):
                        for j in range(2):
                            mm = eng.matmul(ps[:, 6 + k % 2, 0:N], act[j][:, s, k * P:(k + 1) * P], adj[:, s, :],
                                            start=s == 0 and j == 0, stop=s == NT - 1 and j == 1)
                    mm.then_inc(g_up, 1)

            def relu_unit(n, u, act, first, last, m=P, counts=None):
                s = u % SLOTS
                eng.wait_ge(w_lo, u + 1)
                if first and n >= 2:
                    eng.wait_ge(m_r, n - 1)
                for k in range(KT):
                    if counts is not None:
                        eng.wait_ge(counts[0], counts[1] + k + 1)
                    mm = mm3(ps[0:m, 4 + n % 2, 0:N], ring(s, k, m), [b[:, k, :] for b in act],
                             first and k == 0, last and k == KT - 1)
                mm.then_inc(w_used, 1)

            def rows_layer(act, u0, tiles, lastrows, ready, up, bank_free):
                for k in range(tiles):
                    u = u0 + k
                    r = P if k < tiles - 1 else lastrows
                    eng.wait_ge(w_lo, u + 1)
                    eng.wait_ge(m_lo, ready + k + 1)
                    for half in range(HALF):
                        for t in range(NT):
                            if k == 0:
                                bank_free(half * NT + t)
                            mm = mm3(ps[:, 2 * t + half, :], [a[0:r, k, t * P:(t + 1) * P] for a in act],
                                     [b[0:r, u % SLOTS, half * BANK:(half + 1) * BANK] for b in (ring_hi, ring_lo)],
                                     k == 0, k == tiles - 1)
                            if half * NT + t == HALF * NT - 1:
                                mm.then_inc(w_used, 1)
                            elif k == tiles - 1:
                                mm.then_inc(up, 1)

            def aggregate_rows(b, half, t, act, done):
                if b >= 2:
                    eng.wait_ge(done, b - 1)
                for s in range(NT):
                    for j in range(2):
                        mm = eng.matmul(ps[:, 6 + b % 2, :], adj[:, s, t * P:(t + 1) * P],
                                        act[j][:, s, half * BANK:(half + 1) * BANK],
                                        start=s == 0 and j == 0, stop=s == NT - 1 and j == 1)
                mm.then_inc(h_up, 1)

            def fill(chunk):
                for j in range(FILL):
                    eng.wait_ge(fill_ready, chunk * FILL + j + 1)
                    d, wh, wl = FILL_TILES[chunk][3 * j:3 * j + 3]
                    for m in range(NT):
                        eng.matmul(ps[:, m, 0:N], d[:, m * P:(m + 1) * P], wh, start=j == 0, stop=False)
                        mm = eng.matmul(ps[:, m, 0:N], d[:, m * P:(m + 1) * P], wl, start=False, stop=j == FILL - 1)
                mm.then_inc(fill_up, 1)

            fill(0)
            eng.wait_ge(adj_ready, NT)
            aggregate(0, b_n, 0)
            for o in range(MT):
                relu_unit(o, U_W1 + o, a_t, True, True, P if o < MT - 1 else LASTM,
                          (g_lo, 0) if o == 0 else None)
            eng.wait_ge(wedge_added, NT)
            rows_layer(m_t, U_W2, MT, LASTM, 0, z_up, lambda b: eng.wait_ge(m_r, MT) if b == 2 else None)
            for half in range(HALF):
                eng.wait_ge(z_lo, (half + 1) * NT)
                for t in range(NT):
                    aggregate_rows(half * NT + t, half, t, b_n, x2_ready)
            fill(1)
            turn(KT, KT, 2)
            relu_unit(MT, U_S0, a_t, True, False, P, (t_lo, KT))
            eng.wait_ge(adj_ready, 2 * NT)
            aggregate(KT, c_n, len(PARTS))
            for o in range(KT):
                if o:
                    relu_unit(MT + o, U_S0 + 2 * o, a_t, True, False)
                relu_unit(MT + o, U_S0 + 2 * o + 1, b_t, False, True, P, (g_lo, KT) if o == 0 else None)
            eng.wait_ge(wedge_added, 2 * NT)
            rows_layer(k2, U_N1, KT, P, MT, z_up, lambda b: eng.wait_ge(m_r, MT + KT) if b == 2 else None)
            rows_layer(k2, U_S1, KT, P, MT, s_up, lambda b: eng.wait_ge(z_lo, HALF * NT + b + 1))
            eng.wait_ge(z_lo, 2 * HALF * NT)
            for t in range(NT):
                for half in range(HALF):
                    aggregate_rows(t * HALF + half, half, t, c_n, x3_ready)
            eng.wait_ge(wedge_lo, NT)

            def turn_last(t):
                wait_normed(eng, 3, t)
                for k in range(NT):
                    tr = eng.transpose(ps[:, NT + t, k * P:(k + 1) * P], tmp_n[:, t, k * P:(k + 1) * P], ident[:, :])
                tr.then_inc(t_up, 1)

            turn_last(0)
            for t in range(NT):
                if t == 1:
                    turn_last(1)
                    turn_last(2)
                eng.wait_ge(t_lo, 2 * KT + t + 1)
                for k in range(NT):
                    mm = mm3(ps[:, t, 0:N], [a[:, k, t * P:(t + 1) * P] for a in a_t], [b[:, k, :] for b in b_t],
                             k == 0, k == NT - 1)
                mm.then_inc(f_up, 1)


_INS = ['x', 'src', 'dst', 'edge_type_5', 'edge_weight', 'L0_gnn_edge_type_weights', 'L0_gnn_wq', 'L0_gnn_bq',
        'L0_gnn_wk', 'L0_gnn_bk', 'L0_gnn_wv', 'L0_gnn_bv', 'L0_gnn_wiq', 'L0_gnn_biq', 'L0_gnn_wik', 'L0_gnn_bik',
        'L0_gnn_wiv', 'L0_gnn_biv', 'L0_gnn_wo', 'L0_gnn_bo', 'L1_gnn_W1', 'L1_gnn_b1', 'L1_gnn_W2', 'L1_gnn_b2',
        'L2_gnn_W_self0', 'L2_gnn_W_neigh0', 'L2_gnn_b0', 'L2_gnn_W_self1', 'L2_gnn_W_neigh1', 'L2_gnn_b1',
        'L3_gnn_bias']


def kernel(**inputs):
    import numpy as _np
    import concourse.bacc as _bacc
    from concourse import mybir as _mybir
    from concourse.bass_utils import run_bass_kernel_spmd as _run

    nc = _bacc.Bacc("TRN2", target_bir_lowering=False, num_devices=1)
    arrays, args = {}, []
    for name in _INS:
        a = _np.ascontiguousarray(inputs[name])
        arrays[f"in_{name}_dram"] = a
        args.append(nc.dram_tensor(f"in_{name}_dram", a.shape, _mybir.dt.from_np(a.dtype), kind="ExternalInput").ap())
    shape = arrays["in_x_dram"].shape
    args.append(nc.dram_tensor("out_0_dram", shape, _mybir.dt.float32, kind="ExternalOutput").ap())
    gnn_stack(nc, *args)
    r = _run(nc, [arrays], core_ids=[0])
    return r.results[0]["out_0_dram"]
```
